# Optimizing a Trainium2 kernel written in Bass

```python
import numpy as np
import jax
import jax.numpy as jnp

def _softmax(x, axis=-1):
    return jax.nn.softmax(x, axis=axis)

def _gelu(x):
    return jax.nn.gelu(x, approximate=True)

def _silu(x):
    return jax.nn.silu(x)

def _sigmoid(x):
    return jax.nn.sigmoid(x)

def _layernorm(x, axis=-1, eps=1e-05):
    m = jnp.mean(x, axis=axis, keepdims=True)
    v = jnp.var(x, axis=axis, keepdims=True)
    return (x - m) / jnp.sqrt(v + eps)

def _scatter_add(tgt, idx, src, axis=0):
    return tgt.at[idx].add(src)

def _segment_sum(src, seg, n):
    return jax.ops.segment_sum(src, seg, n)
kernel_name = 'mk_audio_tower_d2_tok_audfeat256_r4_6edaaa'

def setup_inputs(seed: int=0):
    np.random.seed(seed)
    _w = jnp.asarray

    def _rec_inputs():
        import jax
        import jax.numpy as jnp
        _rk = jax.random.key(seed)
        x = 7.22013e-05 + 1.00017 * jax.random.normal(jax.random.fold_in(_rk, 1), (64, 256, 128), jnp.float32)
        return x
    x = _rec_inputs()

    def _L0_tok_setup():
        import jax, jax.numpy as jnp
        import numpy as np
        FILTER_SIZE = 8
        INPUT_DIM = 128
        KERNEL_SIZE = 64
        key = jax.random.key(seed)
        k1, k2, k3, k4 = jax.random.split(key, 4)
        user_batch = jax.random.normal(k1, (32, 512, INPUT_DIM), dtype=jnp.float32)
        filt = jax.random.uniform(k2, (FILTER_SIZE, INPUT_DIM), dtype=jnp.float32)
        W_k = jax.random.uniform(k3, (FILTER_SIZE * INPUT_DIM, KERNEL_SIZE), dtype=jnp.float32)
        b_k = jax.random.uniform(k4, (KERNEL_SIZE,), dtype=jnp.float32)
        return {'user_batch': user_batch, 'filt': filt, 'W_k': W_k, 'b_k': b_k}
    _L0_tok_all = _L0_tok_setup()
    _L0_tok_in = {k: v for k, v in _L0_tok_all.items() if k in ('filt', 'W_k', 'b_k')}
    del _L0_tok_all

    def _L0_attn_setup():
        import jax, jax.numpy as jnp
        import numpy as np
        B, N, C, H = (64, 75, 64, 8)
        STD = 0.02

        def _rel_indices(n):
            d = (jnp.arange(n)[None, :] - jnp.arange(n)[:, None]).astype(jnp.float32)
            return jnp.stack([d, jnp.zeros_like(d), d * d], axis=-1)
        key = jax.random.key(seed)
        ks = jax.random.split(key, 6)
        return {'x': jax.random.normal(ks[0], (B, N, C), jnp.float32), 'Wqk': jax.random.normal(ks[1], (2 * C, C), jnp.float32) * STD, 'Wv': jax.random.normal(ks[2], (C, C), jnp.float32) * STD, 'Wpos': jax.random.normal(ks[3], (H, 3), jnp.float32) * STD, 'bpos': jnp.zeros((H,), jnp.float32), 'Wproj': jax.random.normal(ks[4], (C, C), jnp.float32) * STD, 'bproj': jnp.zeros((C,), jnp.float32), 'gating': jnp.ones((H,), jnp.float32)}
    _L0_attn_all = _L0_attn_setup()
    _L0_attn_in = {k: v for k, v in _L0_attn_all.items() if k in ('Wqk', 'Wv', 'Wpos', 'bpos', 'Wproj', 'bproj', 'gating')}
    del _L0_attn_all

    def _L0_ffn_setup():
        import jax, jax.numpy as jnp
        import numpy as np
        B, S, D = (8, 1024, 64)
        H = 4 * D
        CAPACITY = 0.5
        key = jax.random.key(seed)
        ks = jax.random.split(key, 6)
        x = jax.random.normal(ks[0], (B, S, D), dtype=jnp.float32)
        attention_mask = jnp.zeros((B, 1, 1, S), dtype=jnp.float32)
        wr = jax.random.normal(ks[1], (D, 1), dtype=jnp.float32) * 0.02
        br = jnp.zeros((1,), dtype=jnp.float32)
        w1 = jax.random.normal(ks[2], (D, H), dtype=jnp.float32) * 0.02
        b1 = jnp.zeros((H,), dtype=jnp.float32)
        w2 = jax.random.normal(ks[3], (H, D), dtype=jnp.float32) * 0.02
        b2 = jnp.zeros((D,), dtype=jnp.float32)
        return {'x': x, 'attention_mask': attention_mask, 'wr': wr, 'br': br, 'w1': w1, 'b1': b1, 'w2': w2, 'b2': b2}
    _L0_ffn_all = _L0_ffn_setup()
    _L0_ffn_in = {k: v for k, v in _L0_ffn_all.items() if k in ('attention_mask', 'wr', 'br', 'w1', 'b1', 'w2', 'b2')}
    del _L0_ffn_all

    def _L1_attn_setup():
        import jax, jax.numpy as jnp
        import numpy as np
        MAX_ADAPTIVE_LR = 0.1

        def _l2n(z):
            n = jnp.linalg.norm(z, axis=-1, keepdims=True)
            return z / jnp.maximum(n, 1e-12)

        def _mlp(params, z):
            W0, W1, P0, P1 = params
            h = z @ W0 + z @ P0
            h = jax.nn.silu(h)
            return h @ W1 + h @ P1
        key = jax.random.key(seed)
        kx, kf, kp0, kp1 = jax.random.split(key, 4)
        B, T, H, E = (4, 64, 64, 4)
        D = H * E
        x = jax.random.normal(kx, (B, T, H), dtype=jnp.float32)
        W_fused = jax.random.normal(kf, (3 * H + 3, H), dtype=jnp.float32) / np.sqrt(H).astype(np.float32)
        W0 = jnp.zeros((H, D), dtype=jnp.float32)
        W1 = jnp.zeros((D, H), dtype=jnp.float32)
        P0 = jax.random.normal(kp0, (H, D), dtype=jnp.float32)
        P1 = jax.random.normal(kp1, (D, H), dtype=jnp.float32)
        return {'x': x, 'W_fused': W_fused, 'W0': W0, 'W1': W1, 'P0': P0, 'P1': P1}
    _L1_attn_all = _L1_attn_setup()
    _L1_attn_in = {k: v for k, v in _L1_attn_all.items() if k in ('W_fused', 'W0', 'W1', 'P0', 'P1')}
    del _L1_attn_all

    def _L1_ffn_setup():
        import jax, jax.numpy as jnp
        import numpy as np
        B, S, D, H, E, K = (8, 2048, 64, 256, 8, 2)
        key = jax.random.key(seed)
        ks = jax.random.split(key, 7)
        s_in = 1.0 / np.sqrt(D)
        s_hid = 1.0 / np.sqrt(H)
        return {'x': jax.random.normal(ks[0], (B, S, D), dtype=jnp.float32), 'Wg': jax.random.uniform(ks[1], (E, D), jnp.float32, -s_in, s_in), 'bg': jax.random.uniform(ks[2], (E,), jnp.float32, -s_in, s_in), 'W1': jax.random.uniform(ks[3], (E, H, D), jnp.float32, -s_in, s_in), 'b1': jax.random.uniform(ks[4], (E, H), jnp.float32, -s_in, s_in), 'W2': jax.random.uniform(ks[5], (E, D, H), jnp.float32, -s_hid, s_hid), 'b2': jax.random.uniform(ks[6], (E, D), jnp.float32, -s_hid, s_hid)}
    _L1_ffn_all = _L1_ffn_setup()
    _L1_ffn_in = {k: v for k, v in _L1_ffn_all.items() if k in ('Wg', 'bg', 'W1', 'b1', 'W2', 'b2')}
    del _L1_ffn_all
    return {'x': x, 'L0_tok_filt': _L0_tok_in['filt'], 'L0_tok_W_k': _L0_tok_in['W_k'], 'L0_tok_b_k': _L0_tok_in['b_k'], 'L0_attn_Wqk': _L0_attn_in['Wqk'], 'L0_attn_Wv': _L0_attn_in['Wv'], 'L0_attn_Wpos': _L0_attn_in['Wpos'], 'L0_attn_bpos': _L0_attn_in['bpos'], 'L0_attn_Wproj': _L0_attn_in['Wproj'], 'L0_attn_bproj': _L0_attn_in['bproj'], 'L0_attn_gating': _L0_attn_in['gating'], 'L0_ffn_attention_mask': _L0_ffn_in['attention_mask'], 'L0_ffn_wr': _L0_ffn_in['wr'], 'L0_ffn_br': _L0_ffn_in['br'], 'L0_ffn_w1': _L0_ffn_in['w1'], 'L0_ffn_b1': _L0_ffn_in['b1'], 'L0_ffn_w2': _L0_ffn_in['w2'], 'L0_ffn_b2': _L0_ffn_in['b2'], 'L1_attn_W_fused': _L1_attn_in['W_fused'], 'L1_attn_W0': _L1_attn_in['W0'], 'L1_attn_W1': _L1_attn_in['W1'], 'L1_attn_P0': _L1_attn_in['P0'], 'L1_attn_P1': _L1_attn_in['P1'], 'L1_ffn_Wg': _L1_ffn_in['Wg'], 'L1_ffn_bg': _L1_ffn_in['bg'], 'L1_ffn_W1': _L1_ffn_in['W1'], 'L1_ffn_b1': _L1_ffn_in['b1'], 'L1_ffn_W2': _L1_ffn_in['W2'], 'L1_ffn_b2': _L1_ffn_in['b2']}

def reference(x, L0_tok_filt, L0_tok_W_k, L0_tok_b_k, L0_attn_Wqk, L0_attn_Wv, L0_attn_Wpos, L0_attn_bpos, L0_attn_Wproj, L0_attn_bproj, L0_attn_gating, L0_ffn_attention_mask, L0_ffn_wr, L0_ffn_br, L0_ffn_w1, L0_ffn_b1, L0_ffn_w2, L0_ffn_b2, L1_attn_W_fused, L1_attn_W0, L1_attn_W1, L1_attn_P0, L1_attn_P1, L1_ffn_Wg, L1_ffn_bg, L1_ffn_W1, L1_ffn_b1, L1_ffn_W2, L1_ffn_b2):
    import jax
    import jax.numpy as jnp

    def _L0_tok_ref(user_batch, filt, W_k, b_k):
        import jax, jax.numpy as jnp
        import numpy as np
        FILTER_SIZE = 8
        INPUT_DIM = 128
        KERNEL_SIZE = 64
        B, L, D = user_batch.shape
        F = filt.shape[0]
        n_win = L - F
        idx = jnp.arange(n_win)[:, None] + jnp.arange(F)[None, :]
        windows = user_batch[:, idx, :]
        W = W_k.reshape(F, D, -1)
        out = jnp.einsum('blfd,fd,fdk->blk', windows, filt, W)
        return jax.nn.relu(out + b_k)

    def _L0_attn_ref(x, Wqk, Wv, Wpos, bpos, Wproj, bproj, gating):
        import jax, jax.numpy as jnp
        import numpy as np
        B, N, C, H = (64, 75, 64, 8)
        STD = 0.02

        def _rel_indices(n):
            d = (jnp.arange(n)[None, :] - jnp.arange(n)[:, None]).astype(jnp.float32)
            return jnp.stack([d, jnp.zeros_like(d), d * d], axis=-1)
        Bb, Nn, Cc = x.shape
        Hh = gating.shape[0]
        hd = Cc // Hh
        scale = hd ** (-0.5)
        qk = (x @ Wqk.T).reshape(Bb, Nn, 2, Hh, hd)
        q = qk[:, :, 0].transpose(0, 2, 1, 3)
        k = qk[:, :, 1].transpose(0, 2, 1, 3)
        patch_score = jax.nn.softmax(jnp.einsum('bhnd,bhmd->bhnm', q, k) * scale, axis=-1)
        rel = _rel_indices(Nn)
        pos_score = (rel @ Wpos.T + bpos).transpose(2, 0, 1)
        pos_score = jax.nn.softmax(pos_score, axis=-1)
        g = jax.nn.sigmoid(gating)[None, :, None, None]
        attn = (1.0 - g) * patch_score + g * pos_score[None]
        attn = attn / attn.sum(axis=-1, keepdims=True)
        v = (x @ Wv.T).reshape(Bb, Nn, Hh, hd).transpose(0, 2, 1, 3)
        out = jnp.einsum('bhnm,bhmd->bhnd', attn, v)
        out = out.transpose(0, 2, 1, 3).reshape(Bb, Nn, Cc)
        return out @ Wproj.T + bproj

    def _L0_ffn_ref(x, attention_mask, wr, br, w1, b1, w2, b2):
        import jax, jax.numpy as jnp
        import numpy as np
        B, S, D = (8, 1024, 64)
        H = 4 * D
        CAPACITY = 0.5
        b, s, d = x.shape
        weights = (jnp.einsum('bsd,do->bso', x, wr) + br)[..., 0]
        k = max(1, int(CAPACITY * s))
        kk = k - 1 if k > 1 else 1
        _, idx = jax.lax.top_k(weights, k)
        sel_idx = idx[:, :kk]
        sel = jnp.take_along_axis(x, sel_idx[:, :, None], axis=1)
        h = jax.nn.gelu(jnp.einsum('bkd,dh->bkh', sel, w1) + b1)
        y = jnp.einsum('bkh,hd->bkd', h, w2) + b2
        w_sel = jnp.take_along_axis(weights, sel_idx, axis=1)
        y = y * w_sel[..., None]
        batch_idx = jnp.arange(b)[:, None]
        processed = jnp.zeros_like(x).at[batch_idx, sel_idx].set(y)
        return processed + x

    def _L1_attn_ref(x, W_fused, W0, W1, P0, P1):
        import jax, jax.numpy as jnp
        import numpy as np
        MAX_ADAPTIVE_LR = 0.1

        def _l2n(z):
            n = jnp.linalg.norm(z, axis=-1, keepdims=True)
            return z / jnp.maximum(n, 1e-12)

        def _mlp(params, z):
            W0, W1, P0, P1 = params
            h = z @ W0 + z @ P0
            h = jax.nn.silu(h)
            return h @ W1 + h @ P1
        B, T, H = x.shape
        fp = x @ W_fused.T
        q, k, v, alpha, theta, eta = jnp.split(fp, [H, 2 * H, 3 * H, 3 * H + 1, 3 * H + 2], axis=-1)
        q = _l2n(jax.nn.silu(q))
        k = _l2n(jax.nn.silu(k))
        v = jax.nn.silu(v)
        alpha = jax.nn.sigmoid(alpha)
        theta = jax.nn.sigmoid(theta) * MAX_ADAPTIVE_LR
        eta = jax.nn.sigmoid(eta)
        params0 = (W0, W1, P0, P1)
        bat = lambda p: jnp.broadcast_to(p[None], (B,) + p.shape)
        cur_p = jax.tree_util.tree_map(bat, params0)
        cur_m = jax.tree_util.tree_map(jnp.zeros_like, cur_p)

        def loss_fn(params, kk, vv):
            pred = _mlp(params, kk)
            return jnp.mean((pred - vv) ** 2)

        def step(carry, xs):
            cp, cm = carry
            k_t, v_t, q_t, a_t, th_t, e_t = xs
            g = jax.vmap(jax.grad(loss_fn))(cp, k_t, v_t)
            s = lambda c: c[:, :, None]
            nm = jax.tree_util.tree_map(lambda m, gg: m * s(e_t) - s(th_t) * gg, cm, g)
            np_ = jax.tree_util.tree_map(lambda p, m: p * (1.0 - s(a_t)) + m, cp, nm)
            out_t = jax.vmap(_mlp, in_axes=(0, 0))(np_, q_t)
            new_carry = jax.lax.stop_gradient((np_, nm))
            return (new_carry, out_t)
        tT = lambda a: jnp.swapaxes(a, 0, 1)
        xs = tuple(map(tT, (k, v, q, alpha, theta, eta)))
        _, ys = jax.lax.scan(step, (cur_p, cur_m), xs)
        return jnp.swapaxes(ys, 0, 1)

    def _L1_ffn_ref(x, Wg, bg, W1, b1, W2, b2):
        import jax, jax.numpy as jnp
        import numpy as np
        B, S, D, H, E, K = (8, 2048, 64, 256, 8, 2)
        gate_scores = jnp.einsum('bsd,ed->bse', x, Wg) + bg
        topk_scores, topk_idx = jax.lax.top_k(gate_scores, K)
        topk_probs = jax.nn.softmax(topk_scores, axis=-1)
        combine = jnp.sum(topk_probs[..., None] * jax.nn.one_hot(topk_idx, E, dtype=x.dtype), axis=-2)
        out = jnp.zeros_like(x)
        for e in range(E):
            h = jax.nn.relu(jnp.einsum('bsd,hd->bsh', x, W1[e]) + b1[e])
            y = jnp.einsum('bsh,dh->bsd', h, W2[e]) + b2[e]
            out = out + combine[..., e:e + 1] * y
        return out
    h = _L0_tok_ref(x, L0_tok_filt, L0_tok_W_k, L0_tok_b_k)
    h = h + _L0_attn_ref(_layernorm(h, axis=-1), L0_attn_Wqk, L0_attn_Wv, L0_attn_Wpos, L0_attn_bpos, L0_attn_Wproj, L0_attn_bproj, L0_attn_gating)
    h = h + _L0_ffn_ref(_layernorm(h, axis=-1), L0_ffn_attention_mask, L0_ffn_wr, L0_ffn_br, L0_ffn_w1, L0_ffn_b1, L0_ffn_w2, L0_ffn_b2)
    h = h + _L1_attn_ref(_layernorm(h, axis=-1), L1_attn_W_fused, L1_attn_W0, L1_attn_W1, L1_attn_P0, L1_attn_P1)
    h = h + _L1_ffn_ref(_layernorm(h, axis=-1), L1_ffn_Wg, L1_ffn_bg, L1_ffn_W1, L1_ffn_b1, L1_ffn_W2, L1_ffn_b2)
    return h

_drawn_inputs = setup_inputs


def setup_inputs(seed=0):
    import zlib

    import numpy as np

    out = dict(_drawn_inputs(seed))
    spreads = {'L0_attn_bpos': (0.0, 2.0),
     'L0_attn_bproj': (0.0, 0.1),
     'L0_attn_gating': (1.0, 0.6),
     'L0_ffn_b1': (0.0, 0.8),
     'L0_ffn_b2': (0.0, 0.8),
     'L1_attn_W0': (0.0, 2.0),
     'L1_attn_W1': (0.0, 2.0)}
    factors = {'L0_attn_Wqk': 8.0,
     'L0_attn_Wv': 7.697,
     'L0_attn_Wpos': 8.0,
     'L0_attn_Wproj': 7.728,
     'L0_ffn_wr': 8.0,
     'L0_ffn_w1': 8.0,
     'L0_ffn_w2': 8.0,
     'L1_ffn_Wg': 3.159,
     'L1_ffn_bg': 8.0,
     'L1_ffn_W1': 3.39,
     'L1_ffn_b1': 8.0,
     'L1_ffn_W2': 2.754,
     'L1_ffn_b2': 8.0}
    for name, (base, spread) in spreads.items():
        noise = np.random.default_rng([zlib.crc32(name.encode()), seed]).standard_normal(out[name].shape)
        drawn = base * np.exp(spread * noise) if base else spread * noise
        out[name] = jnp.asarray(drawn.astype(out[name].dtype))
    for name, factor in factors.items():
        out[name] = (out[name] * factor).astype(out[name].dtype)
    return out
```

```python
from contextlib import ExitStack

import concourse.bass as bass
from concourse import mybir

F32 = mybir.dt.float32
ALU = mybir.AluOpType
ACT = mybir.ActivationFunctionType
AX = mybir.AxisListType.X

B, L, D, DIN, HID = 64, 248, 64, 128, 256
TL = L // 2
FS = 8
NH = 8
CH, NCH = 16, 16
TOPK = L // 2 - 1
EPS = 1e-5


class Loop:

    def __init__(self, sem, names, unit=1, before=None):
        self.sem, self.unit, self.P = sem, unit, len(names)
        assert len(set(names)) == len(names)
        self.index = {n: i + 1 for i, n in enumerate(names)}
        self.before = self.P if before is None else before

    def wait(self, e, n, name, back=0):
        e.wait_ge(self.sem, n * (self.P * self.unit) + (self.before + self.index[name] - back * self.P) * self.unit)

    def count(self, e, n):
        e.wait_ge(self.sem, n * (self.P * self.unit))


class Space:

    def __init__(self, nc, ctx, name):
        self.nc, self.ctx, self.name = nc, ctx, name

    def sb(self, name, shape):
        return self.ctx.enter_context(self.nc.sbuf_tensor(f"{self.name}_{name}", shape, F32))

    def sem(self, name):
        return self.ctx.enter_context(self.nc.semaphore(f"{self.name}_{name}"))

    def banks(self):
        return [self.ctx.enter_context(self.nc.psum_tensor(f"{self.name}_bank{i}", [128, 512], F32))[:, :] for i in range(8)]


def make_identity(e, ident, sem):
    e.memset(ident[:, :], 0.0).then_inc(sem, 1)
    e.wait_ge(sem, 1)
    e.affine_select(out=ident[:, :], in_=ident[:, :], compare_op=ALU.not_equal, fill=1.0, base=0,
                    pattern=[[-1, 128]], channel_multiplier=1).then_inc(sem, 1)


def norm_vector(e, V, A, n, x, K, t, xn):
    s, q, sq = t
    bc = lambda a: a[:, :].unsqueeze(2).to_broadcast([TL, K, D])
    e.tensor_reduce(s[:, :], x, AX, ALU.add).then_inc(V.sem, 1)
    V.wait(e, n, "mean")
    e.tensor_scalar(s[:, :], s[:, :], 1.0 / D, None, ALU.mult).then_inc(V.sem, 1)
    V.wait(e, n, "meand")
    e.tensor_tensor(xn, x, bc(s), ALU.subtract).then_inc(V.sem, 1)
    V.wait(e, n, "cen")
    e.tensor_tensor(sq[:, :, :], xn, xn, ALU.mult).then_inc(V.sem, 1)
    V.wait(e, n, "sq")
    e.tensor_reduce(q[:, :], sq[:, :, :], AX, ALU.add).then_inc(V.sem, 1)
    A.wait(e, n, "std")
    e.reciprocal(q[:, :], q[:, :]).then_inc(V.sem, 1)
    V.wait(e, n, "rstd")
    e.tensor_tensor(xn, xn, bc(q), ALU.mult).then_inc(V.sem, 1)


def settled(e, sem):
    e.nop().then_inc(sem, 1)


NORM_V = ["mean", "meand", "cen", "sq", "ssq", "rstd", "xn"]


def norm_scalar(e, V, A, n, q, eps):
    V.wait(e, n, "ssq")
    e.activation(q[:, :], q[:, :], ACT.Sqrt, bias=eps[0:TL, 0:1], scale=1.0 / D).then_inc(A.sem, 1)


def token_layer(nc, x, filt, W_k, b_k, H0):
    with ExitStack() as ctx:
        S = Space(nc, ctx, "tok")
        ident = S.sb("ident", [128, 128])
        wf, wk, ft, bk = S.sb("wf", [DIN, FS, D]), S.sb("wk", [DIN, FS, D]), S.sb("ft", [DIN, FS]), S.sb("bk", [128, 1])
        xin, xt = S.sb("xin", [128, 8, DIN]), S.sb("xt", [DIN, 4, 256])
        ht, hrow = S.sb("ht", [128, 2 * L]), S.sb("hrow", [TL, 8, D])
        bank = S.banks()
        s_id, s_w, s_wf = S.sem("ident"), S.sem("weights"), S.sem("filtered")
        V = Loop(S.sem("vector"), ["xt", "row"])
        A = Loop(S.sem("scalar"), ["xt", "relu"])
        T = Loop(S.sem("tensor"), ["xt", "conv", "turn"])
        xin_in = Loop(S.sem("x_in"), ["x"], 16, 0)
        out = Loop(S.sem("out"), ["h"], 16, 0)
        with nc.Block() as block:
            @block.gpsimd
            def _(e):
                make_identity(e, ident, s_id)

            @block.sync
            def _(e):
                e.dma_start(wk[:, :, :], W_k.rearrange("(f d) k -> d f k", f=FS)).then_inc(s_w, 16)
                with nc.allow_non_contiguous_dma("a filter of 4 KB, turned"):
                    e.dma_start(ft[:, :], filt.rearrange("f d -> d f")).then_inc(s_w, 16)
                for g in range(2):
                    e.dma_start(bk[D * g:D * g + D, :], b_k.rearrange("(d a) -> d a", a=1)).then_inc(s_w, 16)
                with e.Fori(0, B // 4) as n:
                    T.wait(e, n, "xt", 1)
                    e.dma_start(xin[:, :, :], x[bass.ds(4 * n, 4), :, :].rearrange("b (c p) d -> p (b c) d", p=128)).then_inc(xin_in.sem, 16)
                    V.wait(e, n, "row")
                    e.dma_start(H0[bass.ds(4 * n, 4), :, :, :].rearrange("b p a d -> p b (a d)"),
                                hrow[:, :, :].rearrange("p (b a) d -> p b (a d)", a=2)).then_inc(out.sem, 16)
                out.count(e, B // 4)

            @block.tensor
            def _(e):
                e.wait_ge(s_id, 2)
                e.wait_ge(s_wf, 1)
                e.nop().then_inc(T.sem, T.P)
                with e.Fori(0, B // 4) as n:
                    xin_in.wait(e, n, "x")
                    V.wait(e, n, "xt", 1)
                    A.wait(e, n, "xt", 1)
                    for k in range(8):
                        mm = e.transpose(bank[k // 4][:, 128 * (k % 4):128 * (k % 4) + 128], xin[:, k, :], ident[:, :])
                    mm.then_inc(T.sem, 1)
                    V.wait(e, n, "xt")
                    A.wait(e, n, "xt")
                    A.wait(e, n, "relu", 1)
                    for f in range(FS):
                        for g in range(2):
                            mm = e.matmul(bank[2][D * g:D * g + D, 0:2 * L], wf[:, f, :], xt[:, 2 * g:2 * g + 2, f:f + L],
                                          start=(f == 0), stop=(f == FS - 1))
                    mm.then_inc(T.sem, 1)
                    A.wait(e, n, "relu")
                    V.wait(e, n, "row", 1)
                    for q in range(4):
                        mm = e.transpose(bank[3][0:TL, 128 * q:128 * q + 128], ht[:, TL * q:TL * q + TL], ident[:, :])
                    mm.then_inc(T.sem, 1)

            @block.scalar
            def _(e):
                e.nop().then_inc(A.sem, A.P)
                e.preload_act_table(ACT.Relu)
                with e.Fori(0, B // 4) as n:
                    T.wait(e, n, "xt")
                    T.wait(e, n, "conv", 1)
                    e.activation(xt[:, 2:4, :], bank[1].rearrange("p (a l) -> p a l", a=2), ACT.Copy).then_inc(A.sem, 1)
                    T.wait(e, n, "conv")
                    T.wait(e, n, "turn", 1)
                    e.activation(ht[:, :], bank[2][:, 0:2 * L], ACT.Relu, bias=bk[:, 0:1]).then_inc(A.sem, 1)

            @block.vector
            def _(e):
                e.wait_ge(s_w, 64)
                e.tensor_tensor(wf[:, :, :], wk[:, :, :], ft[:, :].unsqueeze(2).to_broadcast([DIN, FS, D]), ALU.mult).then_inc(s_wf, 1)
                e.nop().then_inc(V.sem, V.P)
                with e.Fori(0, B // 4) as n:
                    T.wait(e, n, "xt")
                    T.wait(e, n, "conv", 1)
                    e.tensor_copy(xt[:, 0:2, :], bank[0].rearrange("p (a l) -> p a l", a=2)).then_inc(V.sem, 1)
                    T.wait(e, n, "turn")
                    out.count(e, n)
                    e.tensor_copy(hrow[:, :, :].rearrange("p (g q) d -> p g q d", g=2),
                                  bank[3][0:TL, :].rearrange("p (q g d) -> p g q d", q=4, g=2)).then_inc(V.sem, 1)


def attention_layer(nc, Wqk, Wv, Wpos, bpos, Wproj, bproj, gating, H0, H1):
    with ExitStack() as ctx:
        S = Space(nc, ctx, "att")
        ident = S.sb("ident", [128, 128])
        w_raw = S.sb("w_raw", [128, 3, D])
        wT = S.sb("wT", [D + 1, 4, D])
        prm = S.sb("prm", [TL, 40])
        hm = S.sb("hm", [D, NH])
        dist, dist2, cst = S.sb("dist", [TL, 2, L]), S.sb("dist2", [TL, 2, L]), S.sb("cst", [TL, NH])
        pe, pst = S.sb("pe", [TL, L]), S.sb("pst", [TL, 4])
        rt = S.sb("rt", [TL, NH, 2, L])
        omg, sgg = S.sb("omg", [TL, 2, 2, 4]), S.sb("sgg", [TL, 2, 2, 4])
        eps = S.sb("eps", [128, 1])
        ht, xn, sq = S.sb("ht", [TL, 2, D]), S.sb("xn", [TL, 2, D]), S.sb("sq", [TL, 2, D])
        s1, s2 = S.sb("s1", [TL, 2]), S.sb("s2", [TL, 2])
        xT = S.sb("xT", [D, L])
        qa, ka = S.sb("qa", [D + NH, L]), S.sb("ka", [D + NH, NH, L])
        va = S.sb("va", [TL, 2, NH, 32])
        mx = S.sb("mx", [TL, 2, NH])
        ex = S.sb("ex", [TL, NH, 2, L])
        evs, rvs = S.sb("evs", [128, 2 * L]), S.sb("rvs", [128, 2 * L])
        rz, num, rv = S.sb("rz", [TL, 16]), S.sb("num", [TL, 16, 9]), S.sb("rv", [TL, 16, 9])
        at, aT, h1 = S.sb("at", [TL, 2, D]), S.sb("aT", [D + 1, L]), S.sb("h1", [TL, 2, D])
        bank = S.banks()
        s_id, s_w, s_v, s_t, s_a, s_own = S.sem("ident"), S.sem("weights"), S.sem("set_v"), S.sem("set_t"), S.sem("set_a"), S.sem("settled")
        V = Loop(S.sem("vector"), NORM_V + ["xT", "q", "k", "v"] + [f"mx{i}" for i in range(8)] +
                 ["nm", "evs", "rz", "rzg", "num", "rv", "sum", "rd", "at0", "at1", "aT", "h1"])
        A = Loop(S.sem("scalar"), ["std"] + [f"e{h}" for h in range(NH)] + ["rvs"])
        T = Loop(S.sem("tensor"), ["xT", "qk", "v"] + [f"s{i}" for i in range(8)] + ["nm"] + [f"st{h}" for h in range(NH)] +
                 ["ev", "rv", "te", "tr", "aT", "pr"])
        hin = Loop(S.sem("h_in"), ["h"], 16, 0)
        out = Loop(S.sem("out"), ["h"], 16, 0)
        with nc.Block() as block:
            @block.gpsimd
            def _(e):
                make_identity(e, ident, s_id)
                e.wait_ge(s_id, 2)
                e.memset(hm[:, :], 1.0).then_inc(s_id, 1)
                e.wait_ge(s_id, 3)
                e.memset(ka[D:, :, :], 1.0).then_inc(s_id, 1)
                e.wait_ge(s_id, 4)
                e.memset(va[:, :, :, :], 0.0).then_inc(s_id, 1)
                e.wait_ge(s_id, 5)
                e.affine_select(out=hm[:, :], in_=hm[:, :], compare_op=ALU.is_ge, fill=0.0, base=0,
                                pattern=[[-8, NH]], channel_multiplier=1).then_inc(s_id, 1)
                e.wait_ge(s_id, 6)
                e.affine_select(out=hm[:, :], in_=hm[:, :], compare_op=ALU.is_ge, fill=0.0, base=7,
                                pattern=[[8, NH]], channel_multiplier=-1).then_inc(s_id, 1)
                e.wait_ge(s_id, 7)
                e.affine_select(out=ka[D:, :, :], in_=ka[D:, :, :], compare_op=ALU.is_equal, fill=0.0, base=0,
                                pattern=[[-1, NH], [0, L]], channel_multiplier=1).then_inc(s_id, 1)
                e.wait_ge(s_id, 8)
                e.iota(dist[:, :, :], pattern=[[-TL, 2], [1, L]], base=0, channel_multiplier=-1,
                       allow_small_or_imprecise_dtypes=True).then_inc(s_id, 1)
                e.wait_ge(s_id, 9)
                e.memset(va[:, :, :, 8:9], 1.0).then_inc(s_id, 1)
                e.wait_ge(s_id, 10)
                e.memset(aT[D:D + 1, :], 1.0).then_inc(s_id, 1)

            @block.sync
            def _(e):
                e.dma_start(w_raw[:, 0, :], Wqk).then_inc(s_w, 16)
                e.dma_start(w_raw[0:D, 1, :], Wv).then_inc(s_w, 16)
                e.dma_start(w_raw[0:D, 2, :], Wproj).then_inc(s_w, 16)
                e.dma_start(wT[D:D + 1, 3, :], bproj.rearrange("(a n) -> a n", a=1)).then_inc(s_w, 16)
                e.dma_start(prm[:, 0:24], Wpos.rearrange("h c -> (h c)").partition_broadcast(TL)).then_inc(s_w, 16)
                e.dma_start(prm[:, 24:32], bpos.partition_broadcast(TL)).then_inc(s_w, 16)
                e.dma_start(prm[:, 32:40], gating.partition_broadcast(TL)).then_inc(s_w, 16)
                with e.Fori(0, B) as n:
                    V.wait(e, n, "h1", 1)
                    e.dma_start(ht[:, :, :], H0[bass.ds(n, 1), :, :, :].rearrange("b p a d -> p (b a) d")).then_inc(hin.sem, 16)
                    V.wait(e, n, "h1")
                    e.dma_start(H1[bass.ds(n, 1), :, :, :].rearrange("b p a d -> p (b a) d"), h1[:, :, :]).then_inc(out.sem, 16)
                out.count(e, B)

            @block.tensor
            def _(e):
                e.wait_ge(s_w, 16 * 7)
                e.wait_ge(s_id, 2)
                e.transpose(bank[0][0:D, 0:128], w_raw[:, 0, :], ident[:, :]).then_inc(s_t, 1)
                for i in (1, 2):
                    e.transpose(bank[0][0:D, 64 + 64 * i:128 + 64 * i], w_raw[0:D, i, :], ident[0:D, 0:D]).then_inc(s_t, 1)
                for k in range(16):
                    e.wait_ge(s_v, 9 + 6 * k)
                    for mh in range(2):
                        e.transpose(bank[1][0:TL, 128 * mh:128 * mh + TL], pe[:, TL * mh:TL * mh + TL], ident[0:TL, 0:TL]).then_inc(s_t, 1)
                e.wait_ge(s_v, 101)
                e.nop().then_inc(T.sem, T.P)
                with e.Fori(0, B) as n:
                    V.wait(e, n, "xn")
                    settled(e, s_own)
                    for a in range(2):
                        mm = e.transpose(bank[0][0:D, TL * a:TL * a + TL], xn[:, a, :], ident[0:TL, 0:TL])
                    mm.then_inc(T.sem, 1)
                    V.wait(e, n, "xT")
                    settled(e, s_own)
                    for w in range(2):
                        mm = e.matmul(bank[1][0:D, L * w:L * w + L], wT[0:D, w, :], xT[:, :], start=True, stop=True)
                    mm.then_inc(T.sem, 1)
                    for a in range(2):
                        mm = e.matmul(bank[2][0:TL, D * a:D * a + D], xT[:, TL * a:TL * a + TL], wT[0:D, 2, :], start=True, stop=True)
                    mm.then_inc(T.sem, 1)
                    V.wait(e, n, "k")
                    for i in range(8):
                        a, hp = i // 4, i % 4
                        if i >= 2:
                            V.wait(e, n, f"mx{i - 2}")
                        e.matmul(bank[3 + i % 2][0:TL, 0:2 * L], qa[0:D, TL * a:TL * a + TL], ka[0:D, 2 * hp:2 * hp + 2, :],
                                 start=True, stop=True).then_inc(T.sem, 1)
                    V.wait(e, n, "mx7")
                    for a in range(2):
                        mm = e.matmul(bank[5][D:D + NH, TL * a:TL * a + TL], mx[:, a, :], ident[0:TL, 0:TL], start=True, stop=True)
                    mm.then_inc(T.sem, 1)
                    V.wait(e, n, "nm")
                    for h in range(NH):
                        if h >= 2:
                            A.wait(e, n, f"e{h - 2}")
                        for mh in range(2):
                            mm = e.matmul(bank[3 + h % 2][0:TL, L * mh:L * mh + L], ka[:, h, TL * mh:TL * mh + TL], qa[:, :],
                                          start=True, stop=True)
                        mm.then_inc(T.sem, 1)
                    for wts, bk in ((rt, bank[7]), (ex, bank[6])):
                        for g in range(2):
                            for mh in range(2):
                                for j in range(4):
                                    if wts is ex and mh == 0:
                                        A.wait(e, n, f"e{4 * g + j}")
                                    mm = e.matmul(bk[32 * j:32 * j + 32, L * g:L * g + L], va[:, mh, 4 * g + j, :], wts[:, 4 * g + j, mh, :],
                                                  start=(mh == 0), stop=(mh == 1))
                        mm.then_inc(T.sem, 1)
                    for src, bk, need in ((rvs, bank[1], None), (evs, bank[0], None)):
                        if src is rvs:
                            A.wait(e, n, "rvs")
                        else:
                            V.wait(e, n, "evs")
                        for g in range(2):
                            for a in range(2):
                                mm = e.transpose(bk[0:TL, 128 * (2 * g + a):128 * (2 * g + a) + 128], src[:, L * g + TL * a:L * g + TL * a + TL], ident[:, :])
                        mm.then_inc(T.sem, 1)
                    V.wait(e, n, "at1")
                    settled(e, s_own)
                    for a in range(2):
                        mm = e.transpose(bank[2][0:D, 128 + TL * a:128 + TL * a + TL], at[:, a, :], ident[0:TL, 0:TL])
                    mm.then_inc(T.sem, 1)
                    V.wait(e, n, "aT")
                    for a in range(2):
                        mm = e.matmul(bank[2][0:TL, D * a:D * a + D], aT[:, TL * a:TL * a + TL], wT[:, 3, :], start=True, stop=True)
                    mm.then_inc(T.sem, 1)

            @block.scalar
            def _(e):
                e.nop().then_inc(A.sem, A.P)
                e.wait_ge(s_w, 16 * 7)
                e.activation(prm[:, 32:40], prm[:, 32:40], ACT.Sigmoid).then_inc(s_a, 1)
                for k in range(16):
                    e.wait_ge(s_v, 7 + 6 * k)
                    e.activation(pe[:, :], pe[:, :], ACT.Exp, bias=pst[:, 1:2], accum_out=pst[:, 2:3]).then_inc(s_a, 1)
                with e.Fori(0, B) as n:
                    norm_scalar(e, V, A, n, s2, eps)
                    for h in range(NH):
                        T.wait(e, n, f"st{h}")
                        e.activation(ex[:, h, :, :], bank[3 + h % 2][0:TL, 0:2 * L].rearrange("p (m n) -> p m n", m=2), ACT.Exp).then_inc(A.sem, 1)
                    T.wait(e, n, "ev")
                    e.activation(rvs[:, :], bank[7][:, 0:2 * L], ACT.Copy).then_inc(A.sem, 1)

            @block.vector
            def _(e):
                e.nop().then_inc(V.sem, V.P)
                e.memset(eps[:, :], EPS).then_inc(s_v, 1)
                e.wait_ge(s_t, 3)
                e.wait_ge(s_w, 16 * 7)
                e.tensor_copy(wT[0:D, :, :].rearrange("p a b -> p (a b)"), bank[0][0:D, 0:256]).then_inc(s_v, 1)
                e.scalar_tensor_tensor(out=cst[:, :], in0=prm[:, 1:24:3], scalar=0.0, in1=prm[:, 24:32],
                                       op0=ALU.mult, op1=ALU.add).then_inc(s_v, 1)
                e.wait_ge(s_id, 11)
                e.tensor_tensor(dist2[:, :, :], dist[:, :, :], dist[:, :, :], ALU.mult).then_inc(s_v, 1)
                e.wait_ge(s_v, 4)
                for k in range(16):
                    h, nh = k // 2, k % 2
                    v0 = 4 + 6 * k
                    if k:
                        e.wait_ge(s_v, v0)
                    e.tensor_scalar(pe[:, :], dist2[:, nh, :], prm[:, 3 * h + 2:3 * h + 3], cst[:, h:h + 1], ALU.mult, ALU.add).then_inc(s_v, 1)
                    e.wait_ge(s_v, v0 + 1)
                    e.scalar_tensor_tensor(out=pe[:, :], in0=dist[:, nh, :], scalar=prm[:, 3 * h:3 * h + 1], in1=pe[:, :],
                                           op0=ALU.mult, op1=ALU.add).then_inc(s_v, 1)
                    e.wait_ge(s_v, v0 + 2)
                    e.tensor_reduce(pst[:, 1:2], pe[:, :], AX, ALU.max, negate=True).then_inc(s_v, 1)
                    e.wait_ge(s_a, 2 + k)
                    e.reciprocal(pst[:, 3:4], pst[:, 2:3]).then_inc(s_v, 1)
                    e.wait_ge(s_v, v0 + 4)
                    e.tensor_scalar(pe[:, :], pe[:, :], pst[:, 3:4], None, ALU.mult).then_inc(s_v, 1)
                    e.wait_ge(s_t, 3 + 2 * k + 2)
                    e.tensor_copy(rt[:, h, :, TL * nh:TL * nh + TL], bank[1][0:TL, 0:256].rearrange("p (m n) -> p m n", m=2)[:, :, 0:TL]).then_inc(s_v, 1)
                for g in range(2):
                    sg = prm[:, 32 + 4 * g:36 + 4 * g].unsqueeze(1).to_broadcast([TL, 2, 4])
                    e.tensor_copy(sgg[:, g, :, :], sg)
                    ins = e.tensor_scalar(omg[:, g, :, :], sg, -1.0, 1.0, ALU.mult, ALU.add)
                ins.then_inc(s_v, 1)
                e.wait_ge(s_v, 101)
                with e.Fori(0, B) as n:
                    hin.wait(e, n, "h")
                    norm_vector(e, V, A, n, ht[:, :, :], 2, (s1, s2, sq), xn[:, :, :])
                    T.wait(e, n, "xT")
                    e.tensor_copy(xT[:, :], bank[0][0:D, 0:L]).then_inc(V.sem, 1)
                    T.wait(e, n, "qk")
                    e.tensor_scalar(qa[0:D, :], bank[1][0:D, 0:L], float(NH) ** -0.5, None, ALU.mult).then_inc(V.sem, 1)
                    e.tensor_tensor(ka[0:D, :, :], bank[1][0:D, L:2 * L].unsqueeze(1).to_broadcast([D, NH, L]),
                                    hm[:, :].unsqueeze(2).to_broadcast([D, NH, L]), ALU.mult).then_inc(V.sem, 1)
                    T.wait(e, n, "v")
                    e.tensor_copy(va[:, :, :, 0:8], bank[2][0:TL, 0:128].rearrange("p (a h d) -> p a h d", a=2, h=NH)).then_inc(V.sem, 1)
                    for i in range(8):
                        T.wait(e, n, f"s{i}")
                        e.tensor_reduce(mx[:, i // 4, 2 * (i % 4):2 * (i % 4) + 2],
                                        bank[3 + i % 2][0:TL, 0:2 * L].rearrange("p (h m) -> p h m", h=2), AX, ALU.max).then_inc(V.sem, 1)
                    T.wait(e, n, "nm")
                    e.tensor_scalar(qa[D:D + NH, :], bank[5][D:D + NH, 0:L], -1.0, None, ALU.mult).then_inc(V.sem, 1)
                    T.wait(e, n, "rv")
                    e.tensor_copy(evs[:, :], bank[6][:, 0:2 * L]).then_inc(V.sem, 1)
                    T.wait(e, n, "tr")
                    ev = bank[0][0:TL, :].rearrange("p (q c) -> p q c", c=32)
                    rvt = bank[1][0:TL, :].rearrange("p (q c) -> p q c", c=32)
                    flat = lambda t: t[:, :, :, :].rearrange("p g a j -> p (g a j)")
                    e.reciprocal(rz[:, :].unsqueeze(2), ev[:, :, 8:9]).then_inc(V.sem, 1)
                    V.wait(e, n, "rz")
                    e.tensor_tensor(rz[:, :], rz[:, :], flat(omg), ALU.mult).then_inc(V.sem, 1)
                    V.wait(e, n, "rzg")
                    e.tensor_tensor(num[:, :, :], ev[:, :, 0:9], rz[:, :].unsqueeze(2).to_broadcast([TL, 16, 9]), ALU.mult).then_inc(V.sem, 1)
                    e.tensor_tensor(rv[:, :, :], rvt[:, :, 0:9], flat(sgg).unsqueeze(2).to_broadcast([TL, 16, 9]), ALU.mult).then_inc(V.sem, 1)
                    V.wait(e, n, "rv")
                    e.tensor_tensor(num[:, :, :], num[:, :, :], rv[:, :, :], ALU.add).then_inc(V.sem, 1)
                    V.wait(e, n, "sum")
                    e.reciprocal(rz[:, :].unsqueeze(2), num[:, :, 8:9]).then_inc(V.sem, 1)
                    V.wait(e, n, "rd")
                    for a in range(2):
                        v = lambda t: t.rearrange("p (g a j) c -> p a g j c", g=2, a=2)[:, a]
                        e.tensor_tensor(at[:, a, :].rearrange("p (g j c) -> p g j c", g=2, j=4), v(num[:, :, 0:8]),
                                        v(rz[:, :].unsqueeze(2).to_broadcast([TL, 16, 8])), ALU.mult).then_inc(V.sem, 1)
                    T.wait(e, n, "aT")
                    e.tensor_copy(aT[0:D, :], bank[2][0:D, 128:128 + L]).then_inc(V.sem, 1)
                    T.wait(e, n, "pr")
                    out.count(e, n)
                    e.tensor_tensor(h1[:, :, :], bank[2][0:TL, 0:128].rearrange("p (a d) -> p a d", a=2), ht[:, :, :], ALU.add).then_inc(V.sem, 1)


def ffn_layer(nc, wr, br, w1, b1, w2, b2, H1, H2, XN, WD, SW):
    G = B // 4
    with ExitStack() as ctx:
        S = Space(nc, ctx, "ffn")
        ident = S.sb("ident", [128, 128])
        eps = S.sb("eps", [128, 1])
        wrb, brb = S.sb("wrb", [TL, D]), S.sb("brb", [TL, 1])
        w1s, w2s, b1s, b2s = S.sb("w1s", [D, HID]), S.sb("w2s", [128, 2, D]), S.sb("b1s", [128, 2]), S.sb("b2s", [128, 1])
        ht, xn, sq = S.sb("ht", [TL, 8, D]), S.sb("xn", [TL, 8, D]), S.sb("sq", [TL, 8, D])
        s1, s2 = S.sb("s1", [TL, 8]), S.sb("s2", [TL, 8])
        wt = S.sb("wt", [TL, 128])
        wtt = S.sb("wtt", [128, TL])
        wv, wk, m8, ge, eq, pre = S.sb("wv", [B, L]), S.sb("wk", [B, L]), S.sb("m8", [B, 8]), S.sb("ge", [B, L]), S.sb("eq", [B, L]), S.sb("pre", [B, L])
        cnt = S.sb("cnt", [B, 2])
        swp, sw = S.sb("swp", [128, TL]), S.sb("sw", [TL, 128])
        xT = S.sb("xT", [D, 4 * L])
        u, t2, gg = S.sb("u", [128, 4, 2 * L]), S.sb("t2", [128, 4, 2 * L]), S.sb("gg", [128, 4, 2 * L])
        yT, h2 = S.sb("yT", [128, 2 * L]), S.sb("h2", [TL, 8, D])
        bank = S.banks()
        s_id, s_w, s_own = S.sem("ident"), S.sem("weights"), S.sem("settled")
        bc = lambda a, k: a.unsqueeze(2).to_broadcast([TL, k, D])

        with nc.Block() as block:
            V = Loop(S.sem("vector"), NORM_V + ["xr", "w"])
            A = Loop(S.sem("scalar"), ["std"])
            hin, out = Loop(S.sem("h_in"), ["h"], 16, 0), Loop(S.sem("out"), ["x"], 16, 0)
            s_v = S.sem("set")

            @block.gpsimd
            def _(e):
                make_identity(e, ident, s_id)

            @block.sync
            def _(e):
                e.dma_start(wrb[:, :], wr.rearrange("d a -> (d a)").partition_broadcast(TL)).then_inc(s_w, 16)
                e.dma_start(brb[:, :], br.partition_broadcast(TL)).then_inc(s_w, 16)
                e.dma_start(w1s[:, :], w1).then_inc(s_w, 16)
                e.dma_start(w2s[:, :, :], w2.rearrange("(a p) d -> p a d", a=2)).then_inc(s_w, 16)
                with nc.allow_non_contiguous_dma("biases, one an element"):
                    e.dma_start(b1s[:, :], b1.rearrange("(a p) -> p a", a=2)).then_inc(s_w, 16)
                for g in range(2):
                    e.dma_start(b2s[D * g:D * g + D, :], b2.rearrange("(d a) -> d a", a=1)).then_inc(s_w, 16)
                with e.Fori(0, G) as n:
                    V.wait(e, n, "cen", 1)
                    e.dma_start(ht[:, :, :].rearrange("p (b a) d -> p b (a d)", a=2), H1[bass.ds(4 * n, 4), :, :, :].rearrange("b p a d -> p b (a d)")).then_inc(hin.sem, 16)
                    V.wait(e, n, "xn")
                    e.dma_start(XN[bass.ds(4 * n, 4), :, :, :].rearrange("b p a d -> p b (a d)"), xn[:, :, :].rearrange("p (b a) d -> p b (a d)", a=2)).then_inc(out.sem, 16)
                out.count(e, G)

            @block.scalar
            def _(e):
                e.nop().then_inc(A.sem, A.P)
                e.preload_act_table(ACT.Sqrt)
                with e.Fori(0, G) as n:
                    norm_scalar(e, V, A, n, s2, eps)

            @block.vector
            def _(e):
                e.memset(eps[:, :], EPS).then_inc(s_v, 1)
                e.wait_ge(s_v, 1)
                e.nop().then_inc(V.sem, V.P)
                e.wait_ge(s_w, 16 * 7)
                with e.Fori(0, G) as n:
                    hin.wait(e, n, "h")
                    out.count(e, n)
                    V.wait(e, n, "w", 1)
                    norm_vector(e, V, A, n, ht[:, :, :], 8, (s1, s2, sq), xn[:, :, :])
                    V.wait(e, n, "xn")
                    e.tensor_tensor(sq[:, :, :], xn[:, :, :], wrb[:, :].unsqueeze(1).to_broadcast([TL, 8, D]), ALU.mult).then_inc(V.sem, 1)
                    V.wait(e, n, "xr")
                    e.tensor_reduce(wt[:, bass.ds(8 * n, 8)], sq[:, :, :], AX, ALU.add).then_inc(V.sem, 1)

        with nc.Block() as block:
            s_c, s_d, s_t = S.sem("choice"), S.sem("choice_dma"), S.sem("choice_turned")

            @block.tensor
            def _(e):
                e.wait_ge(s_c, 1)
                e.transpose(bank[0][:, 0:TL], wt[:, :], ident[0:TL, 0:TL]).then_inc(s_t, 1)
                e.wait_ge(s_d, 64)
                e.transpose(bank[1][0:TL, 0:128], swp[:, :], ident[:, :]).then_inc(s_t, 1)

            @block.sync
            def _(e):
                e.wait_ge(s_c, 2)
                e.dma_start(WD.rearrange("b (a t) -> (b a) t", a=2), wtt[:, :]).then_inc(s_d, 16)
                e.wait_ge(s_d, 16)
                e.dma_start(wv[:, :], WD).then_inc(s_d, 16)
                e.wait_ge(s_c, 3 + 2 * 15 + 9)
                e.dma_start(SW, pre[:, :]).then_inc(s_d, 16)
                e.wait_ge(s_d, 48)
                e.dma_start(swp[:, :], SW.rearrange("b (a t) -> (b a) t", a=2)).then_inc(s_d, 16)

            @block.vector
            def _(e):
                at = [0]

                def done(ins):
                    ins.then_inc(s_c, 1)
                    at[0] += 1
                    e.wait_ge(s_c, at[0])

                done(e.tensor_scalar(wt[:, :], wt[:, :], brb[:, 0:1], None, ALU.add))
                e.wait_ge(s_t, 1)
                done(e.tensor_copy(wtt[:, :], bank[0][:, 0:TL]))
                e.wait_ge(s_d, 32)
                done(e.tensor_copy(wk[:, :], wv[:, :]))
                rounds, last = divmod(TOPK - 1, 8)
                assert rounds == 15
                for _ in range(rounds):
                    done(e.max(m8[:, :], wk[:, :]))
                    done(e.match_replace(wk[:, :], m8[:, :], wk[:, :], -3.0e38))
                done(e.max(m8[:, :], wk[:, :]))
                thr = m8[:, last:last + 1]
                done(e.tensor_scalar(ge[:, :], wv[:, :], thr, None, ALU.is_gt))
                done(e.tensor_reduce(cnt[:, 0:1], ge[:, :], AX, ALU.add))
                done(e.tensor_scalar(cnt[:, 1:2], cnt[:, 0:1], -1.0, float(TOPK), ALU.mult, ALU.add))
                done(e.tensor_scalar(eq[:, :], wv[:, :], thr, None, ALU.is_equal))
                done(e.tensor_tensor_scan(pre[:, :], eq[:, :], eq[:, :], 0.0, ALU.add, ALU.bypass))
                done(e.scalar_tensor_tensor(out=eq[:, :], in0=pre[:, :], scalar=cnt[:, 1:2], in1=eq[:, :], op0=ALU.is_le, op1=ALU.mult))
                done(e.tensor_tensor(ge[:, :], ge[:, :], eq[:, :], ALU.add))
                done(e.tensor_tensor(pre[:, :], ge[:, :], wv[:, :], ALU.mult))
                e.wait_ge(s_t, 2)
                done(e.tensor_copy(sw[:, :], bank[1][0:TL, 0:128]))

        with nc.Block() as block:
            V = Loop(S.sem("vector2"), ["xT0"] + [f"{a}{i}" for i in range(4) for a in ("uu", "uv", "uw", "gg")] + ["yw", "hx", "h2"])
            A = Loop(S.sem("scalar2"), ["xT1"] + [f"{a}{i}" for i in range(4) for a in ("u", "th")] + ["yT"])
            T = Loop(S.sem("tensor2"), ["xT"] + [f"h{i}" for i in range(4)] + ["y", "turn"])
            hin, xin = Loop(S.sem("h_in2"), ["h"], 16, 0), Loop(S.sem("x_in2"), ["x"], 16, 0)
            out = Loop(S.sem("out2"), ["h"], 16, 0)
            s_v = S.sem("set2")
            grp = lambda t: t.rearrange("p (b a) d -> p b (a d)", a=2)
            dr = lambda t, n: t[bass.ds(4 * n, 4), :, :, :].rearrange("b p a d -> p b (a d)")

            @block.sync
            def _(e):
                with e.Fori(0, G) as n:
                    V.wait(e, n, "h2", 1)
                    e.dma_start(grp(xn[:, :, :]), dr(XN, n)).then_inc(xin.sem, 16)
                    e.dma_start(grp(ht[:, :, :]), dr(H1, n)).then_inc(hin.sem, 16)
                    V.wait(e, n, "h2")
                    e.dma_start(dr(H2, n), grp(h2[:, :, :])).then_inc(out.sem, 16)
                out.count(e, G)

            @block.tensor
            def _(e):
                e.nop().then_inc(T.sem, T.P)
                e.wait_ge(s_v, 1)
                with e.Fori(0, G) as n:
                    xin.wait(e, n, "x")
                    settled(e, s_own)
                    for k in range(8):
                        mm = e.transpose(bank[k // 4][0:D, TL * (k % 4):TL * (k % 4) + TL], xn[:, k, :], ident[0:TL, 0:TL])
                    mm.then_inc(T.sem, 1)
                    V.wait(e, n, "xT0")
                    A.wait(e, n, "xT1")
                    for i in range(4):
                        q, a = i // 2, i % 2
                        e.matmul(bank[2 + i][:, 0:2 * L], w1s[:, 128 * a:128 * a + 128], xT[:, 2 * L * q:2 * L * q + 2 * L],
                                 start=True, stop=True).then_inc(T.sem, 1)
                    V.wait(e, n, "gg3")
                    for a in range(2):
                        for q in range(2):
                            mm = e.matmul(bank[6][D * q:D * q + D, 0:2 * L], w2s[:, a, :], gg[:, 2 * q + a, :], start=(a == 0), stop=(a == 1))
                    mm.then_inc(T.sem, 1)
                    A.wait(e, n, "yT")
                    for k in range(4):
                        mm = e.transpose(bank[7][0:TL, 128 * k:128 * k + 128], yT[:, TL * k:TL * k + TL], ident[:, :])
                    mm.then_inc(T.sem, 1)

            @block.scalar
            def _(e):
                e.nop().then_inc(A.sem, A.P)
                e.preload_act_table(ACT.Tanh)
                with e.Fori(0, G) as n:
                    T.wait(e, n, "xT")
                    e.activation(xT[:, 2 * L:], bank[1][0:D, 0:2 * L], ACT.Copy).then_inc(A.sem, 1)
                    for i in range(4):
                        T.wait(e, n, f"h{i}")
                        e.activation(u[:, i, :], bank[2 + i][:, 0:2 * L], ACT.Identity, bias=b1s[:, i % 2:i % 2 + 1]).then_inc(A.sem, 1)
                        V.wait(e, n, f"uw{i}")
                        e.activation(t2[:, i, :], t2[:, i, :], ACT.Tanh, scale=0.7978845608028654).then_inc(A.sem, 1)
                    T.wait(e, n, "y")
                    e.activation(yT[:, :], bank[6][:, 0:2 * L], ACT.Identity, bias=b2s[:, 0:1]).then_inc(A.sem, 1)

            @block.vector
            def _(e):
                e.nop().then_inc(V.sem, V.P)
                e.tensor_scalar(w2s[:, :, :], w2s[:, :, :], 0.5, None, ALU.mult).then_inc(s_v, 1)
                with e.Fori(0, G) as n:
                    T.wait(e, n, "xT")
                    e.tensor_copy(xT[:, 0:2 * L], bank[0][0:D, 0:2 * L]).then_inc(V.sem, 1)
                    for i in range(4):
                        A.wait(e, n, f"u{i}")
                        e.tensor_tensor(t2[:, i, :], u[:, i, :], u[:, i, :], ALU.mult).then_inc(V.sem, 1)
                        V.wait(e, n, f"uu{i}")
                        e.tensor_scalar(t2[:, i, :], t2[:, i, :], 0.044715, 1.0, ALU.mult, ALU.add).then_inc(V.sem, 1)
                        V.wait(e, n, f"uv{i}")
                        e.tensor_tensor(t2[:, i, :], t2[:, i, :], u[:, i, :], ALU.mult).then_inc(V.sem, 1)
                        A.wait(e, n, f"th{i}")
                        e.scalar_tensor_tensor(out=gg[:, i, :], in0=t2[:, i, :], scalar=1.0, in1=u[:, i, :], op0=ALU.add, op1=ALU.mult).then_inc(V.sem, 1)
                    T.wait(e, n, "turn")
                    out.count(e, n)
                    e.tensor_tensor(h2[:, :, :].rearrange("p (q k) d -> p q k d", q=2),
                                    bank[7][0:TL, :].rearrange("p (k q d) -> p q k d", k=4, q=2),
                                    sw[:, bass.ds(8 * n, 8)].rearrange("p (q k) -> p q k", q=2).unsqueeze(3).to_broadcast([TL, 2, 4, D]), ALU.mult).then_inc(V.sem, 1)
                    hin.wait(e, n, "h")
                    e.tensor_tensor(xn[:, :, :], xn[:, :, :], ht[:, :, :], ALU.add).then_inc(V.sem, 1)
                    V.wait(e, n, "hx")
                    e.tensor_tensor(h2[:, :, :], h2[:, :, :], xn[:, :, :], ALU.add).then_inc(V.sem, 1)


def key_layer(nc, W_fused, H2, ZR, VR, GR):
    NF = 3 * D + 3
    with ExitStack() as ctx:
        S = Space(nc, ctx, "key")
        ident, eps = S.sb("ident", [128, 128]), S.sb("eps", [128, 1])
        wr, wT = S.sb("wr", [128, 2, D]), S.sb("wT", [D, NF])
        zero = S.sb("zero", [128, 64 * D])
        ht, xn, sq = S.sb("ht", [TL, 8, D]), S.sb("xn", [TL, 8, D]), S.sb("sq", [TL, 8, D])
        s1, s2 = S.sb("s1", [TL, 8]), S.sb("s2", [TL, 8])
        xT = S.sb("xT", [D, 4 * L])
        sg, kqv = S.sb("sg", [TL, 8, NF]), S.sb("kqv", [TL, 3, 8, D])
        k2, ss, gt = S.sb("k2", [TL, 16, D]), S.sb("ss", [TL, 16]), S.sb("gt", [TL, 8, 4])
        bank = S.banks()
        s_own, s_own_sp = S.sem("settled"), S.sem("settled_sp")
        s_id, s_w, s_z, s_v, s_t = S.sem("ident"), S.sem("weights"), S.sem("zeros"), S.sem("set_v"), S.sem("set_t")
        V = Loop(S.sem("vector"), NORM_V + ["xT0"] + [f"si{i}" for i in range(4)] + ["k2", "ss", "mx", "rn", "kn", "g0", "g1", "g2", "g3"])
        A = Loop(S.sem("scalar"), ["std", "xT1"] + [f"sg{i}" for i in range(4)] + ["nrm"])
        T = Loop(S.sem("tensor"), ["xT"] + [f"f{i}" for i in range(4)])
        hin = Loop(S.sem("h_in"), ["h"], 16, 0)
        out = Loop(S.sem("out"), ["z"], 16 * 8, 0)
        with nc.Block() as block:
            @block.gpsimd
            def _(e):
                make_identity(e, ident, s_id)

            @block.sync
            def _(e):
                e.dma_start(wr[:, 0, :], W_fused[0:128, :]).then_inc(s_w, 16)
                e.dma_start(wr[0:NF - 128, 1, :], W_fused[128:NF, :]).then_inc(s_w, 16)
                e.wait_ge(s_v, 1)
                z3 = lambda k: zero[:, 0:k * D].rearrange("p (t d) -> p t d", d=D)
                nz = 0
                for t0 in range(0, VR.shape[0], 64):
                    k = min(64, VR.shape[0] - t0)
                    e.dma_start(VR[t0:t0 + k, :, :].rearrange("t p d -> p t d"), z3(k)).then_inc(s_z, 16)
                    nz += 1
                e.dma_start(ZR[0:CH + 1, :, :].rearrange("t p d -> p t d"), z3(CH + 1)).then_inc(s_z, 16)
                k = ZR.shape[0] - CH - L
                e.dma_start(ZR[CH + L:, :, :].rearrange("t p d -> p t d"), z3(k)).then_inc(s_z, 16)
                e.dma_start(GR[:, L:, :], zero[0:B, 0:4 * (CH * NCH - L)].rearrange("p (t g) -> p t g", g=4)).then_inc(s_z, 16)
                e.wait_ge(s_z, 16 * (nz + 3))
                with e.Fori(0, 4) as j:
                    with e.Fori(0, 4) as q:
                        n = 4 * j + q
                        V.wait(e, n, "xn", 1)
                        settled(e, s_own_sp)
                        e.dma_start(ht[:, :, :].rearrange("p (b a) d -> p b (a d)", a=2),
                                    H2[bass.ds(4 * n, 4), :, :, :].rearrange("b p a d -> p b (a d)")).then_inc(hin.sem, 16)
                        V.wait(e, n, "g3")
                        settled(e, s_own_sp)
                        for a in range(2):
                            t0 = TL * a
                            for w, (dst, row) in enumerate(((ZR[CH + 1 + t0:CH + 1 + t0 + TL], 16), (ZR[CH + t0:CH + t0 + TL], 0), (VR[t0:t0 + TL], 0))):
                                e.dma_start(dst[:, bass.ds(32 * j + 4 * q + row, 4), :], kqv[:, w, a:8:2, :]).then_inc(out.sem, 16)
                            e.dma_start(GR[bass.ds(4 * n, 4), t0:t0 + TL, :].rearrange("b t g -> t b g"), gt[:, a:8:2, :]).then_inc(out.sem, 16)
                out.count(e, B // 4)

            @block.tensor
            def _(e):
                e.wait_ge(s_w, 32)
                e.wait_ge(s_id, 2)
                e.transpose(bank[0][0:D, 0:128], wr[:, 0, :], ident[:, :]).then_inc(s_t, 1)
                e.transpose(bank[0][0:D, 128:NF], wr[0:NF - 128, 1, :], ident[0:NF - 128, 0:NF - 128]).then_inc(s_t, 1)
                e.nop().then_inc(T.sem, T.P)
                e.wait_ge(s_v, 3)
                with e.Fori(0, B // 4) as n:
                    V.wait(e, n, "xn")
                    settled(e, s_own)
                    for k in range(8):
                        mm = e.transpose(bank[k // 4][0:D, TL * (k % 4):TL * (k % 4) + TL], xn[:, k, :], ident[0:TL, 0:TL])
                    mm.then_inc(T.sem, 1)
                    V.wait(e, n, "xT0")
                    A.wait(e, n, "xT1")
                    for i in range(4):
                        for a in range(2):
                            k = 2 * i + a
                            mm = e.matmul(bank[2 + i][0:TL, NF * a:NF * a + NF], xT[:, TL * k:TL * k + TL], wT[:, :], start=True, stop=True)
                        mm.then_inc(T.sem, 1)

            @block.scalar
            def _(e):
                e.nop().then_inc(A.sem, A.P)
                with e.Fori(0, B // 4) as n:
                    norm_scalar(e, V, A, n, s2, eps)
                    T.wait(e, n, "xT")
                    e.activation(xT[:, 2 * L:], bank[1][0:D, 0:2 * L], ACT.Copy).then_inc(A.sem, 1)
                    for i in range(4):
                        T.wait(e, n, f"f{i}")
                        V.wait(e, n, "g3", 1)
                        e.activation(sg[:, 2 * i:2 * i + 2, :], bank[2 + i][0:TL, 0:2 * NF].rearrange("p (a f) -> p a f", a=2), ACT.Sigmoid).then_inc(A.sem, 1)
                    V.wait(e, n, "ss")
                    e.activation(ss[:, :], ss[:, :], ACT.Sqrt).then_inc(A.sem, 1)

            @block.vector
            def _(e):
                e.memset(zero[:, :], 0.0).then_inc(s_v, 1)
                e.memset(eps[:, :], EPS).then_inc(s_v, 1)
                e.wait_ge(s_t, 2)
                e.tensor_copy(wT[:, :], bank[0][0:D, 0:NF]).then_inc(s_v, 1)
                e.wait_ge(s_v, 3)
                e.nop().then_inc(V.sem, V.P)
                with e.Fori(0, B // 4) as n:
                    hin.wait(e, n, "h")
                    V.wait(e, n, "g3", 1)
                    T.wait(e, n, "xT", 1)
                    norm_vector(e, V, A, n, ht[:, :, :], 8, (s1, s2, sq), xn[:, :, :])
                    T.wait(e, n, "xT")
                    e.tensor_copy(xT[:, 0:2 * L], bank[0][0:D, 0:2 * L]).then_inc(V.sem, 1)
                    out.count(e, n)
                    for i in range(4):
                        A.wait(e, n, f"sg{i}")
                        e.tensor_tensor(kqv[:, :, 2 * i:2 * i + 2, :].rearrange("p w a d -> p a w d"),
                                        bank[2 + i][0:TL, 0:2 * NF].rearrange("p (a f) -> p a f", a=2)[:, :, 0:3 * D].rearrange("p a (w d) -> p a w d", w=3),
                                        sg[:, 2 * i:2 * i + 2, 0:3 * D].rearrange("p a (w d) -> p a w d", w=3), ALU.mult).then_inc(V.sem, 1)
                    V.wait(e, n, "si3")
                    qk = kqv[:, 0:2, :, :].rearrange("p w k d -> p (w k) d")
                    e.tensor_tensor(k2[:, :, :], qk, qk, ALU.mult).then_inc(V.sem, 1)
                    V.wait(e, n, "k2")
                    e.tensor_reduce(ss[:, :], k2[:, :, :], AX, ALU.add).then_inc(V.sem, 1)
                    A.wait(e, n, "nrm")
                    e.tensor_scalar(ss[:, :], ss[:, :], 1e-12, None, ALU.max).then_inc(V.sem, 1)
                    V.wait(e, n, "mx")
                    e.reciprocal(ss[:, :], ss[:, :]).then_inc(V.sem, 1)
                    V.wait(e, n, "rn")
                    e.tensor_tensor(qk, qk, ss[:, :].unsqueeze(2).to_broadcast([TL, 16, D]), ALU.mult).then_inc(V.sem, 1)
                    e.tensor_copy(gt[:, :, 0:1], sg[:, :, NF - 1:NF]).then_inc(V.sem, 1)
                    e.tensor_scalar(gt[:, :, 1:2], sg[:, :, NF - 3:NF - 2], -1.0, 1.0, ALU.mult, ALU.add).then_inc(V.sem, 1)
                    e.tensor_scalar(gt[:, :, 2:3], sg[:, :, NF - 2:NF - 1], -0.1 * 4.0 / D, None, ALU.mult).then_inc(V.sem, 1)
                    V.wait(e, n, "g2")
                    e.tensor_copy(gt[:, :, 3:4], gt[:, :, 0:1]).then_inc(V.sem, 1)


def expert_layer(nc, Wg, bg, W1, b1, W2, b2, H2, YR, out_dram):
    G = B // 4
    E = NH
    with ExitStack() as ctx:
        S = Space(nc, ctx, "moe")
        ident, eps = S.sb("ident", [128, 128]), S.sb("eps", [128, 1])
        wraw = S.sb("wraw", [128, 2, HID])
        w1T, w2T = S.sb("w1T", [D, E, HID]), S.sb("w2T", [128, E, 2, D])
        wgr, wgT, bgb = S.sb("wgr", [E, D]), S.sb("wgT", [D, E]), S.sb("bgb", [TL, E])
        b1s, b2s = S.sb("b1s", [128, E, 2]), S.sb("b2s", [E, D])
        sel = S.sb("sel", [E, E, 128])
        tri = S.sb("tri", [128, E, E])
        ht, yt, xn, sq = S.sb("ht", [TL, 8, D]), S.sb("yt", [TL, 8, D]), S.sb("xn", [TL, 8, D]), S.sb("sq", [TL, 8, D])
        s1, s2 = S.sb("s1", [TL, 8]), S.sb("s2", [TL, 8])
        xT = S.sb("xT", [D, 4 * L])
        gs, rk, ex, mz = S.sb("gs", [TL, 8, E]), S.sb("rk", [TL, 8, E]), S.sb("ex", [TL, 8, E]), S.sb("mz", [TL, 2, 8])
        c1, c2 = S.sb("c1", [TL, 8, E, E]), S.sb("c2", [TL, 8, E, E])
        cT = S.sb("cT", [E, 4 * L])
        hb, hw = S.sb("hb", [128, 2, 2, 2 * L]), S.sb("hw", [128, 2, 2, 2 * L])
        yT, o = S.sb("yT", [128, 2 * L]), S.sb("o", [TL, 8, D])
        bank = S.banks()
        s_own, s_own_sp = S.sem("settled"), S.sem("settled_sp")
        s_id, s_w, s_v, s_t = S.sem("ident"), S.sem("weights"), S.sem("set_v"), S.sem("set_t")
        EH = [(x_, a) for x_ in range(E) for a in range(2)]
        V = Loop(S.sem("vector"), ["h3"] + NORM_V + ["xT0", "gs", "gt", "eq", "eqt", "cmp", "rk", "m1", "gm", "sel", "z", "rz", "cmb", "cT"] +
                 [f"w{x_}{a}{q}" for x_, a in EH for q in range(2)] + ["o"])
        A = Loop(S.sem("scalar"), ["std", "xT1", "exp", "cT1"] + [f"h{x_}{a}{q}" for x_, a in EH for q in range(2)] + ["yT"])
        order = []
        for i, (x_, a) in enumerate(EH):
            order += ([f"b{x_}0", f"b{x_}1"] if a == 0 else []) + [f"h{x_}{a}0", f"h{x_}{a}1"] + ([f"y{i - 1}"] if i else [])
        T = Loop(S.sem("tensor"), ["xT", "g", "cT"] + order + ["y15", "yb", "turn"])
        hin = Loop(S.sem("h_in"), ["h"], 48, 0)
        out = Loop(S.sem("out"), ["h"], 32, 0)
        with nc.Block() as block:
            @block.gpsimd
            def _(e):
                make_identity(e, ident, s_id)
                e.wait_ge(s_id, 2)
                e.memset(sel[:, :, :], 1.0).then_inc(s_id, 1)
                e.wait_ge(s_id, 3)
                e.affine_select(out=sel[:, :, :], in_=sel[:, :, :], compare_op=ALU.is_equal, fill=0.0, base=0,
                                pattern=[[-1, E], [0, 128]], channel_multiplier=1).then_inc(s_id, 1)
                e.wait_ge(s_id, 4)
                e.memset(tri[:, :, :], 1.0).then_inc(s_id, 1)
                e.wait_ge(s_id, 5)
                e.affine_select(out=tri[:, :, :], in_=tri[:, :, :], compare_op=ALU.is_gt, fill=0.0, base=0,
                                pattern=[[1, E], [-1, E]], channel_multiplier=0).then_inc(s_id, 1)

            @block.sync
            def _(e):
                e.dma_start(wgr[:, :], Wg).then_inc(s_w, 16)
                e.dma_start(bgb[:, :], bg.partition_broadcast(TL)).then_inc(s_w, 16)
                with nc.allow_non_contiguous_dma("biases, one an element"):
                    for a in range(2):
                        e.dma_start(b1s[:, :, a], b1[:, 128 * a:128 * a + 128].rearrange("e p -> p e")).then_inc(s_w, 16)
                e.dma_start(b2s[:, :], b2).then_inc(s_w, 16)
                for x_ in range(E):
                    if x_:
                        e.wait_ge(s_t, 1 + 4 * x_)
                    e.dma_start(wraw[:, 0, 0:2 * D].rearrange("p (a d) -> p a d", a=2), W1[x_].rearrange("(a p) d -> p a d", a=2)).then_inc(s_w, 16)
                    e.dma_start(wraw[0:D, 1, :], W2[x_]).then_inc(s_w, 16)
                with e.Fori(0, 4) as j:
                    with e.Fori(0, 4) as q:
                        n = 4 * j + q
                        V.wait(e, n, "o", 1)
                        e.dma_start(ht[:, :, :].rearrange("p (b a) d -> p b (a d)", a=2),
                                    H2[bass.ds(4 * n, 4), :, :, :].rearrange("b p a d -> p b (a d)")).then_inc(hin.sem, 16)
                        for a in range(2):
                            e.dma_start(yt[:, a:8:2, :], YR[1 + TL * a:1 + TL * a + TL, bass.ds(32 * j + 4 * q + 16, 4), :]).then_inc(hin.sem, 16)
                        V.wait(e, n, "o")
                        settled(e, s_own_sp)
                        for a in range(2):
                            e.dma_start(out_dram[bass.ds(4 * n, 4), TL * a:TL * a + TL, :].rearrange("b t d -> t b d"), o[:, a:8:2, :]).then_inc(out.sem, 16)
                out.count(e, G)

            @block.tensor
            def _(e):
                e.wait_ge(s_id, 2)
                e.wait_ge(s_w, 16 * 7)
                e.transpose(bank[0][0:D, 0:E], wgr[:, :], ident[0:E, 0:E]).then_inc(s_t, 1)
                for x_ in range(E):
                    e.wait_ge(s_w, 16 * (7 + 2 * x_))
                    if x_:
                        e.wait_ge(s_v, 2 + 2 * x_)
                    for a in range(2):
                        e.transpose(bank[1][0:D, 128 * a:128 * a + 128], wraw[:, 0, D * a:D * a + D], ident[:, :]).then_inc(s_t, 1)
                    for a in range(2):
                        e.transpose(bank[2][:, D * a:D * a + D], wraw[0:D, 1, 128 * a:128 * a + 128], ident[0:D, 0:D]).then_inc(s_t, 1)
                e.wait_ge(s_v, 2 + 2 * E)
                e.wait_ge(s_id, 6)
                e.nop().then_inc(T.sem, T.P)
                with e.Fori(0, G) as n:
                    V.wait(e, n, "xn")
                    settled(e, s_own)
                    for k in range(8):
                        mm = e.transpose(bank[k // 4][0:D, TL * (k % 4):TL * (k % 4) + TL], xn[:, k, :], ident[0:TL, 0:TL])
                    mm.then_inc(T.sem, 1)
                    V.wait(e, n, "xT0")
                    A.wait(e, n, "xT1")
                    for k in range(8):
                        mm = e.matmul(bank[2][0:TL, E * k:E * k + E], xT[:, TL * k:TL * k + TL], wgT[:, :], start=True, stop=True)
                    mm.then_inc(T.sem, 1)
                    V.wait(e, n, "cmb")
                    settled(e, s_own)
                    for k in range(8):
                        mm = e.transpose(bank[k // 4][0:E, TL * (k % 4):TL * (k % 4) + TL], ex[:, k, :], ident[0:TL, 0:TL])
                    mm.then_inc(T.sem, 1)
                    V.wait(e, n, "cT")
                    A.wait(e, n, "cT1")

                    def first(i):
                        x_, a = EH[i]
                        if a == 0:
                            if x_:
                                V.wait(e, n, f"w{x_ - 1}11")
                            for q in range(2):
                                e.matmul(bank[q][:, 0:2 * L], sel[:, x_, :], cT[:, 2 * L * q:2 * L * q + 2 * L], start=True, stop=True).then_inc(T.sem, 1)
                        if i >= 2:
                            A.wait(e, n, "h%d%d1" % EH[i - 2])
                        for q in range(2):
                            e.matmul(bank[2 + 2 * a + q][:, 0:2 * L], w1T[:, x_, 128 * a:128 * a + 128], xT[:, 2 * L * q:2 * L * q + 2 * L],
                                     start=True, stop=True).then_inc(T.sem, 1)

                    def second(i):
                        x_, a = EH[i]
                        V.wait(e, n, f"w{x_}{a}1")
                        for q in range(2):
                            mm = e.matmul(bank[6][D * q:D * q + D, 0:2 * L], w2T[:, x_, a, :], hw[:, a, q, :], start=(i == 0), stop=False)
                        return mm

                    for i in range(2 * E):
                        first(i)
                        if i:
                            second(i - 1).then_inc(T.sem, 1)
                    second(2 * E - 1).then_inc(T.sem, 1)
                    for q in range(2):
                        mm = e.matmul(bank[6][D * q:D * q + D, 0:2 * L], b2s[:, :], cT[:, 2 * L * q:2 * L * q + 2 * L], start=False, stop=True)
                    mm.then_inc(T.sem, 1)
                    A.wait(e, n, "yT")
                    for k in range(4):
                        mm = e.transpose(bank[7][0:TL, 128 * k:128 * k + 128], yT[:, TL * k:TL * k + TL], ident[:, :])
                    mm.then_inc(T.sem, 1)

            @block.scalar
            def _(e):
                e.nop().then_inc(A.sem, A.P)
                with e.Fori(0, G) as n:
                    norm_scalar(e, V, A, n, s2, eps)
                    T.wait(e, n, "xT")
                    e.activation(xT[:, 2 * L:], bank[1][0:D, 0:2 * L], ACT.Copy).then_inc(A.sem, 1)
                    V.wait(e, n, "gm")
                    e.activation(ex[:, :, :], gs[:, :, :], ACT.Exp).then_inc(A.sem, 1)
                    T.wait(e, n, "cT")
                    e.activation(cT[:, 2 * L:], bank[1][0:E, 0:2 * L], ACT.Copy).then_inc(A.sem, 1)
                    for i, (x_, a) in enumerate(EH):
                        for q in range(2):
                            T.wait(e, n, f"h{x_}{a}{q}")
                            if i >= 2:
                                V.wait(e, n, f"w{x_ - 1}{a}{q}")
                            e.activation(hb[:, a, q, :], bank[2 + 2 * a + q][:, 0:2 * L], ACT.Relu, bias=b1s[:, x_, a:a + 1]).then_inc(A.sem, 1)
                    T.wait(e, n, "yb")
                    e.activation(yT[:, :], bank[6][:, 0:2 * L], ACT.Copy).then_inc(A.sem, 1)

            @block.vector
            def _(e):
                e.memset(eps[:, :], EPS).then_inc(s_v, 1)
                e.wait_ge(s_t, 1)
                e.tensor_copy(wgT[:, :], bank[0][0:D, 0:E]).then_inc(s_v, 1)
                for x_ in range(E):
                    e.wait_ge(s_t, 1 + 4 * x_ + 4)
                    e.tensor_copy(w1T[:, x_, :], bank[1][0:D, 0:HID]).then_inc(s_v, 1)
                    e.tensor_copy(w2T[:, x_, :, :].rearrange("p a d -> p (a d)"), bank[2][:, 0:2 * D]).then_inc(s_v, 1)
                e.wait_ge(s_v, 2 + 2 * E)
                e.wait_ge(s_id, 6)
                e.nop().then_inc(V.sem, V.P)
                tok = lambda t: t.unsqueeze(2).to_broadcast([TL, 8, E])
                flat = lambda t: t[:, :, :, :].rearrange("p k x y -> p (k x) y")
                with e.Fori(0, G) as n:
                    hin.wait(e, n, "h")
                    e.tensor_tensor(ht[:, :, :], ht[:, :, :], yt[:, :, :], ALU.add).then_inc(V.sem, 1)
                    V.wait(e, n, "h3")
                    norm_vector(e, V, A, n, ht[:, :, :], 8, (s1, s2, sq), xn[:, :, :])
                    T.wait(e, n, "xT")
                    e.tensor_copy(xT[:, 0:2 * L], bank[0][0:D, 0:2 * L]).then_inc(V.sem, 1)
                    T.wait(e, n, "g")
                    e.tensor_tensor(gs[:, :, :], bank[2][0:TL, 0:8 * E].rearrange("p (k x) -> p k x", x=E),
                                    bgb[:, :].unsqueeze(1).to_broadcast([TL, 8, E]), ALU.add).then_inc(V.sem, 1)
                    V.wait(e, n, "gs")
                    mine = gs[:, :, :].unsqueeze(3).to_broadcast([TL, 8, E, E])
                    other = gs[:, :, :].unsqueeze(2).to_broadcast([TL, 8, E, E])
                    e.tensor_tensor(c1[:, :, :, :], other, mine, ALU.is_gt).then_inc(V.sem, 1)
                    e.tensor_tensor(c2[:, :, :, :], other, mine, ALU.is_equal).then_inc(V.sem, 1)
                    V.wait(e, n, "eq")
                    trif = tri[0:TL, :, :].rearrange("p x y -> p (x y)").unsqueeze(1).to_broadcast([TL, 8, E * E])
                    pairs = lambda t: t[:, :, :, :].rearrange("p k x y -> p k (x y)")
                    e.tensor_tensor(pairs(c2), pairs(c2), trif, ALU.mult).then_inc(V.sem, 1)
                    V.wait(e, n, "eqt")
                    e.tensor_tensor(c1[:, :, :, :], c1[:, :, :, :], c2[:, :, :, :], ALU.add).then_inc(V.sem, 1)
                    V.wait(e, n, "cmp")
                    e.tensor_reduce(rk[:, :, :], c1[:, :, :, :], AX, ALU.add).then_inc(V.sem, 1)
                    e.tensor_reduce(mz[:, 0, :], gs[:, :, :], AX, ALU.max).then_inc(V.sem, 1)
                    V.wait(e, n, "m1")
                    e.tensor_tensor(gs[:, :, :], gs[:, :, :], tok(mz[:, 0, :]), ALU.subtract).then_inc(V.sem, 1)
                    A.wait(e, n, "exp")
                    V.wait(e, n, "rk")
                    e.scalar_tensor_tensor(out=ex[:, :, :], in0=rk[:, :, :], scalar=1.5, in1=ex[:, :, :], op0=ALU.is_lt, op1=ALU.mult).then_inc(V.sem, 1)
                    V.wait(e, n, "sel")
                    e.tensor_reduce(mz[:, 1, :], ex[:, :, :], AX, ALU.add).then_inc(V.sem, 1)
                    V.wait(e, n, "z")
                    e.reciprocal(mz[:, 1, :], mz[:, 1, :]).then_inc(V.sem, 1)
                    V.wait(e, n, "rz")
                    e.tensor_tensor(ex[:, :, :], ex[:, :, :], tok(mz[:, 1, :]), ALU.mult).then_inc(V.sem, 1)
                    T.wait(e, n, "cT")
                    e.tensor_copy(cT[:, 0:2 * L], bank[0][0:E, 0:2 * L]).then_inc(V.sem, 1)
                    for i, (x_, a) in enumerate(EH):
                        for q in range(2):
                            A.wait(e, n, f"h{x_}{a}{q}")
                            T.wait(e, n, f"b{x_}{q}" if a == 0 or i < 2 else f"y{i - 2}")
                            e.tensor_tensor(hw[:, a, q, :], hb[:, a, q, :], bank[q][:, 0:2 * L], ALU.mult).then_inc(V.sem, 1)
                    T.wait(e, n, "turn")
                    out.count(e, n)
                    e.tensor_tensor(o[:, :, :].rearrange("p (q k) d -> p q k d", q=2),
                                    bank[7][0:TL, :].rearrange("p (k q d) -> p q k d", k=4, q=2),
                                    ht[:, :, :].rearrange("p (q k) d -> p q k d", q=2), ALU.add).then_inc(V.sem, 1)


class Stages:

    def __init__(self, sem, update, step, unit=1):
        self.sem, self.unit = sem, unit
        self.update, self.steps = update, step
        self.U, self.P = len(update), len(step)
        self.base = self.P
        assert len(set(step)) == self.P and len(set(update)) == self.U
        self.su = {n: i + 1 for i, n in enumerate(step)}
        self.uu = {n: i + 1 for i, n in enumerate(update)}
        self.chunk = self.U + CH * self.P

    def begun(self, c):
        return c * (self.chunk * self.unit) + self.base * self.unit

    def upd(self, c, name):
        return c * (self.chunk * self.unit) + (self.base + self.uu[name]) * self.unit

    def step(self, c, s, name, back=0):
        k = self.base + self.U + self.su[name] - back * self.P
        return c * (self.chunk * self.unit) + s * (self.P * self.unit) + k * self.unit


def recurrent_layer(nc, ZR, VR, GR, YR, S0D, BASED, DOTSD, W0, P0, W1, P1):
    with ExitStack() as ctx:
        def sb(name, shape):
            return ctx.enter_context(nc.sbuf_tensor(name, shape, F32))

        def sem(name):
            return ctx.enter_context(nc.semaphore(name))

        HD, D = 256, 64
        MW = CH + 2 * D
        mv1 = sb("mv1", [128, 2, 16, 4, MW])
        mvt = sb("mvt", [128, 32, 2 * HD])
        hist = sb("hist", [128, 8, 2 * HD + D])
        yth = sb("yth", [128, 32, CH])
        hdiag = sb("hdiag", [128, 2, 16, 4, 32])
        ydiag = sb("ydiag", [128, 8, 4, 32])
        gdiag = sb("gdiag", [128, 2, 4, 32])
        ddiag = sb("ddiag", [128, 2, 4, 32])
        adiag = sb("adiag", [128, 2, 4, 32])
        ident = sb("r_ident", [128, 128])
        ones = sb("r_ones", [128, 128])
        repl = sb("repl", [128, 128])
        mi = sb("mi", [128, 8])
        mu = sb("mu", [128, 2])
        xb = sb("xb", [128, HD])
        work = sb("work", [128, 4, HD])
        x, sg, om, sp = (work[:, q, :] for q in range(4))
        h = sb("h", [128, HD])
        dh = sb("dh", [128, HD])
        dl = sb("dl", [128, HD])
        rep = sb("rep", [128, 3, 8, CH])
        y1 = sb("y1", [128, D])
        y = sb("y", [128, 2, D])
        al = sb("al", [128, 1])
        U = sb("U", [128, CH + 2])
        W = sb("W", [128, CH + 2])
        FAC = sb("FAC", [128, CH + 2])
        Wp = sb("Wp", [128, CH + 2])
        Wn = sb("Wn", [128, CH + 2])
        gates = sb("gates", [128, CH, 4])
        baset = sb("baset", [128, 2 * HD])
        dott = sb("dott", [128, CH])
        vt = sb("vt", [128, D])
        cm = sb("cm", [128, 2, 128])
        cu = sb("cu", [128, 3, 8, 4])
        wy = sb("wy", [128, 2, 2, D])
        wk = sb("wk", [128, 2, 2, D])
        s0s = sb("s0s", [128, 2, 2 * HD])
        zr = sb("zr", [CH * 2, 2, 128])
        ztm = sb("ztm", [128, 2, 32])
        kt = sb("kt", [128, CH])
        krow = sb("krow", [128, 8, D])
        bs = work[:, :, :].rearrange("p (u a) f -> p u (a f)", u=2)
        dsb = sb("dsb", [128, 2, CH])
        d3 = work[:, :, :].rearrange("p a b -> p (a b)")[:, 0:384].rearrange("p (w q) -> p w q", w=3)
        bank = [ctx.enter_context(nc.psum_tensor(f"bank{i}", [128, 512], F32)) for i in range(8)]
        b = [t[:, :] for t in bank]
        psT = (b[0][:, 0:128], b[1][:, 0:128])
        psDT = b[0][:, 128:256]
        psP, psD = b[2], b[2][:, 256:256 + CH]
        psAT, psYT = b[3][:, 0:128], b[3][:, 128:256]
        psGT, psY = b[4][:, 0:128], b[4][:, 128:128 + D]
        psH = b[5]
        psR, psA = b[6][:, 0:HD], b[6][:, HD:2 * HD]
        psE = b[7]
        psZ, psDots, psC, psBase = b[0][:, 0:32], b[1], b[6], (b[3], b[4])

        SLABS = [(n, j) for n in range(8) for j in range(4)]
        vec_u = ["nfac", "srep", "cm0", "cm1", "d3a", "d3b", "d3c", "cu0", "cu1"]
        for k in range(32):
            vec_u += [f"{a}{k}" for a in ("wy", "wk", "sa", "sb", "sn", "oa", "ob", "on", "kt", "ztm")]
        vec_u += ["rw", "rw1", "ru", "ru1", "rf", "rf1", "rp", "ral", "x0"]
        vec_s = ["x", "h", "hd0", "om", "sp", "tabu", "tabw", "tabp", "arep", "alast", "xb1", "xb2",
                 "grep", "adiag", "y1", "y2", "gdiag", "y", "ydiag", "drep", "ddiag", "dh1", "dh2",
                 "setu", "setw", "setf", "setn", "newp", "xpre", "dh3", "d"]
        act_u = []
        for k in range(32):
            act_u += [f"c0{k}", f"c1{k}"] + ([f"bs0{k}", f"bs1{k}", f"ds{k}"] if k % 4 == 3 else [])
        act_s = ["sig", "hd1", "ht", "yt0", "yt1"]
        pe_u = ["ct0", "ct1", "cb"]
        for k in range(32):
            pe_u += [f"zt{k}", f"st{k}", f"so{k}", f"tr{k}", f"ba{k}"]
        pe_s = ["tr", "pred", "at", "sprep", "gt", "a", "yp", "yt", "dd", "dhp", "dt", "e"]
        V = Stages(sem("vector_landed"), vec_u, vec_s)
        A = Stages(sem("scalar_landed"), act_u, act_s)
        T = Stages(sem("tensor_landed"), pe_u, pe_s)
        slab_in = [Stages(sem(f"slab_in{q}"), [f"s{k}" for k in range(q, 32, 2)], [], 16) for q in range(2)]
        zr_in = [Stages(sem(f"zr_in{q}"), [f"z{k}" for k in range(q, 32, 2)], [], 32) for q in range(2)]
        slab_out = Stages(sem("slab_out"), [f"s{k}" for k in range(32)], [], 16)
        base_out = Stages(sem("base_out"), [f"b{n}" for n in range(8)], [], 64)
        chunk_in = Stages(sem("chunk_in"), ["in"], [], 24 * 16)
        base_in = Stages(sem("base_in"), ["first"], ["next"], 32)
        value_in = Stages(sem("value_in"), ["first"], ["next"], 16)
        hist_h = Stages(sem("hist_h"), [], ["h"], 16 * NH)
        hist_y = Stages(sem("hist_y"), [], ["y"], 16 * (NH + 1))
        hist_d = Stages(sem("hist_d"), [], ["d"], 16 * NH)
        for q in (*slab_in, *zr_in, slab_out, base_out, chunk_in, base_in, value_in, hist_h, hist_y, hist_d):
            q.base = 0
        s_set, s_own = sem("set_dma"), sem("settled")
        s_pool = sem("pool_set")
        s_v = sem("vec_set")
        s_p = sem("pe_set")
        s_init = sem("init_out")

        def ap(t, off, *dims):
            row = 1
            for q in t.shape[1:]:
                row *= q
            return bass.AP(t, off, [[row, t.shape[0]]] + [list(q) for q in dims])

        def p_dims(src, off=0):
            return src

        w1s, p1s = x[:, 0:128], x[:, 128:256]
        with nc.Block() as block:
            @block.gpsimd
            def _(e):
                e.memset(ident[:, :], 0.0).then_inc(s_pool, 1)
                e.memset(mi[:, :], 1.0).then_inc(s_pool, 1)
                e.memset(mu[:, :], 1.0).then_inc(s_pool, 1)
                e.wait_ge(s_pool, 3)
                e.affine_select(out=ident[:, :], in_=ident[:, :], compare_op=ALU.not_equal, fill=1.0, base=0,
                                pattern=[[-1, 128]], channel_multiplier=1).then_inc(s_pool, 1)
                for k, (t, w, c) in enumerate(((mi, 8, 16), (mu, 2, 64))):
                    e.affine_select(out=t[:, :], in_=t[:, :], compare_op=ALU.is_ge, fill=0.0, base=0,
                                    pattern=[[-c, w]], channel_multiplier=1).then_inc(s_pool, 1)
                    e.wait_ge(s_pool, 5 + 2 * k)
                    e.affine_select(out=t[:, :], in_=t[:, :], compare_op=ALU.is_ge, fill=0.0, base=c - 1,
                                    pattern=[[c, w]], channel_multiplier=-1).then_inc(s_pool, 1)
                    e.wait_ge(s_pool, 6 + 2 * k)
                e.memset(mv1[:, :, :, :, :], 0.0).then_inc(s_pool, 1)
                e.memset(hdiag[:, :, :, :, :], 0.0).then_inc(s_pool, 1)
                e.memset(hist[:, :, :], 0.0).then_inc(s_pool, 1)

            @block.sync
            def _(e):
                e.dma_start(w1s.rearrange("p (a d) -> p a d", a=2), W1.rearrange("(a p) d -> p a d", p=128)).then_inc(s_set, 16)
                e.dma_start(p1s.rearrange("p (a d) -> p a d", a=2), P1.rearrange("(a p) d -> p a d", p=128)).then_inc(s_set, 16)
                for u in range(2):
                    e.dma_start(sg[64 * u:64 * u + 64, :], W0).then_inc(s_set, 16)
                    e.dma_start(h[64 * u:64 * u + 64, :], P0).then_inc(s_set, 16)
                e.wait_ge(s_v, 7)
                for k in range(32):
                    e.dma_start(S0D[k, :, :], s0s[:, 0, :]).then_inc(s_init, 16)
                e.dma_start(BASED[CH, :, :], s0s[:, 0, :]).then_inc(s_init, 16)
                e.dma_start(DOTSD[CH, :, :], yth[:, 0, :]).then_inc(s_init, 16)
                e.wait_ge(s_init, 34 * 16)

            @block.vector
            def _(e):
                e.wait_ge(s_set, 96)
                e.memset(mvt[:, :, :], 0.0).then_inc(s_v, 1)
                e.memset(s0s[:, 0, HD:], 0.0).then_inc(s_v, 1)
                e.memset(ydiag[:, :, :, :], 0.0).then_inc(s_v, 1)
                e.tensor_tensor(s0s[:, 0, 0:HD], sg, h[:, :], ALU.add).then_inc(s_v, 1)
                for u in range(2):
                    e.tensor_tensor(om.rearrange("p (a u d) -> p a u d", a=2, u=2)[:, :, u, :],
                                    w1s.rearrange("p (a d) -> p a d", a=2),
                                    p1s.rearrange("p (a d) -> p a d", a=2), ALU.add).then_inc(s_v, 1)
                e.memset(yth[:, :, :], 0.0).then_inc(s_v, 1)
                for t in (gdiag, ddiag, adiag):
                    e.memset(t[:, :, :, :], 0.0).then_inc(s_v, 1)
                e.memset(ones[:, :], 1.0).then_inc(s_v, 1)
                e.memset(U[:, :], 0.0).then_inc(s_v, 1)
                e.memset(Wp[:, :], 0.0).then_inc(s_v, 1)
                e.memset(FAC[:, :], 1.0).then_inc(s_v, 1)
                e.memset(y[:, :, :], 0.0).then_inc(s_v, 1)
                e.memset(dl[:, :], 0.0).then_inc(s_v, 1)
                e.wait_ge(s_v, 16)
                e.memset(U[:, CH + 1:CH + 2], 1.0).then_inc(s_v, 1)
                e.memset(Wp[:, CH:CH + 1], 1.0).then_inc(s_v, 1)
                e.wait_ge(s_pool, 4)
                for st in range(2):
                    e.tensor_copy(ap(repl, 16 * st, [32, 4], [1, 16]), ap(ident, 0, [32, 4], [1, 16])).then_inc(s_v, 1)
                e.wait_ge(s_p, 2)
                for a in range(2):
                    e.tensor_copy(mvt[:, :, 128 * a:128 * a + 128], psT[a].unsqueeze(1).to_broadcast([128, 32, 128])).then_inc(s_v, 1)
                e.wait_ge(s_v, 22)
                e.engine_nop().then_inc(V.sem, V.base)

            @block.tensor
            def _(e):
                e.wait_ge(s_v, 6)
                e.wait_ge(s_pool, 4)
                for a in range(2):
                    e.transpose(psT[a], om[:, 128 * a:128 * a + 128], ident[:, :]).then_inc(s_p, 1)
                e.wait_ge(s_p, 2)
                e.nop().then_inc(T.sem, T.base)

            @block.scalar
            def _(e):
                e.nop().then_inc(A.sem, A.base)

        def load_base(e, s):
            e.dma_start(baset[:, :].unsqueeze(1), BASED[s:s + 1, :, :].rearrange("a p f -> p a f")).then_inc(base_in.sem, 16)
            e.dma_start(dott[:, :].unsqueeze(1), DOTSD[s:s + 1, :, :].rearrange("a p f -> p a f")).then_inc(base_in.sem, 16)

        def load_value(e, c, s):
            e.dma_start(vt[:, :].unsqueeze(1), VR[bass.ds(c * CH + s, 1), :, :].rearrange("a p f -> p a f")).then_inc(value_in.sem, 16)

        def to_hist(e, s, src, lo, hi, sm):
            for m in range(2):
                for j in range(4):
                    row = 8 * (2 * HD + D)
                    dst = bass.AP(hist, s * row + (m * 4 + j) * (2 * HD + D) + lo, [[CH * row, 8], [1, hi - lo]])
                    p = 32 * j + 8 * m
                    e.dma_start(dst, src[p:p + 8, :]).then_inc(sm, 16)

        def slab_done(e, c, k):
            e.wait_ge(T.sem, T.upd(c, f"ba{k}"))
            settled(e, s_own)
            e.wait_ge(V.sem, V.upd(c, f"on{k}"))
            e.dma_start(S0D[k, :, :], s0s[:, k % 2, :]).then_inc(slab_out.sem, 16)
            if k % 4 == 3:
                n = k // 4
                e.wait_ge(A.sem, A.upd(c, f"ds{k}"))
                for u in range(2):
                    dst = BASED[0:CH, :, :].rearrange("t (q r) f -> r q t f", r=16)[2 * n + u]
                    e.dma_start(dst, bs[:, u, :]).then_inc(base_out.sem, 16)
                    dst = DOTSD[0:CH, :, :].rearrange("t (q r) f -> r q t f", r=16)[2 * n + u]
                    e.dma_start(dst, dsb[:, u, :]).then_inc(base_out.sem, 16)

        def diag_h(hf):
            return ap(hdiag, hf * 2048, [16, 8], [129, 16])

        def turned_h(hf):
            return psT[hf].rearrange("p (q r) -> p q r", r=16)

        def spread(dst, src):
            return (ap(dst, 0, [16, 8], [136, 2], [1, 8]), src.rearrange("p (q m i) -> p q m i", q=8, m=2),
                    ap(mi, 0, [0, 8], [0, 2], [1, 8]), ALU.mult)

        with nc.Block() as block:
            @block.sync
            def _(e):
                with e.Fori(0, NCH) as c:
                    e.wait_ge(V.sem, V.begun(c))
                    e.wait_ge(T.sem, T.begun(c))
                    e.wait_ge(A.sem, A.begun(c))
                    for q in range(8):
                        e.dma_start(gates[16 * q:16 * q + 16, :, :],
                                    GR[16 * (q // 2):16 * (q // 2) + 16, bass.ds(c * CH, CH), :]).then_inc(chunk_in.sem, 16)
                    for i in range(8):
                        for m in range(2):
                            src = ZR[bass.ds(c * CH, CH), :, :].rearrange("t (j st m i) d -> i st m t j d", j=4, st=2, m=2)[i, 0, m]
                            e.dma_start(krow[16 * i:16 * i + 16, 4 * m:4 * m + 4, :], src).then_inc(chunk_in.sem, 16)
                    for k, (n, j) in enumerate(SLABS):
                        kb = k % 2
                        if k >= 2:
                            e.wait_ge(slab_out.sem, slab_out.upd(c, f"s{k - 2}"))
                            settled(e, s_own)
                            e.wait_ge(T.sem, T.upd(c, f"zt{k - 2}"))
                        e.dma_start(s0s[:, kb, :], S0D[k, :, :]).then_inc(slab_in[kb].sem, 16)
                        for st in range(2):
                            src = ZR[bass.ds(c * CH + CH, CH), :, :].rearrange("t (q n u) d -> t q n (u d)", q=8, n=8)
                            e.dma_start(zr[16 * st:16 * st + 16, kb, :], src[:, 2 * j + st, n, :]).then_inc(zr_in[kb].sem, 16)
                        if k >= 1:
                            slab_done(e, c, k - 1)
                    slab_done(e, c, 31)
                    e.wait_ge(slab_out.sem, slab_out.upd(c, "s31"))
                    e.wait_ge(base_out.sem, base_out.upd(c, "b7"))
                    load_base(e, 0)
                    load_value(e, c, 0)
                    for s in range(CH):
                        e.wait_ge(V.sem, V.step(c, s - 1, "xb2") if s else V.upd(c, "x0"))
                        load_base(e, s + 1)
                        e.wait_ge(V.sem, V.step(c, s, "h"))
                        to_hist(e, s, h[:, :], 0, HD, hist_h.sem)
                        e.wait_ge(V.sem, V.step(c, s, "y1"))
                        load_value(e, c, s + 1)
                        e.wait_ge(V.sem, V.step(c, s, "y"))
                        to_hist(e, s, y[:, 0, :], HD, HD + D, hist_y.sem)
                        e.dma_start(YR[bass.ds(c * CH + s, 1), :, :].rearrange("a p d -> p a d"), y[:, 0:1, :]).then_inc(hist_y.sem, 16)
                        e.wait_ge(V.sem, V.step(c, s, "d"))
                        to_hist(e, s, dl[:, :], HD + D, 2 * HD + D, hist_d.sem)
                e.wait_ge(hist_h.sem, hist_h.unit * CH * NCH)
                e.wait_ge(hist_y.sem, hist_y.unit * CH * NCH)
                e.wait_ge(hist_d.sem, hist_d.unit * CH * NCH)

            @block.scalar
            def _(e):
                e.preload_act_table(ACT.Sigmoid)
                with e.Fori(0, NCH) as c:
                    for k, (n, j) in enumerate(SLABS):
                        e.wait_ge(T.sem, T.upd(c, f"tr{k}"))
                        for hf in range(2):
                            src = psC[:, 256 * hf:256 * hf + 256].rearrange("p (w u d) -> p u w d", w=2, u=2)
                            dst = mv1[:, hf, 2 * n:2 * n + 2, j, CH:].rearrange("p u (w d) -> p u w d", w=2)
                            e.activation(dst, src, ACT.Copy).then_inc(A.sem, 1)
                        if k % 4 == 3:
                            e.wait_ge(T.sem, T.upd(c, f"ba{k}"))
                            if k > 3:
                                e.wait_ge(base_out.sem, base_out.upd(c, f"b{n - 1}"))
                            e.wait_ge(T.sem, T.upd(c, "cb"))
                            for u in range(2):
                                e.activation(bs[:, u, :], (psBase[0], psBase[1])[u], ACT.Copy).then_inc(A.sem, 1)
                            e.activation(dsb[:, :, :], psDots[:, 0:2 * CH].rearrange("p (u s) -> p u s", u=2), ACT.Copy).then_inc(A.sem, 1)
                    with e.Fori(0, CH) as s:
                        e.wait_ge(V.sem, V.step(c, s, "x"))
                        e.activation(sg, x, ACT.Sigmoid).then_inc(A.sem, 1)
                        e.wait_ge(T.sem, T.step(c, s, "tr"))
                        e.activation(diag_h(1), turned_h(1), ACT.Copy).then_inc(A.sem, 1)
                        e.wait_ge(T.sem, T.step(c, s, "pred"))
                        src = ap(hdiag, 0, [2048, 2], [129, 16], [32, 4])
                        dst = mv1[:, :, :, :, bass.ds(s, 1)].rearrange("p a r j o -> p a r (j o)")
                        e.activation(dst, src, ACT.Copy).then_inc(A.sem, 1)
                        e.wait_ge(T.sem, T.step(c, s, "dd"))
                        for u in range(2):
                            src = bass.AP(ydiag, 64 * u * 1024 + u, [[1024, 64], [130, 8], [32, 4]])
                            dst = yth[64 * u:64 * u + 64, :, bass.ds(s, 1)].rearrange("p (n j) o -> p n (j o)", n=8)
                            e.activation(dst, src, ACT.Copy).then_inc(A.sem, 1)

            @block.tensor
            def _(e):
                with e.Fori(0, NCH) as c:
                    for w in range(2):
                        e.wait_ge(V.sem, V.upd(c, "srep"))
                        e.matmul(psP[:, 128 * w:128 * w + 128], rep[:, w, :, :].rearrange("p i s -> p (i s)"), ident[:, :],
                                 start=True, stop=True).then_inc(T.sem, 1)
                    e.wait_ge(V.sem, V.upd(c, "d3c"))
                    e.matmul(psH[:, 0:384], ones[:, :], d3.rearrange("p w q -> p (w q)"), start=True, stop=True).then_inc(T.sem, 1)
                    for k, (n, j) in enumerate(SLABS):
                        kb, slot = k % 2, (n // 4) * 4 + j
                        e.wait_ge(zr_in[kb].sem, zr_in[kb].upd(c, f"z{k}"))
                        if k:
                            e.wait_ge(V.sem, V.upd(c, f"ztm{k - 1}"))
                        e.matmul(psZ, zr[:, kb, :], ident[0:32, 0:32], start=True, stop=True).then_inc(T.sem, 1)
                        e.wait_ge(V.sem, V.upd(c, f"wk{k}"))
                        if k == 0:
                            e.wait_ge(V.sem, V.upd(c, "cu1"))
                            e.wait_ge(hist_h.sem, c * (hist_h.unit * CH))
                            e.wait_ge(hist_d.sem, c * (hist_d.unit * CH))
                        for w in range(2):
                            mm = e.matmul(psH[:, HD * w:HD * w + HD], wy[:, w, :, :].rearrange("p u d -> p (u d)"),
                                          hist[:, slot, 0:HD], start=True, stop=True)
                        mm.then_inc(T.sem, 1)
                        for w in range(2):
                            mm = e.matmul(psE[:, HD * w:HD * w + HD], wk[:, w, :, :].rearrange("p u d -> p (u d)"),
                                          hist[:, slot, HD + D:], start=True, stop=True)
                        mm.then_inc(T.sem, 1)
                        e.wait_ge(V.sem, V.upd(c, f"sn{k}"))
                        if k:
                            e.wait_ge(A.sem, A.upd(c, f"c1{k - 1}"))
                        for hf in range(2):
                            for w in range(2):
                                o = 256 * hf + 128 * w
                                mm = e.transpose(psC[:, o:o + 128], mvt[:, k, HD * w + 128 * hf:HD * w + 128 * hf + 128], ident[:, :])
                        mm.then_inc(T.sem, 1)
                        e.wait_ge(V.sem, V.upd(c, f"ztm{k}"))
                        if k % 4 == 0 and k:
                            e.wait_ge(A.sem, A.upd(c, f"ds{k - 1}"))
                        for u in range(2):
                            rows = slice(32 * j, 32 * j + 32)
                            e.matmul((psBase[0], psBase[1])[u][rows, :], ztm[:, u, :], s0s[:, kb, :], start=True, stop=True)
                            mm = e.matmul(psDots[rows, CH * u:CH * u + CH], ztm[:, u, :], kt[:, :], start=True, stop=True)
                        mm.then_inc(T.sem, 1)
                    with e.Fori(0, CH) as s:
                        e.wait_ge(V.sem, V.step(c, s, "h"))
                        e.wait_ge(A.sem, A.step(c, s, "yt1", 1))
                        for hf in range(2):
                            mm = e.transpose(psT[hf], h[:, 128 * hf:128 * hf + 128], ident[:, :])
                        mm.then_inc(T.sem, 1)
                        for hf in range(2):
                            if hf == 0:
                                e.wait_ge(V.sem, V.step(c, s, "hd0"))
                            else:
                                e.wait_ge(A.sem, A.step(c, s, "hd1"))
                            for r in range(16):
                                for j in range(4):
                                    mm = e.matmul(psP[32 * j:32 * j + 32, 0:MW], hdiag[:, hf, r, j, :], mv1[:, hf, r, j, :],
                                                  start=(hf == 0 and r == 0), stop=(hf == 1 and r == 15))
                        mm.then_inc(T.sem, 1)
                        e.wait_ge(V.sem, V.step(c, s, "arep"))
                        e.matmul(psAT, rep[:, 0, :, :].rearrange("p i s -> p (i s)"), ident[:, :], start=True, stop=True).then_inc(T.sem, 1)
                        e.wait_ge(V.sem, V.step(c, s, "sp"))
                        e.matmul(psR, repl[:, :], sp, start=True, stop=True).then_inc(T.sem, 1)
                        e.wait_ge(V.sem, V.step(c, s, "grep"))
                        e.matmul(psGT, rep[:, 1, :, :].rearrange("p i s -> p (i s)"), ident[:, :], start=True, stop=True).then_inc(T.sem, 1)
                        e.wait_ge(V.sem, V.step(c, s, "adiag"))
                        e.wait_ge(hist_d.sem, c * (hist_d.unit * CH) + s * hist_d.unit)
                        for m in range(2):
                            for j in range(4):
                                mm = e.matmul(psA[32 * j:32 * j + 32, :], adiag[:, m, j, :], hist[:, m * 4 + j, HD + D:],
                                              start=(m == 0), stop=(m == 1))
                        mm.then_inc(T.sem, 1)
                        e.wait_ge(V.sem, V.step(c, s, "gdiag"))
                        e.wait_ge(hist_y.sem, c * (hist_y.unit * CH) + s * hist_y.unit)
                        for m in range(2):
                            for j in range(4):
                                mm = e.matmul(psY[32 * j:32 * j + 32, :], gdiag[:, m, j, :], hist[:, m * 4 + j, HD:HD + D],
                                              start=(m == 0), stop=(m == 1))
                        mm.then_inc(T.sem, 1)
                        e.wait_ge(V.sem, V.step(c, s, "y"))
                        e.matmul(psYT, y[:, :, :].rearrange("p u d -> p (u d)"), repl[:, :], start=True, stop=True).then_inc(T.sem, 1)
                        e.wait_ge(V.sem, V.step(c, s, "ydiag"))
                        for n in range(8):
                            for j in range(4):
                                mm = e.matmul(psD[32 * j:32 * j + 32, :], ydiag[:, n, j, :], yth[:, 4 * n + j, :],
                                              start=(n == 0), stop=(n == 7))
                        mm.then_inc(T.sem, 1)
                        for n in range(8):
                            for j in range(4):
                                mm = e.matmul(psH[32 * j:32 * j + 32, :], ydiag[:, n, j, :], mvt[:, 4 * n + j, :],
                                              start=(n == 0), stop=(n == 7))
                        mm.then_inc(T.sem, 1)
                        e.wait_ge(V.sem, V.step(c, s, "drep"))
                        e.matmul(psDT, rep[:, 2, :, :].rearrange("p i s -> p (i s)"), ident[:, :], start=True, stop=True).then_inc(T.sem, 1)
                        e.wait_ge(V.sem, V.step(c, s, "ddiag"))
                        e.wait_ge(hist_h.sem, hist_h.step(c, s, "h"))
                        for m in range(2):
                            for j in range(4):
                                mm = e.matmul(psE[32 * j:32 * j + 32, 0:HD], ddiag[:, m, j, :], hist[:, m * 4 + j, 0:HD],
                                              start=(m == 0), stop=(m == 1))
                        mm.then_inc(T.sem, 1)

            @block.vector
            def _(e):
                def own(val):
                    e.wait_ge(V.sem, val)

                with e.Fori(0, NCH) as c:
                    def go(ins, name):
                        ins.then_inc(V.sem, 1)

                    own(V.begun(c))
                    N16, N17 = slice(CH, CH + 1), slice(CH + 1, CH + 2)
                    go(e.tensor_tensor(Wn[:, :], U[:, :], FAC[:, :], ALU.mult), "nfac")
                    own(V.upd(c, "nfac"))
                    e.wait_ge(T.sem, T.begun(c))
                    for w, t in enumerate((Wp, Wn)):
                        ins = e.tensor_copy(rep[:, w, :, :], t[:, 0:CH].unsqueeze(1).to_broadcast([128, 8, CH]))
                    go(ins, "srep")
                    for w in range(2):
                        e.wait_ge(T.sem, T.upd(c, "ct1"))
                        go(e.tensor_tensor(cm[:, w, :].rearrange("p (q i) -> p q i", i=8),
                                           psP[:, 128 * w:128 * w + 128].rearrange("p (q i) -> p q i", i=8),
                                           ap(mi, 0, [0, 16], [1, 8]), ALU.mult), "cm")
                    e.wait_ge(A.sem, A.begun(c))
                    e.wait_ge(base_out.sem, c * (base_out.unit * 8))
                    for w, col in enumerate((Wp[:, N16], Wp[:, N17], Wn[:, N17])):
                        go(e.tensor_scalar(d3[:, w, :], ident[:, :], col, None, ALU.mult), "d3")
                    e.wait_ge(T.sem, T.upd(c, "cb"))
                    for u in range(2):
                        src = psH[64 * u:64 * u + 64, 0:384].rearrange("p (w j st n u) -> p w st u n j", w=3, j=4, st=2, u=2)[:, :, 0, u]
                        go(e.tensor_copy(cu[64 * u:64 * u + 64, :, :, :], src), "cu")
                    own(V.upd(c, "cu1"))
                    e.wait_ge(chunk_in.sem, chunk_in.upd(c, "in"))
                    e.wait_ge(hist_y.sem, c * (hist_y.unit * CH))
                    for k, (n, j) in enumerate(SLABS):
                        kb, slot = k % 2, (n // 4) * 4 + j
                        if k:
                            e.wait_ge(T.sem, T.upd(c, f"so{k - 1}"))
                        wt = cm[:, :, 32 * j + 2 * n:32 * j + 2 * n + 2].unsqueeze(3).to_broadcast([128, 2, 2, D])
                        for t, row, name in ((wy, hist[:, slot, HD:HD + D], "wy"), (wk, krow[:, slot, :], "wk")):
                            src = row.unsqueeze(1).unsqueeze(1).to_broadcast([128, 2, 2, D])
                            go(e.tensor_tensor(t[:, :, :, :], src, wt, ALU.mult), name)
                        ca, cb, ce = (cu[:, w, n, j:j + 1] for w in range(3))
                        e.wait_ge(slab_in[kb].sem, slab_in[kb].upd(c, f"s{k}"))
                        for t, ps, names, need in ((mvt[:, k, :], psH, ("sa", "sb", "sn"), f"st{k}"),
                                                   (s0s[:, kb, :], psE, ("oa", "ob", "on"), f"so{k}")):
                            e.wait_ge(T.sem, T.upd(c, need))
                            go(e.scalar_tensor_tensor(out=t[:, 0:HD], in0=t[:, 0:HD], scalar=ca, in1=ps[:, 0:HD],
                                                      op0=ALU.mult, op1=ALU.add), names[0])
                            own(V.upd(c, names[0] + str(k)))
                            go(e.scalar_tensor_tensor(out=t[:, 0:HD], in0=t[:, HD:], scalar=cb, in1=t[:, 0:HD],
                                                      op0=ALU.mult, op1=ALU.add), names[1])
                            own(V.upd(c, names[1] + str(k)))
                            go(e.scalar_tensor_tensor(out=t[:, HD:], in0=t[:, HD:], scalar=ce, in1=ps[:, HD:2 * HD],
                                                      op0=ALU.mult, op1=ALU.add), names[2])
                        e.wait_ge(T.sem, T.upd(c, f"zt{k}"))
                        if k:
                            e.wait_ge(T.sem, T.upd(c, f"ba{k - 1}"))
                        go(e.tensor_copy(kt[:, :], psZ[:, 0:CH]), "kt")
                        go(e.tensor_tensor(ztm[:, :, :], psZ.unsqueeze(1).to_broadcast([128, 2, 32]),
                                           mu[:, :].unsqueeze(2).to_broadcast([128, 2, 32]), ALU.mult), "ztm")
                    own(V.upd(c, "ztm31"))
                    go(e.memset(W[:, :], 0.0), "rw")
                    own(V.upd(c, "rw"))
                    go(e.memset(W[:, N16], 1.0), "rw1")
                    go(e.memset(U[:, :], 0.0), "ru")
                    own(V.upd(c, "ru"))
                    go(e.memset(U[:, N17], 1.0), "ru1")
                    go(e.memset(FAC[:, 0:CH], 0.0), "rf")
                    go(e.memset(FAC[:, CH:], 1.0), "rf1")
                    own(V.upd(c, "rf1"))
                    go(e.tensor_copy(Wp[:, :], W[:, :]), "rp")
                    go(e.memset(al[:, :], 0.0), "ral")
                    e.wait_ge(base_in.sem, base_in.upd(c, "first"))
                    go(e.tensor_copy(xb[:, :], baset[:, 0:HD]), "x0")
                    with e.Fori(0, CH) as s:
                        def st(name, back=0):
                            return V.step(c, s, name, back)

                        nm = lambda ins: ins.then_inc(V.sem, 1)
                        if True:
                            own(V.upd(c, "x0") + s * V.P)
                            nm(e.scalar_tensor_tensor(out=x, in0=dl[:, :], scalar=al[:, 0:1], in1=xb[:, :],
                                                      op0=ALU.mult, op1=ALU.add))
                            e.wait_ge(A.sem, A.step(c, s, "sig"))
                            e.wait_ge(hist_h.sem, c * (hist_h.unit * CH) + s * hist_h.unit)
                            nm(e.tensor_tensor(h[:, :], x, sg, ALU.mult))
                            e.wait_ge(T.sem, T.step(c, s, "tr"))
                            e.wait_ge(A.sem, A.step(c, s, "yt1", 1))
                            nm(e.tensor_copy(diag_h(0), turned_h(0)))
                            nm(e.scalar_tensor_tensor(out=om, in0=sg, scalar=1.0, in1=h[:, :],
                                                      op0=ALU.subtract, op1=ALU.mult))
                            own(st("om"))
                            nm(e.tensor_tensor(sp, sg, om, ALU.subtract))
                            g = lambda q: gates[:, bass.ds(s, 1), q:q + 1].rearrange("p a b -> p (a b)")
                            nm(e.tensor_scalar(U[:, :], U[:, :], g(0), None, ALU.mult))
                            own(st("tabu"))
                            nm(e.scalar_tensor_tensor(out=W[:, :], in0=W[:, :], scalar=g(1), in1=U[:, :],
                                                      op0=ALU.mult, op1=ALU.add))
                            own(st("tabw"))
                            nm(e.tensor_tensor(Wn[:, :], W[:, :], FAC[:, :], ALU.mult))
                            e.wait_ge(base_in.sem, base_in.step(c, s, "next"))
                            own(st("tabp"))
                            nm(e.tensor_tensor(rep[:, 0, :, :], dott[:, :].unsqueeze(1).to_broadcast([128, 8, CH]),
                                               Wn[:, 0:CH].unsqueeze(1).to_broadcast([128, 8, CH]), ALU.mult))
                            nm(e.tensor_scalar(al[:, :], dott[:, bass.ds(s, 1)], g(2), None, ALU.mult))
                            nm(e.tensor_scalar(xb[:, :], baset[:, 0:HD], Wn[:, N16], None, ALU.mult))
                            own(st("xb1"))
                            nm(e.scalar_tensor_tensor(out=xb[:, :], in0=baset[:, HD:], scalar=Wn[:, N17], in1=xb[:, :],
                                                      op0=ALU.mult, op1=ALU.add))
                            e.wait_ge(T.sem, T.step(c, s, "pred"))
                            nm(e.tensor_tensor(rep[:, 1, :, :], psP[:, 0:CH].unsqueeze(1).to_broadcast([128, 8, CH]),
                                               Wp[:, 0:CH].unsqueeze(1).to_broadcast([128, 8, CH]), ALU.mult))
                            e.wait_ge(T.sem, T.step(c, s, "at"))
                            nm(e.tensor_tensor(*spread(adiag, psAT)))
                            e.wait_ge(value_in.sem, value_in.upd(c, "first") + s * 16)
                            nm(e.scalar_tensor_tensor(out=y1[:, :], in0=psP[:, CH:CH + D], scalar=Wp[:, N16], in1=vt[:, :],
                                                      op0=ALU.mult, op1=ALU.subtract))
                            own(st("y1"))
                            nm(e.scalar_tensor_tensor(out=y1[:, :], in0=psP[:, CH + D:MW], scalar=Wp[:, N17], in1=y1[:, :],
                                                      op0=ALU.mult, op1=ALU.add))
                            e.wait_ge(T.sem, T.step(c, s, "gt"))
                            nm(e.tensor_tensor(*spread(gdiag, psGT)))
                            e.wait_ge(T.sem, T.step(c, s, "yp"))
                            own(st("y2"))
                            e.wait_ge(hist_y.sem, c * (hist_y.unit * CH) + s * hist_y.unit)
                            nm(e.tensor_tensor(y[:, :, :], psY.unsqueeze(1).to_broadcast([128, 2, D]),
                                               y1[:, :].unsqueeze(1).to_broadcast([128, 2, D]), ALU.add))
                            e.wait_ge(T.sem, T.step(c, s, "yt"))
                            nm(e.tensor_tensor(ap(ydiag, 0, [16, 8], [130, 8], [1, 2]),
                                               psYT.rearrange("p (q n u) -> p q n u", q=8, n=8),
                                               ap(mu, 0, [0, 8], [0, 8], [1, 2]), ALU.mult))
                            e.wait_ge(T.sem, T.step(c, s, "dd"))
                            nm(e.tensor_tensor(rep[:, 2, :, :], psD.unsqueeze(1).to_broadcast([128, 8, CH]),
                                               Wp[:, 0:CH].unsqueeze(1).to_broadcast([128, 8, CH]), ALU.mult))
                            e.wait_ge(T.sem, T.step(c, s, "dt"))
                            nm(e.tensor_tensor(*spread(ddiag, psDT)))
                            e.wait_ge(T.sem, T.step(c, s, "dhp"))
                            nm(e.tensor_scalar(dh[:, :], psH[:, 0:HD], Wp[:, N16], None, ALU.mult))
                            own(st("dh1"))
                            nm(e.scalar_tensor_tensor(out=dh[:, :], in0=psH[:, HD:], scalar=Wp[:, N17], in1=dh[:, :],
                                                      op0=ALU.mult, op1=ALU.add))
                            own(st("dh2"))
                            nm(e.tensor_copy(U[:, bass.ds(s, 1)], ones[:, 0:1]))
                            nm(e.tensor_copy(W[:, bass.ds(s, 1)], ones[:, 0:1]))
                            nm(e.tensor_copy(FAC[:, bass.ds(s, 1)], g(2)))
                            nm(e.tensor_copy(Wn[:, bass.ds(s, 1)], g(2)))
                            own(st("setn"))
                            nm(e.tensor_copy(Wp[:, :], Wn[:, :]))
                            e.wait_ge(T.sem, T.step(c, s, "a"))
                            nm(e.tensor_tensor(xb[:, :], xb[:, :], psA, ALU.add))
                            e.wait_ge(T.sem, T.step(c, s, "e"))
                            nm(e.tensor_tensor(dh[:, :], dh[:, :], psE[:, 0:HD], ALU.add))
                            own(st("dh3"))
                            e.wait_ge(hist_d.sem, c * (hist_d.unit * CH) + s * hist_d.unit)
                            nm(e.tensor_tensor(dl[:, :], dh[:, :], psR, ALU.mult))


def audio_tower(nc, x, filt, W_k, b_k, Wqk, Wv, Wpos, bpos, Wproj, bproj, gating, wr, br, w1, b1, w2, b2,
                W_fused, W0, W1, P0, P1, Wg, bg, E1, be1, E2, be2, out):
    def scratch(name, *shape):
        return nc.dram_tensor(f"between_{name}", shape, F32, kind="Internal").ap()

    H0, H1, H2, XN = (scratch(n, B, TL, 2, D) for n in ("h_tok", "h_att", "h_ffn", "x_ffn"))
    T_ = CH * NCH
    ZR, VR, YR = scratch("keys", T_ + CH + 1, 128, D), scratch("values", T_ + 1, 128, D), scratch("recurrent", T_, 128, D)
    GR = scratch("gates", B, T_, 4)
    token_layer(nc, x, filt, W_k, b_k, H0)
    attention_layer(nc, Wqk, Wv, Wpos, bpos, Wproj, bproj, gating, H0, H1)
    ffn_layer(nc, wr, br, w1, b1, w2, b2, H1, H2, XN, scratch("w_by_tile", B, L), scratch("w_by_batch", B, L))
    key_layer(nc, W_fused, H2, ZR, VR, GR)
    recurrent_layer(nc, ZR, VR, GR, YR, scratch("state0", 32, 128, 512), scratch("base", CH + 1, 128, 512),
                    scratch("dots", CH + 1, 128, CH), W0, P0, W1, P1)
    expert_layer(nc, Wg, bg, E1, be1, E2, be2, H2, YR, out)


_INS = ['x', 'L0_tok_filt', 'L0_tok_W_k', 'L0_tok_b_k', 'L0_attn_Wqk', 'L0_attn_Wv', 'L0_attn_Wpos', 'L0_attn_bpos',
        'L0_attn_Wproj', 'L0_attn_bproj', 'L0_attn_gating', 'L0_ffn_wr', 'L0_ffn_br', 'L0_ffn_w1', 'L0_ffn_b1',
        'L0_ffn_w2', 'L0_ffn_b2', 'L1_attn_W_fused', 'L1_attn_W0', 'L1_attn_W1', 'L1_attn_P0', 'L1_attn_P1',
        'L1_ffn_Wg', 'L1_ffn_bg', 'L1_ffn_W1', 'L1_ffn_b1', 'L1_ffn_W2', 'L1_ffn_b2']
_OUTS = [((64, 248, 64), 'float32')]


def kernel(**inputs):
    import numpy as _np
    import concourse.bacc as _bacc
    from concourse import mybir as _mybir
    from concourse.bass_utils import run_bass_kernel_spmd as _run

    nc = _bacc.Bacc("TRN2", target_bir_lowering=False, num_devices=1)
    arrays, args = {}, []
    for name in _INS:
        a = _np.ascontiguousarray(inputs[name])
        arrays[f"in_{name}_dram"] = a
        args.append(nc.dram_tensor(f"in_{name}_dram", a.shape, _mybir.dt.from_np(a.dtype), kind="ExternalInput").ap())
    for i, (shape, dtype) in enumerate(_OUTS):
        dt = _mybir.dt.from_np(_np.dtype(dtype))
        args.append(nc.dram_tensor(f"out_{i}_dram", shape, dt, kind="ExternalOutput").ap())
    audio_tower(nc, *args)
    r = _run(nc, [arrays], core_ids=[0])
    got = tuple(r.results[0][f"out_{i}_dram"] for i in range(len(_OUTS)))
    return got[0]
```

```python
from contextlib import ExitStack

import concourse.bass as bass
from concourse import mybir

F32 = mybir.dt.float32
BF16 = mybir.dt.bfloat16
ALU = mybir.AluOpType
ACT = mybir.ActivationFunctionType
AX = mybir.AxisListType.X

B, L, D, DIN, HID = 64, 248, 64, 128, 256
TL = L // 2
FS = 8
NH = 8
CH, NCH = 16, 16
TOPK = L // 2 - 1
EPS = 1e-5


class Loop:

    def __init__(self, sem, names, unit=1, before=None):
        self.sem, self.unit, self.P = sem, unit, len(names)
        assert len(set(names)) == len(names)
        self.index = {n: i + 1 for i, n in enumerate(names)}
        self.before = self.P if before is None else before

    def wait(self, e, n, name, back=0):
        e.wait_ge(self.sem, n * (self.P * self.unit) + (self.before + self.index[name] - back * self.P) * self.unit)

    def count(self, e, n):
        e.wait_ge(self.sem, n * (self.P * self.unit))


class Space:

    def __init__(self, nc, ctx, name):
        self.nc, self.ctx, self.name = nc, ctx, name

    def sb(self, name, shape, dtype=F32):
        return self.ctx.enter_context(self.nc.sbuf_tensor(f"{self.name}_{name}", shape, dtype))

    def sem(self, name):
        return self.ctx.enter_context(self.nc.semaphore(f"{self.name}_{name}"))

    def banks(self):
        return [self.ctx.enter_context(self.nc.psum_tensor(f"{self.name}_bank{i}", [128, 512], F32))[:, :] for i in range(8)]


def make_identity(e, ident, sem):
    e.memset(ident[:, :], 0.0).then_inc(sem, 1)
    e.wait_ge(sem, 1)
    e.affine_select(out=ident[:, :], in_=ident[:, :], compare_op=ALU.not_equal, fill=1.0, base=0,
                    pattern=[[-1, 128]], channel_multiplier=1).then_inc(sem, 1)


def norm_vector(e, V, A, n, x, K, t, xn):
    s, q, sq = t
    bc = lambda a: a[:, :].unsqueeze(2).to_broadcast([TL, K, D])
    e.tensor_reduce(s[:, :], x, AX, ALU.add).then_inc(V.sem, 1)
    V.wait(e, n, "mean")
    e.tensor_scalar(s[:, :], s[:, :], 1.0 / D, None, ALU.mult).then_inc(V.sem, 1)
    V.wait(e, n, "meand")
    e.tensor_tensor(xn, x, bc(s), ALU.subtract).then_inc(V.sem, 1)
    V.wait(e, n, "cen")
    e.tensor_tensor(sq[:, :, :], xn, xn, ALU.mult).then_inc(V.sem, 1)
    V.wait(e, n, "sq")
    e.tensor_reduce(q[:, :], sq[:, :, :], AX, ALU.add).then_inc(V.sem, 1)
    A.wait(e, n, "std")
    e.reciprocal(q[:, :], q[:, :]).then_inc(V.sem, 1)
    V.wait(e, n, "rstd")
    e.tensor_tensor(xn, xn, bc(q), ALU.mult).then_inc(V.sem, 1)


def settled(e, sem):
    e.nop().then_inc(sem, 1)


NORM_V = ["mean", "meand", "cen", "sq", "ssq", "rstd", "xn"]


def norm_scalar(e, V, A, n, q, eps):
    V.wait(e, n, "ssq")
    e.activation(q[:, :], q[:, :], ACT.Sqrt, bias=eps[0:TL, 0:1], scale=1.0 / D).then_inc(A.sem, 1)


def token_layer(nc, x, filt, W_k, b_k, H0):
    with ExitStack() as ctx:
        S = Space(nc, ctx, "tok")
        ident = S.sb("ident", [128, 128])
        wf, wk, ft, bk = S.sb("wf", [DIN, FS, D]), S.sb("wk", [DIN, FS, D]), S.sb("ft", [DIN, FS]), S.sb("bk", [128, 1])
        xin, xt = S.sb("xin", [128, 8, DIN]), S.sb("xt", [DIN, 4, 256])
        ht, hrow = S.sb("ht", [128, 2 * L]), S.sb("hrow", [TL, 8, D])
        bank = S.banks()
        s_id, s_w, s_wf = S.sem("ident"), S.sem("weights"), S.sem("filtered")
        V = Loop(S.sem("vector"), ["xt", "row"])
        A = Loop(S.sem("scalar"), ["xt", "relu"])
        T = Loop(S.sem("tensor"), ["xt", "conv", "turn"])
        xin_in = Loop(S.sem("x_in"), ["x"], 16, 0)
        out = Loop(S.sem("out"), ["h"], 16, 0)
        with nc.Block() as block:
            @block.gpsimd
            def _(e):
                make_identity(e, ident, s_id)

            @block.sync
            def _(e):
                e.dma_start(wk[:, :, :], W_k.rearrange("(f d) k -> d f k", f=FS)).then_inc(s_w, 16)
                with nc.allow_non_contiguous_dma("a filter of 4 KB, turned"):
                    e.dma_start(ft[:, :], filt.rearrange("f d -> d f")).then_inc(s_w, 16)
                for g in range(2):
                    e.dma_start(bk[D * g:D * g + D, :], b_k.rearrange("(d a) -> d a", a=1)).then_inc(s_w, 16)
                with e.Fori(0, B // 4) as n:
                    T.wait(e, n, "xt", 1)
                    e.dma_start(xin[:, :, :], x[bass.ds(4 * n, 4), :, :].rearrange("b (c p) d -> p (b c) d", p=128)).then_inc(xin_in.sem, 16)
                    V.wait(e, n, "row")
                    e.dma_start(H0[bass.ds(4 * n, 4), :, :, :].rearrange("b p a d -> p b (a d)"),
                                hrow[:, :, :].rearrange("p (b a) d -> p b (a d)", a=2)).then_inc(out.sem, 16)
                out.count(e, B // 4)

            @block.tensor
            def _(e):
                e.wait_ge(s_id, 2)
                e.wait_ge(s_wf, 1)
                e.nop().then_inc(T.sem, T.P)
                with e.Fori(0, B // 4) as n:
                    xin_in.wait(e, n, "x")
                    V.wait(e, n, "xt", 1)
                    A.wait(e, n, "xt", 1)
                    for k in range(8):
                        mm = e.transpose(bank[k // 4][:, 128 * (k % 4):128 * (k % 4) + 128], xin[:, k, :], ident[:, :])
                    mm.then_inc(T.sem, 1)
                    V.wait(e, n, "xt")
                    A.wait(e, n, "xt")
                    A.wait(e, n, "relu", 1)
                    for f in range(FS):
                        for g in range(2):
                            mm = e.matmul(bank[2][D * g:D * g + D, 0:2 * L], wf[:, f, :], xt[:, 2 * g:2 * g + 2, f:f + L],
                                          start=(f == 0), stop=(f == FS - 1))
                    mm.then_inc(T.sem, 1)
                    A.wait(e, n, "relu")
                    V.wait(e, n, "row", 1)
                    for q in range(4):
                        mm = e.transpose(bank[3][0:TL, 128 * q:128 * q + 128], ht[:, TL * q:TL * q + TL], ident[:, :])
                    mm.then_inc(T.sem, 1)

            @block.scalar
            def _(e):
                e.nop().then_inc(A.sem, A.P)
                e.preload_act_table(ACT.Relu)
                with e.Fori(0, B // 4) as n:
                    T.wait(e, n, "xt")
                    T.wait(e, n, "conv", 1)
                    e.activation(xt[:, 2:4, :], bank[1].rearrange("p (a l) -> p a l", a=2), ACT.Copy).then_inc(A.sem, 1)
                    T.wait(e, n, "conv")
                    T.wait(e, n, "turn", 1)
                    e.activation(ht[:, :], bank[2][:, 0:2 * L], ACT.Relu, bias=bk[:, 0:1]).then_inc(A.sem, 1)

            @block.vector
            def _(e):
                e.wait_ge(s_w, 64)
                e.tensor_tensor(wf[:, :, :], wk[:, :, :], ft[:, :].unsqueeze(2).to_broadcast([DIN, FS, D]), ALU.mult).then_inc(s_wf, 1)
                e.nop().then_inc(V.sem, V.P)
                with e.Fori(0, B // 4) as n:
                    T.wait(e, n, "xt")
                    T.wait(e, n, "conv", 1)
                    e.tensor_copy(xt[:, 0:2, :], bank[0].rearrange("p (a l) -> p a l", a=2)).then_inc(V.sem, 1)
                    T.wait(e, n, "turn")
                    out.count(e, n)
                    e.tensor_copy(hrow[:, :, :].rearrange("p (g q) d -> p g q d", g=2),
                                  bank[3][0:TL, :].rearrange("p (q g d) -> p g q d", q=4, g=2)).then_inc(V.sem, 1)


def attention_layer(nc, Wqk, Wv, Wpos, bpos, Wproj, bproj, gating, H0, H1):
    with ExitStack() as ctx:
        S = Space(nc, ctx, "att")
        ident = S.sb("ident", [128, 128])
        w_raw = S.sb("w_raw", [128, 3, D])
        wT = S.sb("wT", [D + 1, 4, D])
        prm = S.sb("prm", [TL, 40])
        hm = S.sb("hm", [D, NH])
        dist, dist2, cst = S.sb("dist", [TL, 2, L]), S.sb("dist2", [TL, 2, L]), S.sb("cst", [TL, NH])
        pe, pst = S.sb("pe", [TL, L]), S.sb("pst", [TL, 4])
        rt = S.sb("rt", [TL, NH, 2, L])
        omg, sgg = S.sb("omg", [TL, 2, 2, 4]), S.sb("sgg", [TL, 2, 2, 4])
        eps = S.sb("eps", [128, 1])
        ht, xn, sq = S.sb("ht", [TL, 2, D]), S.sb("xn", [TL, 2, D]), S.sb("sq", [TL, 2, D])
        s1, s2 = S.sb("s1", [TL, 2]), S.sb("s2", [TL, 2])
        xT = S.sb("xT", [D, L])
        qa, ka = S.sb("qa", [D + NH, L]), S.sb("ka", [D + NH, NH, L])
        va = S.sb("va", [TL, 2, NH, 32])
        mx = S.sb("mx", [TL, 2, NH])
        ex = S.sb("ex", [TL, NH, 2, L])
        evs, rvs = S.sb("evs", [128, 2 * L]), S.sb("rvs", [128, 2 * L])
        rz, num, rv = S.sb("rz", [TL, 16]), S.sb("num", [TL, 16, 9]), S.sb("rv", [TL, 16, 9])
        at, aT, h1 = S.sb("at", [TL, 2, D]), S.sb("aT", [D + 1, L]), S.sb("h1", [TL, 2, D])
        bank = S.banks()
        s_id, s_w, s_v, s_t, s_a, s_own = S.sem("ident"), S.sem("weights"), S.sem("set_v"), S.sem("set_t"), S.sem("set_a"), S.sem("settled")
        V = Loop(S.sem("vector"), NORM_V + ["xT", "q", "k", "v"] + [f"mx{i}" for i in range(8)] +
                 ["nm", "evs", "rz", "rzg", "num", "rv", "sum", "rd", "at0", "at1", "aT", "h1"])
        A = Loop(S.sem("scalar"), ["std"] + [f"e{h}" for h in range(NH)] + ["rvs"])
        T = Loop(S.sem("tensor"), ["xT", "qk", "v"] + [f"s{i}" for i in range(8)] + ["nm"] + [f"st{h}" for h in range(NH)] +
                 ["ev", "rv", "te", "tr", "aT", "pr"])
        hin = Loop(S.sem("h_in"), ["h"], 16, 0)
        out = Loop(S.sem("out"), ["h"], 16, 0)
        with nc.Block() as block:
            @block.gpsimd
            def _(e):
                make_identity(e, ident, s_id)
                e.wait_ge(s_id, 2)
                e.memset(hm[:, :], 1.0).then_inc(s_id, 1)
                e.wait_ge(s_id, 3)
                e.memset(ka[D:, :, :], 1.0).then_inc(s_id, 1)
                e.wait_ge(s_id, 4)
                e.memset(va[:, :, :, :], 0.0).then_inc(s_id, 1)
                e.wait_ge(s_id, 5)
                e.affine_select(out=hm[:, :], in_=hm[:, :], compare_op=ALU.is_ge, fill=0.0, base=0,
                                pattern=[[-8, NH]], channel_multiplier=1).then_inc(s_id, 1)
                e.wait_ge(s_id, 6)
                e.affine_select(out=hm[:, :], in_=hm[:, :], compare_op=ALU.is_ge, fill=0.0, base=7,
                                pattern=[[8, NH]], channel_multiplier=-1).then_inc(s_id, 1)
                e.wait_ge(s_id, 7)
                e.affine_select(out=ka[D:, :, :], in_=ka[D:, :, :], compare_op=ALU.is_equal, fill=0.0, base=0,
                                pattern=[[-1, NH], [0, L]], channel_multiplier=1).then_inc(s_id, 1)
                e.wait_ge(s_id, 8)
                e.iota(dist[:, :, :], pattern=[[-TL, 2], [1, L]], base=0, channel_multiplier=-1,
                       allow_small_or_imprecise_dtypes=True).then_inc(s_id, 1)
                e.wait_ge(s_id, 9)
                e.memset(va[:, :, :, 8:9], 1.0).then_inc(s_id, 1)
                e.wait_ge(s_id, 10)
                e.memset(aT[D:D + 1, :], 1.0).then_inc(s_id, 1)

            @block.sync
            def _(e):
                e.dma_start(w_raw[:, 0, :], Wqk).then_inc(s_w, 16)
                e.dma_start(w_raw[0:D, 1, :], Wv).then_inc(s_w, 16)
                e.dma_start(w_raw[0:D, 2, :], Wproj).then_inc(s_w, 16)
                e.dma_start(wT[D:D + 1, 3, :], bproj.rearrange("(a n) -> a n", a=1)).then_inc(s_w, 16)
                e.dma_start(prm[:, 0:24], Wpos.rearrange("h c -> (h c)").partition_broadcast(TL)).then_inc(s_w, 16)
                e.dma_start(prm[:, 24:32], bpos.partition_broadcast(TL)).then_inc(s_w, 16)
                e.dma_start(prm[:, 32:40], gating.partition_broadcast(TL)).then_inc(s_w, 16)
                with e.Fori(0, B) as n:
                    V.wait(e, n, "h1", 1)
                    e.dma_start(ht[:, :, :], H0[bass.ds(n, 1), :, :, :].rearrange("b p a d -> p (b a) d")).then_inc(hin.sem, 16)
                    V.wait(e, n, "h1")
                    e.dma_start(H1[bass.ds(n, 1), :, :, :].rearrange("b p a d -> p (b a) d"), h1[:, :, :]).then_inc(out.sem, 16)
                out.count(e, B)

            @block.tensor
            def _(e):
                e.wait_ge(s_w, 16 * 7)
                e.wait_ge(s_id, 2)
                e.transpose(bank[0][0:D, 0:128], w_raw[:, 0, :], ident[:, :]).then_inc(s_t, 1)
                for i in (1, 2):
                    e.transpose(bank[0][0:D, 64 + 64 * i:128 + 64 * i], w_raw[0:D, i, :], ident[0:D, 0:D]).then_inc(s_t, 1)
                for k in range(16):
                    e.wait_ge(s_v, 9 + 6 * k)
                    for mh in range(2):
                        e.transpose(bank[1][0:TL, 128 * mh:128 * mh + TL], pe[:, TL * mh:TL * mh + TL], ident[0:TL, 0:TL]).then_inc(s_t, 1)
                e.wait_ge(s_v, 101)
                e.nop().then_inc(T.sem, T.P)
                with e.Fori(0, B) as n:
                    V.wait(e, n, "xn")
                    settled(e, s_own)
                    for a in range(2):
                        mm = e.transpose(bank[0][0:D, TL * a:TL * a + TL], xn[:, a, :], ident[0:TL, 0:TL])
                    mm.then_inc(T.sem, 1)
                    V.wait(e, n, "xT")
                    settled(e, s_own)
                    for w in range(2):
                        mm = e.matmul(bank[1][0:D, L * w:L * w + L], wT[0:D, w, :], xT[:, :], start=True, stop=True)
                    mm.then_inc(T.sem, 1)
                    for a in range(2):
                        mm = e.matmul(bank[2][0:TL, D * a:D * a + D], xT[:, TL * a:TL * a + TL], wT[0:D, 2, :], start=True, stop=True)
                    mm.then_inc(T.sem, 1)
                    V.wait(e, n, "k")
                    for i in range(8):
                        a, hp = i // 4, i % 4
                        if i >= 2:
                            V.wait(e, n, f"mx{i - 2}")
                        e.matmul(bank[3 + i % 2][0:TL, 0:2 * L], qa[0:D, TL * a:TL * a + TL], ka[0:D, 2 * hp:2 * hp + 2, :],
                                 start=True, stop=True).then_inc(T.sem, 1)
                    V.wait(e, n, "mx7")
                    for a in range(2):
                        mm = e.matmul(bank[5][D:D + NH, TL * a:TL * a + TL], mx[:, a, :], ident[0:TL, 0:TL], start=True, stop=True)
                    mm.then_inc(T.sem, 1)
                    V.wait(e, n, "nm")
                    for h in range(NH):
                        if h >= 2:
                            A.wait(e, n, f"e{h - 2}")
                        for mh in range(2):
                            mm = e.matmul(bank[3 + h % 2][0:TL, L * mh:L * mh + L], ka[:, h, TL * mh:TL * mh + TL], qa[:, :],
                                          start=True, stop=True)
                        mm.then_inc(T.sem, 1)
                    for wts, bk in ((rt, bank[7]), (ex, bank[6])):
                        for g in range(2):
                            for mh in range(2):
                                for j in range(4):
                                    if wts is ex and mh == 0:
                                        A.wait(e, n, f"e{4 * g + j}")
                                    mm = e.matmul(bk[32 * j:32 * j + 32, L * g:L * g + L], va[:, mh, 4 * g + j, :], wts[:, 4 * g + j, mh, :],
                                                  start=(mh == 0), stop=(mh == 1))
                        mm.then_inc(T.sem, 1)
                    for src, bk, need in ((rvs, bank[1], None), (evs, bank[0], None)):
                        if src is rvs:
                            A.wait(e, n, "rvs")
                        else:
                            V.wait(e, n, "evs")
                        for g in range(2):
                            for a in range(2):
                                mm = e.transpose(bk[0:TL, 128 * (2 * g + a):128 * (2 * g + a) + 128], src[:, L * g + TL * a:L * g + TL * a + TL], ident[:, :])
                        mm.then_inc(T.sem, 1)
                    V.wait(e, n, "at1")
                    settled(e, s_own)
                    for a in range(2):
                        mm = e.transpose(bank[2][0:D, 128 + TL * a:128 + TL * a + TL], at[:, a, :], ident[0:TL, 0:TL])
                    mm.then_inc(T.sem, 1)
                    V.wait(e, n, "aT")
                    for a in range(2):
                        mm = e.matmul(bank[2][0:TL, D * a:D * a + D], aT[:, TL * a:TL * a + TL], wT[:, 3, :], start=True, stop=True)
                    mm.then_inc(T.sem, 1)

            @block.scalar
            def _(e):
                e.nop().then_inc(A.sem, A.P)
                e.wait_ge(s_w, 16 * 7)
                e.activation(prm[:, 32:40], prm[:, 32:40], ACT.Sigmoid).then_inc(s_a, 1)
                for k in range(16):
                    e.wait_ge(s_v, 7 + 6 * k)
                    e.activation(pe[:, :], pe[:, :], ACT.Exp, bias=pst[:, 1:2], accum_out=pst[:, 2:3]).then_inc(s_a, 1)
                with e.Fori(0, B) as n:
                    norm_scalar(e, V, A, n, s2, eps)
                    for h in range(NH):
                        T.wait(e, n, f"st{h}")
                        e.activation(ex[:, h, :, :], bank[3 + h % 2][0:TL, 0:2 * L].rearrange("p (m n) -> p m n", m=2), ACT.Exp).then_inc(A.sem, 1)
                    T.wait(e, n, "ev")
                    e.activation(rvs[:, :], bank[7][:, 0:2 * L], ACT.Copy).then_inc(A.sem, 1)

            @block.vector
            def _(e):
                e.nop().then_inc(V.sem, V.P)
                e.memset(eps[:, :], EPS).then_inc(s_v, 1)
                e.wait_ge(s_t, 3)
                e.wait_ge(s_w, 16 * 7)
                e.tensor_copy(wT[0:D, :, :].rearrange("p a b -> p (a b)"), bank[0][0:D, 0:256]).then_inc(s_v, 1)
                e.scalar_tensor_tensor(out=cst[:, :], in0=prm[:, 1:24:3], scalar=0.0, in1=prm[:, 24:32],
                                       op0=ALU.mult, op1=ALU.add).then_inc(s_v, 1)
                e.wait_ge(s_id, 11)
                e.tensor_tensor(dist2[:, :, :], dist[:, :, :], dist[:, :, :], ALU.mult).then_inc(s_v, 1)
                e.wait_ge(s_v, 4)
                for k in range(16):
                    h, nh = k // 2, k % 2
                    v0 = 4 + 6 * k
                    if k:
                        e.wait_ge(s_v, v0)
                    e.tensor_scalar(pe[:, :], dist2[:, nh, :], prm[:, 3 * h + 2:3 * h + 3], cst[:, h:h + 1], ALU.mult, ALU.add).then_inc(s_v, 1)
                    e.wait_ge(s_v, v0 + 1)
                    e.scalar_tensor_tensor(out=pe[:, :], in0=dist[:, nh, :], scalar=prm[:, 3 * h:3 * h + 1], in1=pe[:, :],
                                           op0=ALU.mult, op1=ALU.add).then_inc(s_v, 1)
                    e.wait_ge(s_v, v0 + 2)
                    e.tensor_reduce(pst[:, 1:2], pe[:, :], AX, ALU.max, negate=True).then_inc(s_v, 1)
                    e.wait_ge(s_a, 2 + k)
                    e.reciprocal(pst[:, 3:4], pst[:, 2:3]).then_inc(s_v, 1)
                    e.wait_ge(s_v, v0 + 4)
                    e.tensor_scalar(pe[:, :], pe[:, :], pst[:, 3:4], None, ALU.mult).then_inc(s_v, 1)
                    e.wait_ge(s_t, 3 + 2 * k + 2)
                    e.tensor_copy(rt[:, h, :, TL * nh:TL * nh + TL], bank[1][0:TL, 0:256].rearrange("p (m n) -> p m n", m=2)[:, :, 0:TL]).then_inc(s_v, 1)
                for g in range(2):
                    sg = prm[:, 32 + 4 * g:36 + 4 * g].unsqueeze(1).to_broadcast([TL, 2, 4])
                    e.tensor_copy(sgg[:, g, :, :], sg)
                    ins = e.tensor_scalar(omg[:, g, :, :], sg, -1.0, 1.0, ALU.mult, ALU.add)
                ins.then_inc(s_v, 1)
                e.wait_ge(s_v, 101)
                with e.Fori(0, B) as n:
                    hin.wait(e, n, "h")
                    norm_vector(e, V, A, n, ht[:, :, :], 2, (s1, s2, sq), xn[:, :, :])
                    T.wait(e, n, "xT")
                    e.tensor_copy(xT[:, :], bank[0][0:D, 0:L]).then_inc(V.sem, 1)
                    T.wait(e, n, "qk")
                    e.tensor_scalar(qa[0:D, :], bank[1][0:D, 0:L], float(NH) ** -0.5, None, ALU.mult).then_inc(V.sem, 1)
                    e.tensor_tensor(ka[0:D, :, :], bank[1][0:D, L:2 * L].unsqueeze(1).to_broadcast([D, NH, L]),
                                    hm[:, :].unsqueeze(2).to_broadcast([D, NH, L]), ALU.mult).then_inc(V.sem, 1)
                    T.wait(e, n, "v")
                    e.tensor_copy(va[:, :, :, 0:8], bank[2][0:TL, 0:128].rearrange("p (a h d) -> p a h d", a=2, h=NH)).then_inc(V.sem, 1)
                    for i in range(8):
                        T.wait(e, n, f"s{i}")
                        e.tensor_reduce(mx[:, i // 4, 2 * (i % 4):2 * (i % 4) + 2],
                                        bank[3 + i % 2][0:TL, 0:2 * L].rearrange("p (h m) -> p h m", h=2), AX, ALU.max).then_inc(V.sem, 1)
                    T.wait(e, n, "nm")
                    e.tensor_scalar(qa[D:D + NH, :], bank[5][D:D + NH, 0:L], -1.0, None, ALU.mult).then_inc(V.sem, 1)
                    T.wait(e, n, "rv")
                    e.tensor_copy(evs[:, :], bank[6][:, 0:2 * L]).then_inc(V.sem, 1)
                    T.wait(e, n, "tr")
                    ev = bank[0][0:TL, :].rearrange("p (q c) -> p q c", c=32)
                    rvt = bank[1][0:TL, :].rearrange("p (q c) -> p q c", c=32)
                    flat = lambda t: t[:, :, :, :].rearrange("p g a j -> p (g a j)")
                    e.reciprocal(rz[:, :].unsqueeze(2), ev[:, :, 8:9]).then_inc(V.sem, 1)
                    V.wait(e, n, "rz")
                    e.tensor_tensor(rz[:, :], rz[:, :], flat(omg), ALU.mult).then_inc(V.sem, 1)
                    V.wait(e, n, "rzg")
                    e.tensor_tensor(num[:, :, :], ev[:, :, 0:9], rz[:, :].unsqueeze(2).to_broadcast([TL, 16, 9]), ALU.mult).then_inc(V.sem, 1)
                    e.tensor_tensor(rv[:, :, :], rvt[:, :, 0:9], flat(sgg).unsqueeze(2).to_broadcast([TL, 16, 9]), ALU.mult).then_inc(V.sem, 1)
                    V.wait(e, n, "rv")
                    e.tensor_tensor(num[:, :, :], num[:, :, :], rv[:, :, :], ALU.add).then_inc(V.sem, 1)
                    V.wait(e, n, "sum")
                    e.reciprocal(rz[:, :].unsqueeze(2), num[:, :, 8:9]).then_inc(V.sem, 1)
                    V.wait(e, n, "rd")
                    for a in range(2):
                        v = lambda t: t.rearrange("p (g a j) c -> p a g j c", g=2, a=2)[:, a]
                        e.tensor_tensor(at[:, a, :].rearrange("p (g j c) -> p g j c", g=2, j=4), v(num[:, :, 0:8]),
                                        v(rz[:, :].unsqueeze(2).to_broadcast([TL, 16, 8])), ALU.mult).then_inc(V.sem, 1)
                    T.wait(e, n, "aT")
                    e.tensor_copy(aT[0:D, :], bank[2][0:D, 128:128 + L]).then_inc(V.sem, 1)
                    T.wait(e, n, "pr")
                    out.count(e, n)
                    e.tensor_tensor(h1[:, :, :], bank[2][0:TL, 0:128].rearrange("p (a d) -> p a d", a=2), ht[:, :, :], ALU.add).then_inc(V.sem, 1)


def ffn_layer(nc, wr, br, w1, b1, w2, b2, H1, H2, XN, WD, SW):
    G = B // 4
    with ExitStack() as ctx:
        S = Space(nc, ctx, "ffn")
        ident = S.sb("ident", [128, 128])
        eps = S.sb("eps", [128, 1])
        wrb, brb = S.sb("wrb", [TL, D]), S.sb("brb", [TL, 1])
        w1s, w2s, b1s, b2s = S.sb("w1s", [D, HID]), S.sb("w2s", [128, 2, D]), S.sb("b1s", [128, 2]), S.sb("b2s", [128, 1])
        ht, xn, sq = S.sb("ht", [TL, 8, D]), S.sb("xn", [TL, 8, D]), S.sb("sq", [TL, 8, D])
        s1, s2 = S.sb("s1", [TL, 8]), S.sb("s2", [TL, 8])
        wt = S.sb("wt", [TL, 128])
        wtt = S.sb("wtt", [128, TL])
        wv, wk, m8, ge, eq, pre = S.sb("wv", [B, L]), S.sb("wk", [B, L]), S.sb("m8", [B, 8]), S.sb("ge", [B, L]), S.sb("eq", [B, L]), S.sb("pre", [B, L])
        cnt = S.sb("cnt", [B, 2])
        swp, sw = S.sb("swp", [128, TL]), S.sb("sw", [TL, 128])
        xT = S.sb("xT", [D, 4 * L])
        u, t2, gg = S.sb("u", [128, 4, 2 * L]), S.sb("t2", [128, 4, 2 * L]), S.sb("gg", [128, 4, 2 * L])
        yT, h2 = S.sb("yT", [128, 2 * L]), S.sb("h2", [TL, 8, D])
        bank = S.banks()
        s_id, s_w, s_own = S.sem("ident"), S.sem("weights"), S.sem("settled")
        bc = lambda a, k: a.unsqueeze(2).to_broadcast([TL, k, D])

        with nc.Block() as block:
            V = Loop(S.sem("vector"), NORM_V + ["xr", "w"])
            A = Loop(S.sem("scalar"), ["std"])
            hin, out = Loop(S.sem("h_in"), ["h"], 16, 0), Loop(S.sem("out"), ["x"], 16, 0)
            s_v = S.sem("set")

            @block.gpsimd
            def _(e):
                make_identity(e, ident, s_id)

            @block.sync
            def _(e):
                e.dma_start(wrb[:, :], wr.rearrange("d a -> (d a)").partition_broadcast(TL)).then_inc(s_w, 16)
                e.dma_start(brb[:, :], br.partition_broadcast(TL)).then_inc(s_w, 16)
                e.dma_start(w1s[:, :], w1).then_inc(s_w, 16)
                e.dma_start(w2s[:, :, :], w2.rearrange("(a p) d -> p a d", a=2)).then_inc(s_w, 16)
                with nc.allow_non_contiguous_dma("biases, one an element"):
                    e.dma_start(b1s[:, :], b1.rearrange("(a p) -> p a", a=2)).then_inc(s_w, 16)
                for g in range(2):
                    e.dma_start(b2s[D * g:D * g + D, :], b2.rearrange("(d a) -> d a", a=1)).then_inc(s_w, 16)
                with e.Fori(0, G) as n:
                    V.wait(e, n, "cen", 1)
                    e.dma_start(ht[:, :, :].rearrange("p (b a) d -> p b (a d)", a=2), H1[bass.ds(4 * n, 4), :, :, :].rearrange("b p a d -> p b (a d)")).then_inc(hin.sem, 16)
                    V.wait(e, n, "xn")
                    e.dma_start(XN[bass.ds(4 * n, 4), :, :, :].rearrange("b p a d -> p b (a d)"), xn[:, :, :].rearrange("p (b a) d -> p b (a d)", a=2)).then_inc(out.sem, 16)
                out.count(e, G)

            @block.scalar
            def _(e):
                e.nop().then_inc(A.sem, A.P)
                e.preload_act_table(ACT.Sqrt)
                with e.Fori(0, G) as n:
                    norm_scalar(e, V, A, n, s2, eps)

            @block.vector
            def _(e):
                e.memset(eps[:, :], EPS).then_inc(s_v, 1)
                e.wait_ge(s_v, 1)
                e.nop().then_inc(V.sem, V.P)
                e.wait_ge(s_w, 16 * 7)
                with e.Fori(0, G) as n:
                    hin.wait(e, n, "h")
                    out.count(e, n)
                    V.wait(e, n, "w", 1)
                    norm_vector(e, V, A, n, ht[:, :, :], 8, (s1, s2, sq), xn[:, :, :])
                    V.wait(e, n, "xn")
                    e.tensor_tensor(sq[:, :, :], xn[:, :, :], wrb[:, :].unsqueeze(1).to_broadcast([TL, 8, D]), ALU.mult).then_inc(V.sem, 1)
                    V.wait(e, n, "xr")
                    e.tensor_reduce(wt[:, bass.ds(8 * n, 8)], sq[:, :, :], AX, ALU.add).then_inc(V.sem, 1)

        with nc.Block() as block:
            s_c, s_d, s_t = S.sem("choice"), S.sem("choice_dma"), S.sem("choice_turned")

            @block.tensor
            def _(e):
                e.wait_ge(s_c, 1)
                e.transpose(bank[0][:, 0:TL], wt[:, :], ident[0:TL, 0:TL]).then_inc(s_t, 1)
                e.wait_ge(s_d, 64)
                e.transpose(bank[1][0:TL, 0:128], swp[:, :], ident[:, :]).then_inc(s_t, 1)

            @block.sync
            def _(e):
                e.wait_ge(s_c, 2)
                e.dma_start(WD.rearrange("b (a t) -> (b a) t", a=2), wtt[:, :]).then_inc(s_d, 16)
                e.wait_ge(s_d, 16)
                e.dma_start(wv[:, :], WD).then_inc(s_d, 16)
                e.wait_ge(s_c, 3 + 2 * 15 + 9)
                e.dma_start(SW, pre[:, :]).then_inc(s_d, 16)
                e.wait_ge(s_d, 48)
                e.dma_start(swp[:, :], SW.rearrange("b (a t) -> (b a) t", a=2)).then_inc(s_d, 16)

            @block.vector
            def _(e):
                at = [0]

                def done(ins):
                    ins.then_inc(s_c, 1)
                    at[0] += 1
                    e.wait_ge(s_c, at[0])

                done(e.tensor_scalar(wt[:, :], wt[:, :], brb[:, 0:1], None, ALU.add))
                e.wait_ge(s_t, 1)
                done(e.tensor_copy(wtt[:, :], bank[0][:, 0:TL]))
                e.wait_ge(s_d, 32)
                done(e.tensor_copy(wk[:, :], wv[:, :]))
                rounds, last = divmod(TOPK - 1, 8)
                assert rounds == 15
                for _ in range(rounds):
                    done(e.max(m8[:, :], wk[:, :]))
                    done(e.match_replace(wk[:, :], m8[:, :], wk[:, :], -3.0e38))
                done(e.max(m8[:, :], wk[:, :]))
                thr = m8[:, last:last + 1]
                done(e.tensor_scalar(ge[:, :], wv[:, :], thr, None, ALU.is_gt))
                done(e.tensor_reduce(cnt[:, 0:1], ge[:, :], AX, ALU.add))
                done(e.tensor_scalar(cnt[:, 1:2], cnt[:, 0:1], -1.0, float(TOPK), ALU.mult, ALU.add))
                done(e.tensor_scalar(eq[:, :], wv[:, :], thr, None, ALU.is_equal))
                done(e.tensor_tensor_scan(pre[:, :], eq[:, :], eq[:, :], 0.0, ALU.add, ALU.bypass))
                done(e.scalar_tensor_tensor(out=eq[:, :], in0=pre[:, :], scalar=cnt[:, 1:2], in1=eq[:, :], op0=ALU.is_le, op1=ALU.mult))
                done(e.tensor_tensor(ge[:, :], ge[:, :], eq[:, :], ALU.add))
                done(e.tensor_tensor(pre[:, :], ge[:, :], wv[:, :], ALU.mult))
                e.wait_ge(s_t, 2)
                done(e.tensor_copy(sw[:, :], bank[1][0:TL, 0:128]))

        with nc.Block() as block:
            V = Loop(S.sem("vector2"), ["xT0"] + [f"{a}{i}" for i in range(4) for a in ("uu", "uv", "uw", "gg")] + ["yw", "hx", "h2"])
            A = Loop(S.sem("scalar2"), ["xT1"] + [f"{a}{i}" for i in range(4) for a in ("u", "th")] + ["yT"])
            T = Loop(S.sem("tensor2"), ["xT"] + [f"h{i}" for i in range(4)] + ["y", "turn"])
            hin, xin = Loop(S.sem("h_in2"), ["h"], 16, 0), Loop(S.sem("x_in2"), ["x"], 16, 0)
            out = Loop(S.sem("out2"), ["h"], 16, 0)
            s_v = S.sem("set2")
            grp = lambda t: t.rearrange("p (b a) d -> p b (a d)", a=2)
            dr = lambda t, n: t[bass.ds(4 * n, 4), :, :, :].rearrange("b p a d -> p b (a d)")

            @block.sync
            def _(e):
                with e.Fori(0, G) as n:
                    V.wait(e, n, "h2", 1)
                    e.dma_start(grp(xn[:, :, :]), dr(XN, n)).then_inc(xin.sem, 16)
                    e.dma_start(grp(ht[:, :, :]), dr(H1, n)).then_inc(hin.sem, 16)
                    V.wait(e, n, "h2")
                    e.dma_start(dr(H2, n), grp(h2[:, :, :])).then_inc(out.sem, 16)
                out.count(e, G)

            @block.tensor
            def _(e):
                e.nop().then_inc(T.sem, T.P)
                e.wait_ge(s_v, 1)
                with e.Fori(0, G) as n:
                    xin.wait(e, n, "x")
                    settled(e, s_own)
                    for k in range(8):
                        mm = e.transpose(bank[k // 4][0:D, TL * (k % 4):TL * (k % 4) + TL], xn[:, k, :], ident[0:TL, 0:TL])
                    mm.then_inc(T.sem, 1)
                    V.wait(e, n, "xT0")
                    A.wait(e, n, "xT1")
                    for i in range(4):
                        q, a = i // 2, i % 2
                        e.matmul(bank[2 + i][:, 0:2 * L], w1s[:, 128 * a:128 * a + 128], xT[:, 2 * L * q:2 * L * q + 2 * L],
                                 start=True, stop=True).then_inc(T.sem, 1)
                    V.wait(e, n, "gg3")
                    for a in range(2):
                        for q in range(2):
                            mm = e.matmul(bank[6][D * q:D * q + D, 0:2 * L], w2s[:, a, :], gg[:, 2 * q + a, :], start=(a == 0), stop=(a == 1))
                    mm.then_inc(T.sem, 1)
                    A.wait(e, n, "yT")
                    for k in range(4):
                        mm = e.transpose(bank[7][0:TL, 128 * k:128 * k + 128], yT[:, TL * k:TL * k + TL], ident[:, :])
                    mm.then_inc(T.sem, 1)

            @block.scalar
            def _(e):
                e.nop().then_inc(A.sem, A.P)
                e.preload_act_table(ACT.Tanh)
                with e.Fori(0, G) as n:
                    T.wait(e, n, "xT")
                    e.activation(xT[:, 2 * L:], bank[1][0:D, 0:2 * L], ACT.Copy).then_inc(A.sem, 1)
                    for i in range(4):
                        T.wait(e, n, f"h{i}")
                        e.activation(u[:, i, :], bank[2 + i][:, 0:2 * L], ACT.Identity, bias=b1s[:, i % 2:i % 2 + 1]).then_inc(A.sem, 1)
                        V.wait(e, n, f"uw{i}")
                        e.activation(t2[:, i, :], t2[:, i, :], ACT.Tanh, scale=0.7978845608028654).then_inc(A.sem, 1)
                    T.wait(e, n, "y")
                    e.activation(yT[:, :], bank[6][:, 0:2 * L], ACT.Identity, bias=b2s[:, 0:1]).then_inc(A.sem, 1)

            @block.vector
            def _(e):
                e.nop().then_inc(V.sem, V.P)
                e.tensor_scalar(w2s[:, :, :], w2s[:, :, :], 0.5, None, ALU.mult).then_inc(s_v, 1)
                with e.Fori(0, G) as n:
                    T.wait(e, n, "xT")
                    e.tensor_copy(xT[:, 0:2 * L], bank[0][0:D, 0:2 * L]).then_inc(V.sem, 1)
                    for i in range(4):
                        A.wait(e, n, f"u{i}")
                        e.tensor_tensor(t2[:, i, :], u[:, i, :], u[:, i, :], ALU.mult).then_inc(V.sem, 1)
                        V.wait(e, n, f"uu{i}")
                        e.tensor_scalar(t2[:, i, :], t2[:, i, :], 0.044715, 1.0, ALU.mult, ALU.add).then_inc(V.sem, 1)
                        V.wait(e, n, f"uv{i}")
                        e.tensor_tensor(t2[:, i, :], t2[:, i, :], u[:, i, :], ALU.mult).then_inc(V.sem, 1)
                        A.wait(e, n, f"th{i}")
                        e.scalar_tensor_tensor(out=gg[:, i, :], in0=t2[:, i, :], scalar=1.0, in1=u[:, i, :], op0=ALU.add, op1=ALU.mult).then_inc(V.sem, 1)
                    T.wait(e, n, "turn")
                    out.count(e, n)
                    e.tensor_tensor(h2[:, :, :].rearrange("p (q k) d -> p q k d", q=2),
                                    bank[7][0:TL, :].rearrange("p (k q d) -> p q k d", k=4, q=2),
                                    sw[:, bass.ds(8 * n, 8)].rearrange("p (q k) -> p q k", q=2).unsqueeze(3).to_broadcast([TL, 2, 4, D]), ALU.mult).then_inc(V.sem, 1)
                    hin.wait(e, n, "h")
                    e.tensor_tensor(xn[:, :, :], xn[:, :, :], ht[:, :, :], ALU.add).then_inc(V.sem, 1)
                    V.wait(e, n, "hx")
                    e.tensor_tensor(h2[:, :, :], h2[:, :, :], xn[:, :, :], ALU.add).then_inc(V.sem, 1)


def key_layer(nc, W_fused, H2, ZR, VR, GR):
    NF = 3 * D + 3
    with ExitStack() as ctx:
        S = Space(nc, ctx, "key")
        ident, eps = S.sb("ident", [128, 128]), S.sb("eps", [128, 1])
        wr, wT = S.sb("wr", [128, 2, D]), S.sb("wT", [D, NF])
        zero = S.sb("zero", [128, 64 * D])
        ht, xn, sq = S.sb("ht", [TL, 8, D]), S.sb("xn", [TL, 8, D]), S.sb("sq", [TL, 8, D])
        s1, s2 = S.sb("s1", [TL, 8]), S.sb("s2", [TL, 8])
        xT = S.sb("xT", [D, 4 * L])
        sg, kqv = S.sb("sg", [TL, 8, NF]), S.sb("kqv", [TL, 3, 8, D])
        k2, ss, gt = S.sb("k2", [TL, 16, D]), S.sb("ss", [TL, 16]), S.sb("gt", [TL, 8, 4])
        bank = S.banks()
        s_own, s_own_sp = S.sem("settled"), S.sem("settled_sp")
        s_id, s_w, s_z, s_v, s_t = S.sem("ident"), S.sem("weights"), S.sem("zeros"), S.sem("set_v"), S.sem("set_t")
        V = Loop(S.sem("vector"), NORM_V + ["xT0"] + [f"si{i}" for i in range(4)] + ["k2", "ss", "mx", "rn", "kn", "g0", "g1", "g2", "g3"])
        A = Loop(S.sem("scalar"), ["std", "xT1"] + [f"sg{i}" for i in range(4)] + ["nrm"])
        T = Loop(S.sem("tensor"), ["xT"] + [f"f{i}" for i in range(4)])
        hin = Loop(S.sem("h_in"), ["h"], 16, 0)
        out = Loop(S.sem("out"), ["z"], 16 * 8, 0)
        with nc.Block() as block:
            @block.gpsimd
            def _(e):
                make_identity(e, ident, s_id)

            @block.sync
            def _(e):
                e.dma_start(wr[:, 0, :], W_fused[0:128, :]).then_inc(s_w, 16)
                e.dma_start(wr[0:NF - 128, 1, :], W_fused[128:NF, :]).then_inc(s_w, 16)
                e.wait_ge(s_v, 1)
                z3 = lambda k: zero[:, 0:k * D].rearrange("p (t d) -> p t d", d=D)
                nz = 0
                for t0 in range(0, VR.shape[0], 64):
                    k = min(64, VR.shape[0] - t0)
                    e.dma_start(VR[t0:t0 + k, :, :].rearrange("t p d -> p t d"), z3(k)).then_inc(s_z, 16)
                    nz += 1
                e.dma_start(ZR[0:CH + 1, :, :].rearrange("t p d -> p t d"), z3(CH + 1)).then_inc(s_z, 16)
                k = ZR.shape[0] - CH - L
                e.dma_start(ZR[CH + L:, :, :].rearrange("t p d -> p t d"), z3(k)).then_inc(s_z, 16)
                e.dma_start(GR[:, L:, :], zero[0:B, 0:4 * (CH * NCH - L)].rearrange("p (t g) -> p t g", g=4)).then_inc(s_z, 16)
                e.wait_ge(s_z, 16 * (nz + 3))
                with e.Fori(0, 4) as j:
                    with e.Fori(0, 4) as q:
                        n = 4 * j + q
                        V.wait(e, n, "xn", 1)
                        settled(e, s_own_sp)
                        e.dma_start(ht[:, :, :].rearrange("p (b a) d -> p b (a d)", a=2),
                                    H2[bass.ds(4 * n, 4), :, :, :].rearrange("b p a d -> p b (a d)")).then_inc(hin.sem, 16)
                        V.wait(e, n, "g3")
                        settled(e, s_own_sp)
                        for a in range(2):
                            t0 = TL * a
                            for w, (dst, row) in enumerate(((ZR[CH + 1 + t0:CH + 1 + t0 + TL], 16), (ZR[CH + t0:CH + t0 + TL], 0), (VR[t0:t0 + TL], 0))):
                                e.dma_start(dst[:, bass.ds(32 * j + 4 * q + row, 4), :], kqv[:, w, a:8:2, :]).then_inc(out.sem, 16)
                            e.dma_start(GR[bass.ds(4 * n, 4), t0:t0 + TL, :].rearrange("b t g -> t b g"), gt[:, a:8:2, :]).then_inc(out.sem, 16)
                out.count(e, B // 4)

            @block.tensor
            def _(e):
                e.wait_ge(s_w, 32)
                e.wait_ge(s_id, 2)
                e.transpose(bank[0][0:D, 0:128], wr[:, 0, :], ident[:, :]).then_inc(s_t, 1)
                e.transpose(bank[0][0:D, 128:NF], wr[0:NF - 128, 1, :], ident[0:NF - 128, 0:NF - 128]).then_inc(s_t, 1)
                e.nop().then_inc(T.sem, T.P)
                e.wait_ge(s_v, 3)
                with e.Fori(0, B // 4) as n:
                    V.wait(e, n, "xn")
                    settled(e, s_own)
                    for k in range(8):
                        mm = e.transpose(bank[k // 4][0:D, TL * (k % 4):TL * (k % 4) + TL], xn[:, k, :], ident[0:TL, 0:TL])
                    mm.then_inc(T.sem, 1)
                    V.wait(e, n, "xT0")
                    A.wait(e, n, "xT1")
                    for i in range(4):
                        for a in range(2):
                            k = 2 * i + a
                            mm = e.matmul(bank[2 + i][0:TL, NF * a:NF * a + NF], xT[:, TL * k:TL * k + TL], wT[:, :], start=True, stop=True)
                        mm.then_inc(T.sem, 1)

            @block.scalar
            def _(e):
                e.nop().then_inc(A.sem, A.P)
                with e.Fori(0, B // 4) as n:
                    norm_scalar(e, V, A, n, s2, eps)
                    T.wait(e, n, "xT")
                    e.activation(xT[:, 2 * L:], bank[1][0:D, 0:2 * L], ACT.Copy).then_inc(A.sem, 1)
                    for i in range(4):
                        T.wait(e, n, f"f{i}")
                        V.wait(e, n, "g3", 1)
                        e.activation(sg[:, 2 * i:2 * i + 2, :], bank[2 + i][0:TL, 0:2 * NF].rearrange("p (a f) -> p a f", a=2), ACT.Sigmoid).then_inc(A.sem, 1)
                    V.wait(e, n, "ss")
                    e.activation(ss[:, :], ss[:, :], ACT.Sqrt).then_inc(A.sem, 1)

            @block.vector
            def _(e):
                e.memset(zero[:, :], 0.0).then_inc(s_v, 1)
                e.memset(eps[:, :], EPS).then_inc(s_v, 1)
                e.wait_ge(s_t, 2)
                e.tensor_copy(wT[:, :], bank[0][0:D, 0:NF]).then_inc(s_v, 1)
                e.wait_ge(s_v, 3)
                e.nop().then_inc(V.sem, V.P)
                with e.Fori(0, B // 4) as n:
                    hin.wait(e, n, "h")
                    V.wait(e, n, "g3", 1)
                    T.wait(e, n, "xT", 1)
                    norm_vector(e, V, A, n, ht[:, :, :], 8, (s1, s2, sq), xn[:, :, :])
                    T.wait(e, n, "xT")
                    e.tensor_copy(xT[:, 0:2 * L], bank[0][0:D, 0:2 * L]).then_inc(V.sem, 1)
                    out.count(e, n)
                    for i in range(4):
                        A.wait(e, n, f"sg{i}")
                        e.tensor_tensor(kqv[:, :, 2 * i:2 * i + 2, :].rearrange("p w a d -> p a w d"),
                                        bank[2 + i][0:TL, 0:2 * NF].rearrange("p (a f) -> p a f", a=2)[:, :, 0:3 * D].rearrange("p a (w d) -> p a w d", w=3),
                                        sg[:, 2 * i:2 * i + 2, 0:3 * D].rearrange("p a (w d) -> p a w d", w=3), ALU.mult).then_inc(V.sem, 1)
                    V.wait(e, n, "si3")
                    qk = kqv[:, 0:2, :, :].rearrange("p w k d -> p (w k) d")
                    e.tensor_tensor(k2[:, :, :], qk, qk, ALU.mult).then_inc(V.sem, 1)
                    V.wait(e, n, "k2")
                    e.tensor_reduce(ss[:, :], k2[:, :, :], AX, ALU.add).then_inc(V.sem, 1)
                    A.wait(e, n, "nrm")
                    e.tensor_scalar(ss[:, :], ss[:, :], 1e-12, None, ALU.max).then_inc(V.sem, 1)
                    V.wait(e, n, "mx")
                    e.reciprocal(ss[:, :], ss[:, :]).then_inc(V.sem, 1)
                    V.wait(e, n, "rn")
                    e.tensor_tensor(qk, qk, ss[:, :].unsqueeze(2).to_broadcast([TL, 16, D]), ALU.mult).then_inc(V.sem, 1)
                    e.tensor_copy(gt[:, :, 0:1], sg[:, :, NF - 1:NF]).then_inc(V.sem, 1)
                    e.tensor_scalar(gt[:, :, 1:2], sg[:, :, NF - 3:NF - 2], -1.0, 1.0, ALU.mult, ALU.add).then_inc(V.sem, 1)
                    e.tensor_scalar(gt[:, :, 2:3], sg[:, :, NF - 2:NF - 1], -0.1 * 4.0 / D, None, ALU.mult).then_inc(V.sem, 1)
                    V.wait(e, n, "g2")
                    e.tensor_copy(gt[:, :, 3:4], gt[:, :, 0:1]).then_inc(V.sem, 1)


def expert_layer(nc, Wg, bg, W1, b1, W2, b2, H2, YR, out_dram):
    G = B // 4
    E = NH
    with ExitStack() as ctx:
        S = Space(nc, ctx, "moe")
        ident, eps = S.sb("ident", [128, 128]), S.sb("eps", [128, 1])
        wraw = S.sb("wraw", [128, 2, HID])
        W_PARTS = [S.sb(f"w_{q}", [128, E, HID], BF16) for q in ("11", "22", "31")]
        wrest = S.sb("wrest", [D, HID])
        w2T = S.sb("w2T", [128, E, 2, D])
        x21, x13, xrest = S.sb("x21", [128, 4 * L], BF16), S.sb("x13", [128, 4 * L], BF16), S.sb("xrest", [D, 4 * L])
        c123, cpart, crest = S.sb("c123", [72, 4 * L], BF16), S.sb("cpart", [E, 4 * L], BF16), S.sb("crest", [E, 4 * L])
        wgr, wgT, bgb = S.sb("wgr", [E, D]), S.sb("wgT", [D, E]), S.sb("bgb", [TL, E])
        b1s, b2s = S.sb("b1s", [128, E, 2]), S.sb("b2s", [E, D])
        sel = S.sb("sel", [72, E, 128], BF16)
        tri = S.sb("tri", [128, E, E])
        ht, yt, xn, sq = S.sb("ht", [TL, 8, D]), S.sb("yt", [TL, 8, D]), S.sb("xn", [TL, 8, D]), S.sb("sq", [TL, 8, D])
        s1, s2 = S.sb("s1", [TL, 8]), S.sb("s2", [TL, 8])
        xT = S.sb("xT", [D, 4 * L])
        gs, rk, ex, mz = S.sb("gs", [TL, 8, E]), S.sb("rk", [TL, 8, E]), S.sb("ex", [TL, 8, E]), S.sb("mz", [TL, 2, 8])
        c1, c2 = S.sb("c1", [TL, 8, E, E]), S.sb("c2", [TL, 8, E, E])
        cT = S.sb("cT", [E, 4 * L])
        hb, hw = S.sb("hb", [128, 2, 2, 2 * L]), S.sb("hw", [128, 2, 2, 2 * L])
        yT, o = S.sb("yT", [128, 2 * L]), S.sb("o", [TL, 8, D])
        bank = S.banks()
        s_own, s_own_sp = S.sem("settled"), S.sem("settled_sp")
        s_id, s_w, s_v, s_t = S.sem("ident"), S.sem("weights"), S.sem("set_v"), S.sem("set_t")
        NW = 8
        EH = [(x_, a) for x_ in range(E) for a in range(2)]
        V = Loop(S.sem("vector"), ["h3"] + NORM_V + ["xT0", "x1", "xr", "x3", "gs", "gt", "eq", "eqt", "cmp", "rk", "m1", "gm", "sel", "z", "rz", "cmb", "cT", "cr", "cp", "c3"] +
                 [f"w{x_}{a}{q}" for x_, a in EH for q in range(2)] + ["o"])
        A = Loop(S.sem("scalar"), ["std", "xT1", "x1", "x2", "exp", "cT1", "c1", "c2"] + [f"h{x_}{a}{q}" for x_, a in EH for q in range(2)] + ["yT"])
        order = []
        for i, (x_, a) in enumerate(EH):
            order += ([f"b{x_}0", f"b{x_}1"] if a == 0 else []) + [f"h{x_}{a}0", f"h{x_}{a}1"] + ([f"y{i - 1}"] if i else [])
        T = Loop(S.sem("tensor"), ["xT", "g", "cT"] + order + ["y15", "yb", "turn"])
        hin = Loop(S.sem("h_in"), ["h"], 48, 0)
        out = Loop(S.sem("out"), ["h"], 32, 0)
        with nc.Block() as block:
            @block.gpsimd
            def _(e):
                make_identity(e, ident, s_id)
                e.wait_ge(s_id, 2)
                e.memset(tri[:, :, :], 1.0).then_inc(s_id, 1)
                e.wait_ge(s_id, 3)
                e.affine_select(out=tri[:, :, :], in_=tri[:, :, :], compare_op=ALU.is_gt, fill=0.0, base=0,
                                pattern=[[1, E], [-1, E]], channel_multiplier=0).then_inc(s_id, 1)

            @block.sync
            def _(e):
                e.dma_start(wgr[:, :], Wg).then_inc(s_w, 16)
                e.dma_start(bgb[:, :], bg.partition_broadcast(TL)).then_inc(s_w, 16)
                with nc.allow_non_contiguous_dma("biases, one an element"):
                    for a in range(2):
                        e.dma_start(b1s[:, :, a], b1[:, 128 * a:128 * a + 128].rearrange("e p -> p e")).then_inc(s_w, 16)
                e.dma_start(b2s[:, :], b2).then_inc(s_w, 16)
                for x_ in range(E):
                    if x_:
                        e.wait_ge(s_t, 1 + 4 * x_)
                    e.dma_start(wraw[:, 0, 0:2 * D].rearrange("p (a d) -> p a d", a=2), W1[x_].rearrange("(a p) d -> p a d", a=2)).then_inc(s_w, 16)
                    e.dma_start(wraw[0:D, 1, :], W2[x_]).then_inc(s_w, 16)
                with e.Fori(0, 4) as j:
                    with e.Fori(0, 4) as q:
                        n = 4 * j + q
                        V.wait(e, n, "o", 1)
                        e.dma_start(ht[:, :, :].rearrange("p (b a) d -> p b (a d)", a=2),
                                    H2[bass.ds(4 * n, 4), :, :, :].rearrange("b p a d -> p b (a d)")).then_inc(hin.sem, 16)
                        for a in range(2):
                            e.dma_start(yt[:, a:8:2, :], YR[1 + TL * a:1 + TL * a + TL, bass.ds(32 * j + 4 * q + 16, 4), :]).then_inc(hin.sem, 16)
                        V.wait(e, n, "o")
                        settled(e, s_own_sp)
                        for a in range(2):
                            e.dma_start(out_dram[bass.ds(4 * n, 4), TL * a:TL * a + TL, :].rearrange("b t d -> t b d"), o[:, a:8:2, :]).then_inc(out.sem, 16)
                out.count(e, G)

            @block.tensor
            def _(e):
                e.wait_ge(s_id, 2)
                e.wait_ge(s_w, 16 * 7)
                e.transpose(bank[0][0:D, 0:E], wgr[:, :], ident[0:E, 0:E]).then_inc(s_t, 1)
                for x_ in range(E):
                    e.wait_ge(s_w, 16 * (7 + 2 * x_))
                    if x_:
                        e.wait_ge(s_v, 2 + NW * x_)
                    for a in range(2):
                        e.transpose(bank[1][0:D, 128 * a:128 * a + 128], wraw[:, 0, D * a:D * a + D], ident[:, :]).then_inc(s_t, 1)
                    for a in range(2):
                        e.transpose(bank[2][:, D * a:D * a + D], wraw[0:D, 1, 128 * a:128 * a + 128], ident[0:D, 0:D]).then_inc(s_t, 1)
                e.wait_ge(s_v, 2 + NW * E + 5)
                e.wait_ge(s_id, 4)
                e.nop().then_inc(T.sem, T.P)
                with e.Fori(0, G) as n:
                    V.wait(e, n, "xn")
                    settled(e, s_own)
                    for k in range(8):
                        mm = e.transpose(bank[k // 4][0:D, TL * (k % 4):TL * (k % 4) + TL], xn[:, k, :], ident[0:TL, 0:TL])
                    mm.then_inc(T.sem, 1)
                    V.wait(e, n, "xT0")
                    A.wait(e, n, "xT1")
                    for k in range(8):
                        mm = e.matmul(bank[2][0:TL, E * k:E * k + E], xT[:, TL * k:TL * k + TL], wgT[:, :], start=True, stop=True)
                    mm.then_inc(T.sem, 1)
                    V.wait(e, n, "cmb")
                    settled(e, s_own)
                    for k in range(8):
                        mm = e.transpose(bank[k // 4][0:E, TL * (k % 4):TL * (k % 4) + TL], ex[:, k, :], ident[0:TL, 0:TL])
                    mm.then_inc(T.sem, 1)
                    V.wait(e, n, "c3")
                    A.wait(e, n, "c2")

                    def first(i):
                        x_, a = EH[i]
                        if a == 0:
                            if x_:
                                V.wait(e, n, f"w{x_ - 1}11")
                            for q in range(2):
                                e.matmul(bank[q][:, 0:2 * L], sel[:, x_, :], c123[:, 2 * L * q:2 * L * q + 2 * L], start=True, stop=True).then_inc(T.sem, 1)
                        if i >= 2:
                            A.wait(e, n, "h%d%d1" % EH[i - 2])
                        for q in range(2):
                            for k, (w, xp) in enumerate(zip(W_PARTS, (x21, x21, x13))):
                                mm = e.matmul(bank[2 + 2 * a + q][:, 0:2 * L], w[:, x_, 128 * a:128 * a + 128], xp[:, 2 * L * q:2 * L * q + 2 * L],
                                              start=(k == 0), stop=(k == 2))
                            mm.then_inc(T.sem, 1)

                    def second(i):
                        x_, a = EH[i]
                        V.wait(e, n, f"w{x_}{a}1")
                        for q in range(2):
                            mm = e.matmul(bank[6][D * q:D * q + D, 0:2 * L], w2T[:, x_, a, :], hw[:, a, q, :], start=(i == 0), stop=False)
                        return mm

                    for i in range(2 * E):
                        first(i)
                        if i:
                            second(i - 1).then_inc(T.sem, 1)
                    second(2 * E - 1).then_inc(T.sem, 1)
                    for q in range(2):
                        mm = e.matmul(bank[6][D * q:D * q + D, 0:2 * L], b2s[:, :], cT[:, 2 * L * q:2 * L * q + 2 * L], start=False, stop=True)
                    mm.then_inc(T.sem, 1)
                    A.wait(e, n, "yT")
                    for k in range(4):
                        mm = e.transpose(bank[7][0:TL, 128 * k:128 * k + 128], yT[:, TL * k:TL * k + TL], ident[:, :])
                    mm.then_inc(T.sem, 1)

            @block.scalar
            def _(e):
                e.nop().then_inc(A.sem, A.P)
                with e.Fori(0, G) as n:
                    norm_scalar(e, V, A, n, s2, eps)
                    T.wait(e, n, "xT")
                    e.activation(xT[:, 2 * L:], bank[1][0:D, 0:2 * L], ACT.Copy).then_inc(A.sem, 1)
                    V.wait(e, n, "xT0")
                    A.wait(e, n, "xT1")
                    e.activation(x21[D:, :], xT[:, :], ACT.Copy).then_inc(A.sem, 1)
                    V.wait(e, n, "xr")
                    e.activation(x21[0:D, :], xrest[:, :], ACT.Copy).then_inc(A.sem, 1)
                    V.wait(e, n, "gm")
                    e.activation(ex[:, :, :], gs[:, :, :], ACT.Exp).then_inc(A.sem, 1)
                    T.wait(e, n, "cT")
                    e.activation(cT[:, 2 * L:], bank[1][0:E, 0:2 * L], ACT.Copy).then_inc(A.sem, 1)
                    V.wait(e, n, "cT")
                    A.wait(e, n, "cT1")
                    e.activation(c123[0:E, :], cT[:, :], ACT.Copy).then_inc(A.sem, 1)
                    V.wait(e, n, "cr")
                    e.activation(c123[32:32 + E, :], crest[:, :], ACT.Copy).then_inc(A.sem, 1)
                    for i, (x_, a) in enumerate(EH):
                        for q in range(2):
                            T.wait(e, n, f"h{x_}{a}{q}")
                            if i >= 2:
                                V.wait(e, n, f"w{x_ - 1}{a}{q}")
                            e.activation(hb[:, a, q, :], bank[2 + 2 * a + q][:, 0:2 * L], ACT.Relu, bias=b1s[:, x_, a:a + 1]).then_inc(A.sem, 1)
                    T.wait(e, n, "yb")
                    e.activation(yT[:, :], bank[6][:, 0:2 * L], ACT.Copy).then_inc(A.sem, 1)

            @block.vector
            def _(e):
                e.memset(eps[:, :], EPS).then_inc(s_v, 1)
                e.wait_ge(s_t, 1)
                e.tensor_copy(wgT[:, :], bank[0][0:D, 0:E]).then_inc(s_v, 1)
                for x_ in range(E):
                    e.wait_ge(s_t, 1 + 4 * x_ + 4)
                    w11, w22, w31 = (w[:, x_, :] for w in W_PARTS)
                    ps = bank[1][0:D, 0:HID]
                    for dst in (w11[0:D], w11[D:], w31[D:]):
                        e.tensor_copy(dst, ps).then_inc(s_v, 1)
                    e.wait_ge(s_v, 2 + NW * x_ + 3)
                    e.tensor_tensor(wrest[:, :], ps, w11[0:D], ALU.subtract).then_inc(s_v, 1)
                    e.wait_ge(s_v, 2 + NW * x_ + 4)
                    for dst in (w22[0:D], w22[D:]):
                        e.tensor_copy(dst, wrest[:, :]).then_inc(s_v, 1)
                    e.wait_ge(s_v, 2 + NW * x_ + 6)
                    e.tensor_tensor(w31[0:D], wrest[:, :], w22[0:D], ALU.subtract).then_inc(s_v, 1)
                    e.tensor_copy(w2T[:, x_, :, :].rearrange("p a d -> p (a d)"), bank[2][:, 0:2 * D]).then_inc(s_v, 1)
                e.wait_ge(s_id, 4)
                e.memset(sel[:, :, :], 0.0).then_inc(s_v, 1)
                e.memset(c123[:, :], 0.0).then_inc(s_v, 1)
                e.wait_ge(s_v, 2 + NW * E + 2)
                for g in range(3):
                    e.tensor_copy(sel[32 * g:32 * g + E, :, :], ident[32 * g:32 * g + E, 32 * g:32 * g + E].unsqueeze(2).to_broadcast([E, E, 128])).then_inc(s_v, 1)
                e.wait_ge(s_v, 2 + NW * E + 5)
                e.nop().then_inc(V.sem, V.P)
                tok = lambda t: t.unsqueeze(2).to_broadcast([TL, 8, E])
                flat = lambda t: t[:, :, :, :].rearrange("p k x y -> p (k x) y")
                with e.Fori(0, G) as n:
                    hin.wait(e, n, "h")
                    e.tensor_tensor(ht[:, :, :], ht[:, :, :], yt[:, :, :], ALU.add).then_inc(V.sem, 1)
                    V.wait(e, n, "h3")
                    norm_vector(e, V, A, n, ht[:, :, :], 8, (s1, s2, sq), xn[:, :, :])
                    T.wait(e, n, "xT")
                    e.tensor_copy(xT[:, 0:2 * L], bank[0][0:D, 0:2 * L]).then_inc(V.sem, 1)
                    V.wait(e, n, "xT0")
                    A.wait(e, n, "xT1")
                    e.tensor_copy(x13[0:D, :], xT[:, :]).then_inc(V.sem, 1)
                    V.wait(e, n, "x1")
                    e.tensor_tensor(xrest[:, :], xT[:, :], x13[0:D, :], ALU.subtract).then_inc(V.sem, 1)
                    A.wait(e, n, "x2")
                    e.tensor_tensor(x13[D:, :], xrest[:, :], x21[0:D, :], ALU.subtract).then_inc(V.sem, 1)
                    T.wait(e, n, "g")
                    e.tensor_tensor(gs[:, :, :], bank[2][0:TL, 0:8 * E].rearrange("p (k x) -> p k x", x=E),
                                    bgb[:, :].unsqueeze(1).to_broadcast([TL, 8, E]), ALU.add).then_inc(V.sem, 1)
                    V.wait(e, n, "gs")
                    mine = gs[:, :, :].unsqueeze(3).to_broadcast([TL, 8, E, E])
                    other = gs[:, :, :].unsqueeze(2).to_broadcast([TL, 8, E, E])
                    e.tensor_tensor(c1[:, :, :, :], other, mine, ALU.is_gt).then_inc(V.sem, 1)
                    e.tensor_tensor(c2[:, :, :, :], other, mine, ALU.is_equal).then_inc(V.sem, 1)
                    V.wait(e, n, "eq")
                    trif = tri[0:TL, :, :].rearrange("p x y -> p (x y)").unsqueeze(1).to_broadcast([TL, 8, E * E])
                    pairs = lambda t: t[:, :, :, :].rearrange("p k x y -> p k (x y)")
                    e.tensor_tensor(pairs(c2), pairs(c2), trif, ALU.mult).then_inc(V.sem, 1)
                    V.wait(e, n, "eqt")
                    e.tensor_tensor(c1[:, :, :, :], c1[:, :, :, :], c2[:, :, :, :], ALU.add).then_inc(V.sem, 1)
                    V.wait(e, n, "cmp")
                    e.tensor_reduce(rk[:, :, :], c1[:, :, :, :], AX, ALU.add).then_inc(V.sem, 1)
                    e.tensor_reduce(mz[:, 0, :], gs[:, :, :], AX, ALU.max).then_inc(V.sem, 1)
                    V.wait(e, n, "m1")
                    e.tensor_tensor(gs[:, :, :], gs[:, :, :], tok(mz[:, 0, :]), ALU.subtract).then_inc(V.sem, 1)
                    A.wait(e, n, "exp")
                    V.wait(e, n, "rk")
                    e.scalar_tensor_tensor(out=ex[:, :, :], in0=rk[:, :, :], scalar=1.5, in1=ex[:, :, :], op0=ALU.is_lt, op1=ALU.mult).then_inc(V.sem, 1)
                    V.wait(e, n, "sel")
                    e.tensor_reduce(mz[:, 1, :], ex[:, :, :], AX, ALU.add).then_inc(V.sem, 1)
                    V.wait(e, n, "z")
                    e.reciprocal(mz[:, 1, :], mz[:, 1, :]).then_inc(V.sem, 1)
                    V.wait(e, n, "rz")
                    e.tensor_tensor(ex[:, :, :], ex[:, :, :], tok(mz[:, 1, :]), ALU.mult).then_inc(V.sem, 1)
                    T.wait(e, n, "cT")
                    e.tensor_copy(cT[:, 0:2 * L], bank[0][0:E, 0:2 * L]).then_inc(V.sem, 1)
                    A.wait(e, n, "c1")
                    e.tensor_tensor(crest[:, :], cT[:, :], c123[0:E, :], ALU.subtract).then_inc(V.sem, 1)
                    V.wait(e, n, "cr")
                    e.tensor_copy(cpart[:, :], crest[:, :]).then_inc(V.sem, 1)
                    V.wait(e, n, "cp")
                    e.tensor_tensor(c123[64:64 + E, :], crest[:, :], cpart[:, :], ALU.subtract).then_inc(V.sem, 1)
                    for i, (x_, a) in enumerate(EH):
                        for q in range(2):
                            A.wait(e, n, f"h{x_}{a}{q}")
                            T.wait(e, n, f"b{x_}{q}" if a == 0 or i < 2 else f"y{i - 2}")
                            e.tensor_tensor(hw[:, a, q, :], hb[:, a, q, :], bank[q][:, 0:2 * L], ALU.mult).then_inc(V.sem, 1)
                    T.wait(e, n, "turn")
                    out.count(e, n)
                    e.tensor_tensor(o[:, :, :].rearrange("p (q k) d -> p q k d", q=2),
                                    bank[7][0:TL, :].rearrange("p (k q d) -> p q k d", k=4, q=2),
                                    ht[:, :, :].rearrange("p (q k) d -> p q k d", q=2), ALU.add).then_inc(V.sem, 1)


class Stages:

    def __init__(self, sem, update, step, unit=1):
        self.sem, self.unit = sem, unit
        self.update, self.steps = update, step
        self.U, self.P = len(update), len(step)
        self.base = self.P
        assert len(set(step)) == self.P and len(set(update)) == self.U
        self.su = {n: i + 1 for i, n in enumerate(step)}
        self.uu = {n: i + 1 for i, n in enumerate(update)}
        self.chunk = self.U + CH * self.P

    def begun(self, c):
        return c * (self.chunk * self.unit) + self.base * self.unit

    def upd(self, c, name):
        return c * (self.chunk * self.unit) + (self.base + self.uu[name]) * self.unit

    def step(self, c, s, name, back=0):
        k = self.base + self.U + self.su[name] - back * self.P
        return c * (self.chunk * self.unit) + s * (self.P * self.unit) + k * self.unit


def recurrent_layer(nc, ZR, VR, GR, YR, S0D, BASED, W0, P0, W1, P1):
    with ExitStack() as ctx:
        def sb(name, shape):
            return ctx.enter_context(nc.sbuf_tensor(name, shape, F32))

        def sem(name):
            return ctx.enter_context(nc.semaphore(name))

        HD, D = 256, 64
        LAST = L + 1 - CH * (NCH - 1)
        MW = CH + 2 * D
        mv1 = sb("mv1", [128, 2, 16, 4, MW])
        mvt = sb("mvt", [128, 32, 2 * HD])
        hist = sb("hist", [128, 8, 2 * HD + D])
        yth = sb("yth", [128, 32, CH])
        hdiag = sb("hdiag", [128, 2, 16, 4, 32])
        ydiag = sb("ydiag", [128, 8, 4, 32])
        gdiag = sb("gdiag", [128, 2, 4, 32])
        ddiag = sb("ddiag", [128, 2, 4, 32])
        adiag = sb("adiag", [128, 2, 4, 32])
        ident = sb("r_ident", [128, 128])
        ones = sb("r_ones", [128, 128])
        repl = sb("repl", [128, 128])
        mi = sb("mi", [128, 8])
        mu = sb("mu", [128, 2])
        xb = sb("xb", [128, HD])
        BW = 2 * HD + CH
        work = sb("work", [128, 2 * BW])
        x, sg, om, sp = (work[:, HD * q:HD * q + HD] for q in range(4))
        h = sb("h", [128, HD])
        dh = sb("dh", [128, HD])
        dl = sb("dl", [128, HD])
        rep = sb("rep", [128, 3, 8, CH])
        y1 = sb("y1", [128, D])
        y = sb("y", [128, 2, D])
        al = sb("al", [128, 1])
        U = sb("U", [128, CH + 2])
        W = sb("W", [128, CH + 2])
        FAC = sb("FAC", [128, CH + 2])
        Wp = sb("Wp", [128, CH + 2])
        Wn = sb("Wn", [128, CH + 2])
        gates = sb("gates", [128, CH, 4])
        baset = sb("baset", [128, BW])
        dott = baset[:, 2 * HD:]
        vt = sb("vt", [128, D])
        cm = sb("cm", [128, 2, 128])
        cu = sb("cu", [128, 3, 8, 4])
        wy, wk = (h[:, :], dh[:, :]), (dl[:, :], xb[:, :])
        SB = 4
        s0s = sb("s0s", [128, SB, 2 * HD])
        zr = sb("zr", [CH * 2, 2, 128])
        ztm = sb("ztm", [128, 2, 2, 32])
        kt = sb("kt", [128, 2, CH])
        krow = sb("krow", [128, 8, D])
        bs = work[:, :].rearrange("p (a f) -> p a f", a=2)
        d3 = work[:, 0:384].rearrange("p (w q) -> p w q", w=3)
        bank = [ctx.enter_context(nc.psum_tensor(f"bank{i}", [128, 512], F32)) for i in range(8)]
        b = [t[:, :] for t in bank]
        psT = (b[0][:, 0:128], b[1][:, 0:128])
        psDT = b[0][:, 128:256]
        psP, psD = b[2], b[2][:, 256:256 + CH]
        psAT, psYT = b[3][:, 0:128], b[3][:, 128:256]
        psGT, psY = b[4][:, 0:128], b[4][:, 128:128 + D]
        psH = b[5]
        psR, psA = b[6][:, 0:HD], b[6][:, HD:2 * HD]
        psE = b[7]
        psZ, psDots, psC, psBase = b[0][:, 0:32], b[0][:, 32:64], b[6], (b[3], b[4])
        psNew = ((b[5], b[7]), (b[1], b[2]))

        SLABS = [(n, j) for n in range(8) for j in range(4)]
        vec_u = ["nfac", "srep", "cm0", "cm1", "d3a", "d3b", "d3c", "cu0", "cu1", "wy0", "wk0"]
        for k in range(32):
            vec_u += [f"wy{k + 1}", f"wk{k + 1}"] if k < 31 else []
            vec_u += [f"{a}{k}" for a in ("sa", "oa", "sb", "ob", "sn", "on")]
        vec_u += ["rw", "rw1", "ru", "ru1", "rf", "rf1", "rp", "ral", "x0"]
        vec_s = ["xa", "xz", "ha", "h", "hd0", "om", "sp", "tabu", "tabw", "tabp", "arep", "alast", "xb1", "xb2",
                 "setu", "setw", "setf", "setn", "grep", "adiag", "y1", "y2", "gdiag", "y", "ydiag", "xpre", "drep",
                 "ddiag", "dh1", "dh2", "newp", "dh3a", "dh3", "da", "d"]
        act_u = []
        for k in range(32):
            act_u += [f"kt{k}", f"zm0{k}", f"zm1{k}", f"c0{k}", f"c1{k}"] + ([f"ds{k}", f"bs0{k}", f"bs1{k}"] if k % 4 == 3 else [])
        act_s = ["siga", "sig", "hd1", "ht", "yt0", "yt1"]
        pe_u = ["ct0", "ct1", "cb", "st0", "so0"]
        for k in range(32):
            pe_u += [f"st{k + 1}", f"so{k + 1}"] if k < 31 else []
            pe_u += [f"zt{k}", f"tr{k}", f"ba{k}"]
        pe_s = ["tra", "tr", "pred", "at", "sprep", "gt", "a", "yp", "yt", "dd", "dt", "dhp", "e"]
        V = Stages(sem("vector_landed"), vec_u, vec_s)
        A = Stages(sem("scalar_landed"), act_u, act_s)
        T = Stages(sem("tensor_landed"), pe_u, pe_s)
        slab_in = [Stages(sem(f"slab_in{q}"), [f"s{k}" for k in range(q, 32, SB)], [], 16) for q in range(SB)]
        slab_out = [Stages(sem(f"slab_out{q}"), [f"s{k}" for k in range(q, 32, SB)], [], 16) for q in range(SB)]
        zr_in = [Stages(sem(f"zr_in{q}"), [f"z{k}" for k in range(q, 32, 2)], [], 16) for q in range(2)]
        base_out = Stages(sem("base_out"), [f"b{n}" for n in range(8)], [], 8 * 16)
        gates_in = Stages(sem("gates_in"), ["in"], [], 8 * 16)
        keys_in = Stages(sem("keys_in"), ["in"], [], 16 * 16)
        base_in = Stages(sem("base_in"), ["first"], ["next"], 16)
        value_in = Stages(sem("value_in"), ["first"], ["next"], 16)
        hist_h = Stages(sem("hist_h"), [], ["h"], 16 * NH)
        hist_y = Stages(sem("hist_y"), [], ["y"], 16 * (NH + 1))
        hist_d = Stages(sem("hist_d"), [], ["d"], 16 * NH)
        for q in (*slab_in, *zr_in, *slab_out, base_out, gates_in, keys_in, base_in, value_in, hist_h, hist_y, hist_d):
            q.base = 0
        s_set, s_own = sem("set_dma"), sem("settled")
        s_pool = sem("pool_set")
        s_v = sem("vec_set")
        s_p = sem("pe_set")
        s_init = sem("init_out")

        def ap(t, off, *dims):
            row = 1
            for q in t.shape[1:]:
                row *= q
            return bass.AP(t, off, [[row, t.shape[0]]] + [list(q) for q in dims])

        def p_dims(src, off=0):
            return src

        w1s, p1s = x[:, 0:128], x[:, 128:256]
        with nc.Block() as block:
            @block.gpsimd
            def _(e):
                e.memset(ident[:, :], 0.0).then_inc(s_pool, 1)
                e.memset(mi[:, :], 1.0).then_inc(s_pool, 1)
                e.memset(mu[:, :], 1.0).then_inc(s_pool, 1)
                e.wait_ge(s_pool, 3)
                e.affine_select(out=ident[:, :], in_=ident[:, :], compare_op=ALU.not_equal, fill=1.0, base=0,
                                pattern=[[-1, 128]], channel_multiplier=1).then_inc(s_pool, 1)
                for k, (t, w, c) in enumerate(((mi, 8, 16), (mu, 2, 64))):
                    e.affine_select(out=t[:, :], in_=t[:, :], compare_op=ALU.is_ge, fill=0.0, base=0,
                                    pattern=[[-c, w]], channel_multiplier=1).then_inc(s_pool, 1)
                    e.wait_ge(s_pool, 5 + 2 * k)
                    e.affine_select(out=t[:, :], in_=t[:, :], compare_op=ALU.is_ge, fill=0.0, base=c - 1,
                                    pattern=[[c, w]], channel_multiplier=-1).then_inc(s_pool, 1)
                    e.wait_ge(s_pool, 6 + 2 * k)
                e.memset(mv1[:, :, :, :, :], 0.0).then_inc(s_pool, 1)
                e.memset(hdiag[:, :, :, :, :], 0.0).then_inc(s_pool, 1)
                e.memset(hist[:, :, :], 0.0).then_inc(s_pool, 1)

            @block.sync
            def _(e):
                e.dma_start(w1s.rearrange("p (a d) -> p a d", a=2), W1.rearrange("(a p) d -> p a d", p=128)).then_inc(s_set, 16)
                e.dma_start(p1s.rearrange("p (a d) -> p a d", a=2), P1.rearrange("(a p) d -> p a d", p=128)).then_inc(s_set, 16)
                for u in range(2):
                    e.dma_start(sg[64 * u:64 * u + 64, :], W0).then_inc(s_set, 16)
                    e.dma_start(h[64 * u:64 * u + 64, :], P0).then_inc(s_set, 16)
                e.wait_ge(s_v, 7)
                for k in range(32):
                    e.dma_start(S0D[k, :, :], s0s[:, 0, :]).then_inc(s_init, 16)
                e.dma_start(BASED[CH, :, 0:2 * HD], s0s[:, 0, :]).then_inc(s_init, 16)
                e.dma_start(BASED[CH, :, 2 * HD:], yth[:, 0, :]).then_inc(s_init, 16)
                e.wait_ge(s_init, 34 * 16)

            @block.vector
            def _(e):
                e.wait_ge(s_set, 96)
                e.memset(mvt[:, :, :], 0.0).then_inc(s_v, 1)
                e.memset(s0s[:, 0, HD:], 0.0).then_inc(s_v, 1)
                e.memset(ydiag[:, :, :, :], 0.0).then_inc(s_v, 1)
                e.tensor_tensor(s0s[:, 0, 0:HD], sg, h[:, :], ALU.add).then_inc(s_v, 1)
                for u in range(2):
                    e.tensor_tensor(om.rearrange("p (a u d) -> p a u d", a=2, u=2)[:, :, u, :],
                                    w1s.rearrange("p (a d) -> p a d", a=2),
                                    p1s.rearrange("p (a d) -> p a d", a=2), ALU.add).then_inc(s_v, 1)
                e.memset(yth[:, :, :], 0.0).then_inc(s_v, 1)
                for t in (gdiag, ddiag, adiag):
                    e.memset(t[:, :, :, :], 0.0).then_inc(s_v, 1)
                e.memset(ones[:, :], 1.0).then_inc(s_v, 1)
                e.memset(U[:, :], 0.0).then_inc(s_v, 1)
                e.memset(Wp[:, :], 0.0).then_inc(s_v, 1)
                e.memset(FAC[:, :], 1.0).then_inc(s_v, 1)
                e.memset(y[:, :, :], 0.0).then_inc(s_v, 1)
                e.memset(dl[:, :], 0.0).then_inc(s_v, 1)
                e.wait_ge(s_v, 16)
                e.memset(U[:, CH + 1:CH + 2], 1.0).then_inc(s_v, 1)
                e.memset(Wp[:, CH:CH + 1], 1.0).then_inc(s_v, 1)
                e.wait_ge(s_pool, 4)
                for st in range(2):
                    e.tensor_copy(ap(repl, 16 * st, [32, 4], [1, 16]), ap(ident, 0, [32, 4], [1, 16])).then_inc(s_v, 1)
                e.wait_ge(s_p, 2)
                for a in range(2):
                    e.tensor_copy(mvt[:, :, 128 * a:128 * a + 128], psT[a].unsqueeze(1).to_broadcast([128, 32, 128])).then_inc(s_v, 1)
                e.wait_ge(s_v, 22)
                e.engine_nop().then_inc(V.sem, V.base)

            @block.tensor
            def _(e):
                e.wait_ge(s_v, 6)
                e.wait_ge(s_pool, 4)
                for a in range(2):
                    e.transpose(psT[a], om[:, 128 * a:128 * a + 128], ident[:, :]).then_inc(s_p, 1)
                e.wait_ge(s_p, 2)
                e.nop().then_inc(T.sem, T.base)

            @block.scalar
            def _(e):
                e.nop().then_inc(A.sem, A.base)

        def load_base(e, s):
            e.dma_start(baset[:, :].unsqueeze(1), BASED[s:s + 1, :, :].rearrange("a p f -> p a f")).then_inc(base_in.sem, 16)

        def load_value(e, c, s):
            e.dma_start(vt[:, :].unsqueeze(1), VR[bass.ds(c * CH + s, 1), :, :].rearrange("a p f -> p a f")).then_inc(value_in.sem, 16)

        def to_hist(e, s, src, lo, hi, sm):
            for m in range(2):
                for j in range(4):
                    row = 8 * (2 * HD + D)
                    dst = bass.AP(hist, s * row + (m * 4 + j) * (2 * HD + D) + lo, [[CH * row, 8], [1, hi - lo]])
                    p = 32 * j + 8 * m
                    e.dma_start(dst, src[p:p + 8, :]).then_inc(sm, 16)

        def slab_done(e, c, k):
            e.wait_ge(T.sem, T.upd(c, f"ba{k}"))
            settled(e, s_own)
            e.wait_ge(V.sem, V.upd(c, f"on{k}"))
            e.dma_start(S0D[k, :, :], s0s[:, k % SB, :]).then_inc(slab_out[k % SB].sem, 16)

        def products_done(e, c, n, half):
            e.wait_ge(A.sem, A.upd(c, f"bs1{4 * n + 3}"))
            settled(e, s_own)
            for j in (2 * half, 2 * half + 1):
                for u in range(2):
                    dst = BASED[0:CH, :, :].rearrange("t (q r) f -> r q t f", r=16)[2 * n + u, 2 * j:2 * j + 2]
                    row = 64 * (j % 2) + 32 * u
                    e.dma_start(dst, bs[row:row + 32, half, :]).then_inc(base_out.sem, 16)

        def load_slab(e, k):
            e.dma_start(s0s[:, k % SB, :], S0D[k, :, :]).then_inc(slab_in[k % SB].sem, 16)

        def load_new_keys(e, c, k):
            n, j = SLABS[k]
            src = ZR[bass.ds(c * CH + CH, CH), :, :].rearrange("t (q n u) d -> t q n (u d)", q=8, n=8)
            e.dma_start(zr[:, k % 2, :], src[:, 2 * j:2 * j + 2, n, :].rearrange("t st f -> st t f")).then_inc(zr_in[k % 2].sem, 16)

        def load_ahead(e, c):
            for i in range(8):
                for m in range(2):
                    src = ZR[bass.ds(c * CH, CH), :, :].rearrange("t (j st m i) d -> i st m t j d", j=4, st=2, m=2)[i, 0, m]
                    e.dma_start(krow[16 * i:16 * i + 16, 4 * m:4 * m + 4, :], src).then_inc(keys_in.sem, 16)
            for k in range(SB):
                load_slab(e, k)
            for k in range(2):
                load_new_keys(e, c, k)

        def diag_h(hf):
            return ap(hdiag, hf * 2048, [16, 8], [129, 16])

        def turned_h(hf):
            return psT[hf].rearrange("p (q r) -> p q r", r=16)

        def spread(dst, src):
            return (ap(dst, 0, [16, 8], [136, 2], [1, 8]), src.rearrange("p (q m i) -> p q m i", q=8, m=2),
                    ap(mi, 0, [0, 8], [0, 2], [1, 8]), ALU.mult)

        with nc.Block() as block:
            @block.sync
            def _(e):
                load_ahead(e, 0)

                def chunk(c, steps):
                    e.wait_ge(V.sem, V.begun(c))
                    e.wait_ge(T.sem, T.begun(c))
                    e.wait_ge(A.sem, A.begun(c))
                    for q in range(8):
                        e.dma_start(gates[16 * q:16 * q + 16, :, :],
                                    GR[16 * (q // 2):16 * (q // 2) + 16, bass.ds(c * CH, CH), :]).then_inc(gates_in.sem, 16)
                    for k in range(2, 32 + 2):
                        if k < 32:
                            if k >= SB:
                                e.wait_ge(slab_out[k % SB].sem, slab_out[k % SB].upd(c, f"s{k - SB}"))
                                settled(e, s_own)
                                load_slab(e, k)
                            e.wait_ge(T.sem, T.upd(c, f"zt{k - 2}"))
                            settled(e, s_own)
                            load_new_keys(e, c, k)
                        slab_done(e, c, k - 2)
                        if k >= 6 and k % 4 in (2, 3):
                            products_done(e, c, k // 4 - 1, k % 4 - 2)
                    for half in range(2):
                        products_done(e, c, 7, half)
                    for k in range(32 - SB, 32):
                        e.wait_ge(slab_out[k % SB].sem, slab_out[k % SB].upd(c, f"s{k}"))
                        settled(e, s_own)
                    e.wait_ge(base_out.sem, base_out.upd(c, "b7"))
                    load_base(e, 0)
                    load_value(e, c, 0)
                    for s in range(steps):
                        e.wait_ge(V.sem, V.step(c, s - 1, "xb2") if s else V.upd(c, "x0"))
                        load_base(e, s + 1)
                        e.wait_ge(V.sem, V.step(c, s, "h"))
                        to_hist(e, s, h[:, :], 0, HD, hist_h.sem)
                        if s == 0 and steps == CH:
                            load_ahead(e, c + 1)
                        e.wait_ge(V.sem, V.step(c, s, "y1"))
                        settled(e, s_own)
                        load_value(e, c, s + 1)
                        e.wait_ge(V.sem, V.step(c, s, "y"))
                        to_hist(e, s, y[:, 0, :], HD, HD + D, hist_y.sem)
                        e.dma_start(YR[bass.ds(c * CH + s, 1), :, :].rearrange("a p d -> p a d"), y[:, 0:1, :]).then_inc(hist_y.sem, 16)
                        e.wait_ge(V.sem, V.step(c, s, "d"))
                        to_hist(e, s, dl[:, :], HD + D, 2 * HD + D, hist_d.sem)

                with e.Fori(0, NCH - 1) as c:
                    chunk(c, CH)
                chunk(NCH - 1, LAST)
                e.wait_ge(hist_h.sem, hist_h.unit * (L + 1))
                e.wait_ge(hist_y.sem, hist_y.unit * (L + 1))
                e.wait_ge(hist_d.sem, hist_d.unit * (L + 1))

            @block.scalar
            def _(e):
                e.preload_act_table(ACT.Sigmoid)

                def chunk(c, steps):
                    for k, (n, j) in enumerate(SLABS):
                        e.wait_ge(T.sem, T.upd(c, f"zt{k}"))
                        e.activation(kt[:, k % 2, :], psZ[:, 0:CH], ACT.Copy).then_inc(A.sem, 1)
                        for u in range(2):
                            e.activation(ztm[:, k % 2, u, :], psZ, ACT.Copy, scale=mu[:, u:u + 1]).then_inc(A.sem, 1)
                        e.wait_ge(T.sem, T.upd(c, f"tr{k}"))
                        for hf in range(2):
                            src = psC[:, 256 * hf:256 * hf + 256].rearrange("p (w u d) -> p u w d", w=2, u=2)
                            dst = mv1[:, hf, 2 * n:2 * n + 2, j, CH:].rearrange("p u (w d) -> p u w d", w=2)
                            e.activation(dst, src, ACT.Copy).then_inc(A.sem, 1)
                        if k % 4 == 3:
                            e.wait_ge(T.sem, T.upd(c, f"ba{k}"))
                            if k > 3:
                                e.wait_ge(base_out.sem, base_out.upd(c, f"b{n - 1}"))
                            e.wait_ge(T.sem, T.upd(c, "cb"))
                            e.activation(bs[:, :, 2 * HD:], psDots.rearrange("p (a s) -> p a s", a=2), ACT.Copy).then_inc(A.sem, 1)
                            for a in range(2):
                                e.activation(bs[:, a, 0:2 * HD], psBase[a], ACT.Copy).then_inc(A.sem, 1)
                    with e.Fori(0, steps) as s:
                        for hf, name in enumerate(("xa", "xz")):
                            e.wait_ge(V.sem, V.step(c, s, name))
                            half = slice(128 * hf, 128 * hf + 128)
                            e.activation(sg[:, half], x[:, half], ACT.Sigmoid).then_inc(A.sem, 1)
                        e.wait_ge(T.sem, T.step(c, s, "tr"))
                        e.activation(diag_h(1), turned_h(1), ACT.Copy).then_inc(A.sem, 1)
                        e.wait_ge(T.sem, T.step(c, s, "pred"))
                        src = ap(hdiag, 0, [2048, 2], [129, 16], [32, 4])
                        dst = mv1[:, :, :, :, bass.ds(s, 1)].rearrange("p a r j o -> p a r (j o)")
                        e.activation(dst, src, ACT.Copy).then_inc(A.sem, 1)
                        e.wait_ge(T.sem, T.step(c, s, "dd"))
                        for u in range(2):
                            src = bass.AP(ydiag, 64 * u * 1024 + u, [[1024, 64], [130, 8], [32, 4]])
                            dst = yth[64 * u:64 * u + 64, :, bass.ds(s, 1)].rearrange("p (n j) o -> p n (j o)", n=8)
                            e.activation(dst, src, ACT.Copy).then_inc(A.sem, 1)

                with e.Fori(0, NCH - 1) as c:
                    chunk(c, CH)
                chunk(NCH - 1, LAST)

            @block.tensor
            def _(e):
                def chunk(c, steps):
                    for w in range(2):
                        e.wait_ge(V.sem, V.upd(c, "srep"))
                        e.matmul(psP[:, 128 * w:128 * w + 128], rep[:, w, :, :].rearrange("p i s -> p (i s)"), ident[:, :],
                                 start=True, stop=True).then_inc(T.sem, 1)
                    e.wait_ge(V.sem, V.upd(c, "d3c"))
                    e.matmul(psH[:, 0:384], ones[:, :], d3.rearrange("p w q -> p (w q)"), start=True, stop=True).then_inc(T.sem, 1)

                    def new_terms(k):
                        n, j = SLABS[k]
                        slot = (n // 4) * 4 + j
                        e.wait_ge(V.sem, V.upd(c, f"wk{k}"))
                        if k == 0:
                            e.wait_ge(V.sem, V.upd(c, "cu1"))
                            e.wait_ge(hist_h.sem, c * (hist_h.unit * CH))
                            e.wait_ge(hist_d.sem, c * (hist_d.unit * CH))
                        if k >= 2:
                            e.wait_ge(V.sem, V.upd(c, f"on{k - 2}"))
                        for lay, wt, lo in ((0, wy[k % 2], 0), (1, wk[k % 2], HD + D)):
                            for w in range(2):
                                mm = e.matmul(psNew[k % 2][lay][:, HD * w:HD * w + HD], wt[:, 128 * w:128 * w + 128],
                                              hist[:, slot, lo:lo + HD], start=True, stop=True)
                            mm.then_inc(T.sem, 1)

                    new_terms(0)
                    for k, (n, j) in enumerate(SLABS):
                        if k < 31:
                            new_terms(k + 1)
                        e.wait_ge(zr_in[k % 2].sem, zr_in[k % 2].upd(c, f"z{k}"))
                        if k:
                            e.wait_ge(A.sem, A.upd(c, f"ds{k - 1}" if k % 4 == 0 else f"zm1{k - 1}"))
                        e.matmul(psZ, zr[:, k % 2, :], ident[0:32, 0:32], start=True, stop=True).then_inc(T.sem, 1)
                        e.wait_ge(V.sem, V.upd(c, f"sn{k}"))
                        if k:
                            e.wait_ge(A.sem, A.upd(c, f"c1{k - 1}"))
                        for hf in range(2):
                            for w in range(2):
                                o = 256 * hf + 128 * w
                                mm = e.transpose(psC[:, o:o + 128], mvt[:, k, HD * w + 128 * hf:HD * w + 128 * hf + 128], ident[:, :])
                        mm.then_inc(T.sem, 1)
                        e.wait_ge(V.sem, V.upd(c, f"on{k}"))
                        e.wait_ge(A.sem, A.upd(c, f"zm1{k}"))
                        rows, zk = slice(64 * (j % 2), 64 * (j % 2) + 64), ztm[:, k % 2, :, :].rearrange("p u z -> p (u z)")
                        e.matmul(psBase[j // 2][rows, :], zk, s0s[:, k % SB, :], start=True, stop=True)
                        e.matmul(psDots[rows, CH * (j // 2):CH * (j // 2) + CH], zk, kt[:, k % 2, :], start=True, stop=True).then_inc(T.sem, 1)
                    with e.Fori(0, steps) as s:
                        e.wait_ge(A.sem, A.step(c, s, "yt1", 1))
                        for hf, name in enumerate(("ha", "h")):
                            e.wait_ge(V.sem, V.step(c, s, name))
                            e.transpose(psT[hf], h[:, 128 * hf:128 * hf + 128], ident[:, :]).then_inc(T.sem, 1)
                        for hf in range(2):
                            if hf == 0:
                                e.wait_ge(V.sem, V.step(c, s, "hd0"))
                            else:
                                e.wait_ge(A.sem, A.step(c, s, "hd1"))
                            for r in range(16):
                                for j in range(4):
                                    mm = e.matmul(psP[32 * j:32 * j + 32, 0:MW], hdiag[:, hf, r, j, :], mv1[:, hf, r, j, :],
                                                  start=(hf == 0 and r == 0), stop=(hf == 1 and r == 15))
                        mm.then_inc(T.sem, 1)
                        e.wait_ge(V.sem, V.step(c, s, "arep"))
                        e.matmul(psAT, rep[:, 0, :, :].rearrange("p i s -> p (i s)"), ident[:, :], start=True, stop=True).then_inc(T.sem, 1)
                        e.wait_ge(V.sem, V.step(c, s, "sp"))
                        e.matmul(psR, repl[:, :], sp, start=True, stop=True).then_inc(T.sem, 1)
                        e.wait_ge(V.sem, V.step(c, s, "grep"))
                        e.matmul(psGT, rep[:, 1, :, :].rearrange("p i s -> p (i s)"), ident[:, :], start=True, stop=True).then_inc(T.sem, 1)
                        e.wait_ge(V.sem, V.step(c, s, "adiag"))
                        e.wait_ge(hist_d.sem, c * (hist_d.unit * CH) + s * hist_d.unit)
                        for m in range(2):
                            for j in range(4):
                                mm = e.matmul(psA[32 * j:32 * j + 32, :], adiag[:, m, j, :], hist[:, m * 4 + j, HD + D:],
                                              start=(m == 0), stop=(m == 1))
                        mm.then_inc(T.sem, 1)
                        e.wait_ge(V.sem, V.step(c, s, "gdiag"))
                        e.wait_ge(hist_y.sem, c * (hist_y.unit * CH) + s * hist_y.unit)
                        for m in range(2):
                            for j in range(4):
                                mm = e.matmul(psY[32 * j:32 * j + 32, :], gdiag[:, m, j, :], hist[:, m * 4 + j, HD:HD + D],
                                              start=(m == 0), stop=(m == 1))
                        mm.then_inc(T.sem, 1)
                        e.wait_ge(V.sem, V.step(c, s, "y"))
                        e.matmul(psYT, y[:, :, :].rearrange("p u d -> p (u d)"), repl[:, :], start=True, stop=True).then_inc(T.sem, 1)
                        e.wait_ge(V.sem, V.step(c, s, "ydiag"))
                        for n in range(8):
                            for j in range(4):
                                mm = e.matmul(psD[32 * j:32 * j + 32, :], ydiag[:, n, j, :], yth[:, 4 * n + j, :],
                                              start=(n == 0), stop=(n == 7))
                        mm.then_inc(T.sem, 1)
                        for n in range(8):
                            if n == 4:
                                e.wait_ge(V.sem, V.step(c, s, "drep"))
                                e.matmul(psDT, rep[:, 2, :, :].rearrange("p i s -> p (i s)"), ident[:, :], start=True, stop=True).then_inc(T.sem, 1)
                            for j in range(4):
                                mm = e.matmul(psH[32 * j:32 * j + 32, :], ydiag[:, n, j, :], mvt[:, 4 * n + j, :],
                                              start=(n == 0), stop=(n == 7))
                        mm.then_inc(T.sem, 1)
                        e.wait_ge(V.sem, V.step(c, s, "ddiag"))
                        e.wait_ge(hist_h.sem, hist_h.step(c, s, "h"))
                        for m in range(2):
                            for j in range(4):
                                mm = e.matmul(psE[32 * j:32 * j + 32, 0:HD], ddiag[:, m, j, :], hist[:, m * 4 + j, 0:HD],
                                              start=(m == 0), stop=(m == 1))
                        mm.then_inc(T.sem, 1)

                with e.Fori(0, NCH - 1) as c:
                    chunk(c, CH)
                chunk(NCH - 1, LAST)

            @block.vector
            def _(e):
                def own(val):
                    e.wait_ge(V.sem, val)

                def chunk(c, steps):
                    def go(ins, name):
                        ins.then_inc(V.sem, 1)

                    own(V.begun(c))
                    N16, N17 = slice(CH, CH + 1), slice(CH + 1, CH + 2)
                    go(e.tensor_tensor(Wn[:, :], U[:, :], FAC[:, :], ALU.mult), "nfac")
                    own(V.upd(c, "nfac"))
                    e.wait_ge(T.sem, T.begun(c))
                    for w, t in enumerate((Wp, Wn)):
                        ins = e.tensor_copy(rep[:, w, :, :], t[:, 0:CH].unsqueeze(1).to_broadcast([128, 8, CH]))
                    go(ins, "srep")
                    for w in range(2):
                        e.wait_ge(T.sem, T.upd(c, "ct1"))
                        go(e.tensor_tensor(cm[:, w, :].rearrange("p (q i) -> p q i", i=8),
                                           psP[:, 128 * w:128 * w + 128].rearrange("p (q i) -> p q i", i=8),
                                           ap(mi, 0, [0, 16], [1, 8]), ALU.mult), "cm")
                    e.wait_ge(A.sem, A.begun(c))
                    e.wait_ge(base_out.sem, c * (base_out.unit * 8))
                    for w, col in enumerate((Wp[:, N16], Wp[:, N17], Wn[:, N17])):
                        go(e.tensor_scalar(d3[:, w, :], ident[:, :], col, None, ALU.mult), "d3")
                    e.wait_ge(T.sem, T.upd(c, "cb"))
                    for u in range(2):
                        src = psH[64 * u:64 * u + 64, 0:384].rearrange("p (w j st n u) -> p w st u n j", w=3, j=4, st=2, u=2)[:, :, 0, u]
                        go(e.tensor_copy(cu[64 * u:64 * u + 64, :, :, :], src), "cu")
                    own(V.upd(c, "cu1"))
                    e.wait_ge(keys_in.sem, keys_in.upd(c, "in"))
                    e.wait_ge(hist_y.sem, c * (hist_y.unit * CH))

                    def weigh(k):
                        n, j = SLABS[k]
                        slot = (n // 4) * 4 + j
                        if k >= 2:
                            e.wait_ge(T.sem, T.upd(c, f"so{k - 2}"))
                        wt = cm[:, :, 32 * j + 2 * n:32 * j + 2 * n + 2].unsqueeze(3).to_broadcast([128, 2, 2, D])
                        for t, row, name in ((wy, hist[:, slot, HD:HD + D], "wy"), (wk, krow[:, slot, :], "wk")):
                            src = row.unsqueeze(1).unsqueeze(1).to_broadcast([128, 2, 2, D])
                            go(e.tensor_tensor(t[k % 2].rearrange("p (w u d) -> p w u d", w=2, u=2), src, wt, ALU.mult), name)

                    e.wait_ge(hist_h.sem, c * (hist_h.unit * CH))
                    e.wait_ge(hist_d.sem, c * (hist_d.unit * CH))
                    weigh(0)
                    for k, (n, j) in enumerate(SLABS):
                        if k < 31:
                            weigh(k + 1)
                        ca, cb, ce = (cu[:, w, n, j:j + 1] for w in range(3))
                        e.wait_ge(slab_in[k % SB].sem, slab_in[k % SB].upd(c, f"s{k}"))
                        both = ((mvt[:, k, :], psNew[k % 2][0], "s"), (s0s[:, k % SB, :], psNew[k % 2][1], "o"))
                        for t, ps, lay in both:
                            e.wait_ge(T.sem, T.upd(c, f"st{k}" if lay == "s" else f"so{k}"))
                            go(e.scalar_tensor_tensor(out=t[:, 0:HD], in0=t[:, 0:HD], scalar=ca, in1=ps[:, 0:HD],
                                                      op0=ALU.mult, op1=ALU.add), lay + "a")
                        for t, ps, lay in both:
                            own(V.upd(c, f"{lay}a{k}"))
                            go(e.scalar_tensor_tensor(out=t[:, 0:HD], in0=t[:, HD:], scalar=cb, in1=t[:, 0:HD],
                                                      op0=ALU.mult, op1=ALU.add), lay + "b")
                        for t, ps, lay in both:
                            own(V.upd(c, f"{lay}b{k}"))
                            go(e.scalar_tensor_tensor(out=t[:, HD:], in0=t[:, HD:], scalar=ce, in1=ps[:, HD:2 * HD],
                                                      op0=ALU.mult, op1=ALU.add), lay + "n")
                    own(V.upd(c, "on31"))
                    go(e.memset(W[:, :], 0.0), "rw")
                    own(V.upd(c, "rw"))
                    go(e.memset(W[:, N16], 1.0), "rw1")
                    go(e.memset(U[:, :], 0.0), "ru")
                    own(V.upd(c, "ru"))
                    go(e.memset(U[:, N17], 1.0), "ru1")
                    go(e.memset(FAC[:, 0:CH], 0.0), "rf")
                    go(e.memset(FAC[:, CH:], 1.0), "rf1")
                    own(V.upd(c, "rf1"))
                    go(e.tensor_copy(Wp[:, :], W[:, :]), "rp")
                    go(e.memset(al[:, :], 0.0), "ral")
                    e.wait_ge(gates_in.sem, gates_in.upd(c, "in"))
                    e.wait_ge(base_in.sem, base_in.upd(c, "first"))
                    e.wait_ge(T.sem, T.upd(c, "ba31"))
                    go(e.tensor_copy(xb[:, :], baset[:, 0:HD]), "x0")
                    with e.Fori(0, steps) as s:
                        def st(name, back=0):
                            return V.step(c, s, name, back)

                        nm = lambda ins: ins.then_inc(V.sem, 1)
                        if True:
                            own(V.upd(c, "x0") + s * V.P)
                            for hf in range(2):
                                half = slice(128 * hf, 128 * hf + 128)
                                nm(e.scalar_tensor_tensor(out=x[:, half], in0=dl[:, half], scalar=al[:, 0:1], in1=xb[:, half],
                                                          op0=ALU.mult, op1=ALU.add))
                            e.wait_ge(hist_h.sem, c * (hist_h.unit * CH) + s * hist_h.unit)
                            for hf, name in enumerate(("siga", "sig")):
                                half = slice(128 * hf, 128 * hf + 128)
                                e.wait_ge(A.sem, A.step(c, s, name))
                                nm(e.tensor_tensor(h[:, half], x[:, half], sg[:, half], ALU.mult))
                            e.wait_ge(T.sem, T.step(c, s, "tra"))
                            e.wait_ge(A.sem, A.step(c, s, "yt1", 1))
                            nm(e.tensor_copy(diag_h(0), turned_h(0)))
                            own(st("h"))
                            nm(e.scalar_tensor_tensor(out=om, in0=sg, scalar=1.0, in1=h[:, :],
                                                      op0=ALU.subtract, op1=ALU.mult))
                            own(st("om"))
                            nm(e.tensor_tensor(sp, sg, om, ALU.subtract))
                            g = lambda q: gates[:, bass.ds(s, 1), q:q + 1].rearrange("p a b -> p (a b)")
                            nm(e.tensor_scalar(U[:, :], U[:, :], g(0), None, ALU.mult))
                            own(st("tabu"))
                            nm(e.scalar_tensor_tensor(out=W[:, :], in0=W[:, :], scalar=g(1), in1=U[:, :],
                                                      op0=ALU.mult, op1=ALU.add))
                            own(st("tabw"))
                            nm(e.tensor_tensor(Wn[:, :], W[:, :], FAC[:, :], ALU.mult))
                            e.wait_ge(base_in.sem, base_in.step(c, s, "next"))
                            own(st("tabp"))
                            nm(e.tensor_tensor(rep[:, 0, :, :], dott.unsqueeze(1).to_broadcast([128, 8, CH]),
                                               Wn[:, 0:CH].unsqueeze(1).to_broadcast([128, 8, CH]), ALU.mult))
                            nm(e.tensor_scalar(al[:, :], dott[:, bass.ds(s, 1)], g(2), None, ALU.mult))
                            nm(e.tensor_scalar(xb[:, :], baset[:, 0:HD], Wn[:, N16], None, ALU.mult))
                            own(st("xb1"))
                            nm(e.scalar_tensor_tensor(out=xb[:, :], in0=baset[:, HD:2 * HD], scalar=Wn[:, N17], in1=xb[:, :],
                                                      op0=ALU.mult, op1=ALU.add))
                            own(st("xb2"))
                            nm(e.tensor_copy(U[:, bass.ds(s, 1)], ones[:, 0:1]))
                            nm(e.tensor_copy(W[:, bass.ds(s, 1)], ones[:, 0:1]))
                            nm(e.tensor_copy(FAC[:, bass.ds(s, 1)], g(2)))
                            nm(e.tensor_copy(Wn[:, bass.ds(s, 1)], g(2)))
                            e.wait_ge(T.sem, T.step(c, s, "pred"))
                            nm(e.tensor_tensor(rep[:, 1, :, :], psP[:, 0:CH].unsqueeze(1).to_broadcast([128, 8, CH]),
                                               Wp[:, 0:CH].unsqueeze(1).to_broadcast([128, 8, CH]), ALU.mult))
                            e.wait_ge(T.sem, T.step(c, s, "at"))
                            nm(e.tensor_tensor(*spread(adiag, psAT)))
                            e.wait_ge(value_in.sem, value_in.upd(c, "first") + s * 16)
                            nm(e.scalar_tensor_tensor(out=y1[:, :], in0=psP[:, CH:CH + D], scalar=Wp[:, N16], in1=vt[:, :],
                                                      op0=ALU.mult, op1=ALU.subtract))
                            own(st("y1"))
                            nm(e.scalar_tensor_tensor(out=y1[:, :], in0=psP[:, CH + D:MW], scalar=Wp[:, N17], in1=y1[:, :],
                                                      op0=ALU.mult, op1=ALU.add))
                            e.wait_ge(T.sem, T.step(c, s, "gt"))
                            nm(e.tensor_tensor(*spread(gdiag, psGT)))
                            e.wait_ge(T.sem, T.step(c, s, "yp"))
                            own(st("y2"))
                            e.wait_ge(hist_y.sem, c * (hist_y.unit * CH) + s * hist_y.unit)
                            nm(e.tensor_tensor(y[:, :, :], psY.unsqueeze(1).to_broadcast([128, 2, D]),
                                               y1[:, :].unsqueeze(1).to_broadcast([128, 2, D]), ALU.add))
                            e.wait_ge(T.sem, T.step(c, s, "yt"))
                            nm(e.tensor_tensor(ap(ydiag, 0, [16, 8], [130, 8], [1, 2]),
                                               psYT.rearrange("p (q n u) -> p q n u", q=8, n=8),
                                               ap(mu, 0, [0, 8], [0, 8], [1, 2]), ALU.mult))
                            e.wait_ge(T.sem, T.step(c, s, "a"))
                            nm(e.tensor_tensor(xb[:, :], xb[:, :], psA, ALU.add))
                            e.wait_ge(T.sem, T.step(c, s, "dd"))
                            nm(e.tensor_tensor(rep[:, 2, :, :], psD.unsqueeze(1).to_broadcast([128, 8, CH]),
                                               Wp[:, 0:CH].unsqueeze(1).to_broadcast([128, 8, CH]), ALU.mult))
                            e.wait_ge(T.sem, T.step(c, s, "dt"))
                            nm(e.tensor_tensor(*spread(ddiag, psDT)))
                            e.wait_ge(T.sem, T.step(c, s, "dhp"))
                            nm(e.tensor_scalar(dh[:, :], psH[:, 0:HD], Wp[:, N16], None, ALU.mult))
                            own(st("dh1"))
                            nm(e.scalar_tensor_tensor(out=dh[:, :], in0=psH[:, HD:], scalar=Wp[:, N17], in1=dh[:, :],
                                                      op0=ALU.mult, op1=ALU.add))
                            own(st("dh2"))
                            nm(e.tensor_copy(Wp[:, :], Wn[:, :]))
                            e.wait_ge(T.sem, T.step(c, s, "e"))
                            halves = (slice(0, 128), slice(128, 256))
                            for half in halves:
                                nm(e.tensor_tensor(dh[:, half], dh[:, half], psE[:, half], ALU.add))
                            e.wait_ge(hist_d.sem, c * (hist_d.unit * CH) + s * hist_d.unit)
                            for half, name in zip(halves, ("dh3a", "dh3")):
                                own(st(name))
                                nm(e.tensor_tensor(dl[:, half], dh[:, half], psR[:, half], ALU.mult))

                with e.Fori(0, NCH - 1) as c:
                    chunk(c, CH)
                chunk(NCH - 1, LAST)


def audio_tower(nc, x, filt, W_k, b_k, Wqk, Wv, Wpos, bpos, Wproj, bproj, gating, wr, br, w1, b1, w2, b2,
                W_fused, W0, W1, P0, P1, Wg, bg, E1, be1, E2, be2, out):
    def scratch(name, *shape):
        return nc.dram_tensor(f"between_{name}", shape, F32, kind="Internal").ap()

    H0, H1, H2, XN = (scratch(n, B, TL, 2, D) for n in ("h_tok", "h_att", "h_ffn", "x_ffn"))
    T_ = CH * NCH
    ZR, VR, YR = scratch("keys", T_ + CH + 1, 128, D), scratch("values", T_ + 1, 128, D), scratch("recurrent", T_, 128, D)
    GR = scratch("gates", B, T_, 4)
    token_layer(nc, x, filt, W_k, b_k, H0)
    attention_layer(nc, Wqk, Wv, Wpos, bpos, Wproj, bproj, gating, H0, H1)
    ffn_layer(nc, wr, br, w1, b1, w2, b2, H1, H2, XN, scratch("w_by_tile", B, L), scratch("w_by_batch", B, L))
    key_layer(nc, W_fused, H2, ZR, VR, GR)
    recurrent_layer(nc, ZR, VR, GR, YR, scratch("state0", 32, 128, 512), scratch("base", CH + 1, 128, 512 + CH),
                    W0, P0, W1, P1)
    expert_layer(nc, Wg, bg, E1, be1, E2, be2, H2, YR, out)


_INS = ['x', 'L0_tok_filt', 'L0_tok_W_k', 'L0_tok_b_k', 'L0_attn_Wqk', 'L0_attn_Wv', 'L0_attn_Wpos', 'L0_attn_bpos',
        'L0_attn_Wproj', 'L0_attn_bproj', 'L0_attn_gating', 'L0_ffn_wr', 'L0_ffn_br', 'L0_ffn_w1', 'L0_ffn_b1',
        'L0_ffn_w2', 'L0_ffn_b2', 'L1_attn_W_fused', 'L1_attn_W0', 'L1_attn_W1', 'L1_attn_P0', 'L1_attn_P1',
        'L1_ffn_Wg', 'L1_ffn_bg', 'L1_ffn_W1', 'L1_ffn_b1', 'L1_ffn_W2', 'L1_ffn_b2']
_OUTS = [((64, 248, 64), 'float32')]


def kernel(**inputs):
    import numpy as _np
    import concourse.bacc as _bacc
    from concourse import mybir as _mybir
    from concourse.bass_utils import run_bass_kernel_spmd as _run

    nc = _bacc.Bacc("TRN2", target_bir_lowering=False, num_devices=1)
    arrays, args = {}, []
    for name in _INS:
        a = _np.ascontiguousarray(inputs[name])
        arrays[f"in_{name}_dram"] = a
        args.append(nc.dram_tensor(f"in_{name}_dram", a.shape, _mybir.dt.from_np(a.dtype), kind="ExternalInput").ap())
    for i, (shape, dtype) in enumerate(_OUTS):
        dt = _mybir.dt.from_np(_np.dtype(dtype))
        args.append(nc.dram_tensor(f"out_{i}_dram", shape, dt, kind="ExternalOutput").ap())
    audio_tower(nc, *args)
    r = _run(nc, [arrays], core_ids=[0])
    got = tuple(r.results[0][f"out_{i}_dram"] for i in range(len(_OUTS)))
    return got[0]
```

```python
from contextlib import ExitStack

import concourse.bass as bass
from concourse import mybir

F32 = mybir.dt.float32
BF16 = mybir.dt.bfloat16
ALU = mybir.AluOpType
ACT = mybir.ActivationFunctionType
AX = mybir.AxisListType.X

B, L, D, DIN, HID = 64, 248, 64, 128, 256
TL = L // 2
FS = 8
NH = 8
CH, NCH = 16, 16
TOPK = L // 2 - 1
EPS = 1e-5
WARM = 3


class Loop:

    def __init__(self, sem, names, unit=1, before=None):
        self.sem, self.unit, self.P = sem, unit, len(names)
        assert len(set(names)) == len(names)
        self.index = {n: i + 1 for i, n in enumerate(names)}
        self.before = self.P if before is None else before

    def wait(self, e, n, name, back=0):
        e.wait_ge(self.sem, n * (self.P * self.unit) + (self.before + self.index[name] - back * self.P) * self.unit)

    def count(self, e, n):
        e.wait_ge(self.sem, n * (self.P * self.unit))


class Space:

    def __init__(self, nc, ctx, name):
        self.nc, self.ctx, self.name = nc, ctx, name

    def sb(self, name, shape, dtype=F32):
        return self.ctx.enter_context(self.nc.sbuf_tensor(f"{self.name}_{name}", shape, dtype))

    def sem(self, name):
        return self.ctx.enter_context(self.nc.semaphore(f"{self.name}_{name}"))

    def banks(self):
        return [self.ctx.enter_context(self.nc.psum_tensor(f"{self.name}_bank{i}", [128, 512], F32))[:, :] for i in range(8)]


def make_identity(e, ident, sem):
    e.memset(ident[:, :], 0.0).then_inc(sem, 1)
    e.wait_ge(sem, 1)
    e.affine_select(out=ident[:, :], in_=ident[:, :], compare_op=ALU.not_equal, fill=1.0, base=0,
                    pattern=[[-1, 128]], channel_multiplier=1).then_inc(sem, 1)


def norm_center(e, V, n, x, K, t, xn):
    s, q, sq = t
    e.tensor_reduce(s[:, :], x, AX, ALU.add).then_inc(V.sem, 1)
    V.wait(e, n, "mean")
    e.tensor_scalar(s[:, :], s[:, :], 1.0 / D, None, ALU.mult).then_inc(V.sem, 1)
    V.wait(e, n, "meand")
    e.tensor_tensor(xn, x, s[:, :].unsqueeze(2).to_broadcast([TL, K, D]), ALU.subtract).then_inc(V.sem, 1)


def norm_square(e, V, n, K, t, xn):
    s, q, sq = t
    V.wait(e, n, "cen")
    e.tensor_tensor(sq[:, :, :], xn, xn, ALU.mult).then_inc(V.sem, 1)
    V.wait(e, n, "sq")
    e.tensor_reduce(q[:, :], sq[:, :, :], AX, ALU.add).then_inc(V.sem, 1)


def norm_scale(e, V, A, n, K, t, xn):
    s, q, sq = t
    A.wait(e, n, "std")
    e.reciprocal(q[:, :], q[:, :]).then_inc(V.sem, 1)
    V.wait(e, n, "rstd")
    e.tensor_tensor(xn, xn, q[:, :].unsqueeze(2).to_broadcast([TL, K, D]), ALU.mult).then_inc(V.sem, 1)


def norm_vector(e, V, A, n, x, K, t, xn):
    norm_center(e, V, n, x, K, t, xn)
    norm_square(e, V, n, K, t, xn)
    norm_scale(e, V, A, n, K, t, xn)


def settled(e, sem):
    e.nop().then_inc(sem, 1)


NORM_V = ["mean", "meand", "cen", "sq", "ssq", "rstd", "xn"]


def norm_scalar(e, V, A, n, q, eps):
    V.wait(e, n, "ssq")
    e.activation(q[:, :], q[:, :], ACT.Sqrt, bias=eps[0:TL, 0:1], scale=1.0 / D).then_inc(A.sem, 1)


def token_layer(nc, x, filt, W_k, b_k, H0, X0):
    with ExitStack() as ctx:
        S = Space(nc, ctx, "tok")
        ident = S.sb("ident", [128, 128])
        wf, wk, ft, bk = S.sb("wf", [DIN, FS, D]), S.sb("wk", [DIN, FS, D]), S.sb("ft", [DIN, FS]), S.sb("bk", [128, 1])
        xin, xt = S.sb("xin", [128, 8, DIN]), S.sb("xt", [DIN, 4, 256])
        ht, hrow = S.sb("ht", [128, 2 * L]), S.sb("hrow", [TL, 8, D])
        xn, sq, s1, s2, eps = S.sb("xn", [TL, 8, D]), S.sb("sq", [TL, 8, D]), S.sb("s1", [TL, 8]), S.sb("s2", [TL, 8]), S.sb("eps", [128, 1])
        bank = S.banks()
        s_id, s_w, s_wf = S.sem("ident"), S.sem("weights"), S.sem("filtered")
        V, A, T = Loop(S.sem("vector"), ["xt"]), Loop(S.sem("scalar"), ["xt", "relu"]), Loop(S.sem("tensor"), ["xt", "conv"])
        VE, AE, TE = Loop(S.sem("vector_end"), ["row"] + NORM_V), Loop(S.sem("scalar_end"), ["std"]), Loop(S.sem("tensor_end"), ["turn"])
        xin_in = Loop(S.sem("x_in"), ["x"], 16, 0)
        out = Loop(S.sem("out"), ["h"], 32, 0)
        G = B // 4
        with nc.Block() as block:
            @block.gpsimd
            def _(e):
                make_identity(e, ident, s_id)

            @block.sync
            def _(e):
                e.dma_start(wk[:, :, :], W_k.rearrange("(f d) k -> d f k", f=FS)).then_inc(s_w, 16)
                with nc.allow_non_contiguous_dma("a filter of 4 KB, turned"):
                    e.dma_start(ft[:, :], filt.rearrange("f d -> d f")).then_inc(s_w, 16)
                for g in range(2):
                    e.dma_start(bk[D * g:D * g + D, :], b_k.rearrange("(d a) -> d a", a=1)).then_inc(s_w, 16)
                rows = lambda t, n: t[bass.ds(4 * n, 4), :, :, :].rearrange("b p a d -> p b (a d)")

                def load(n):
                    T.wait(e, n, "xt", 1)
                    e.dma_start(xin[:, :, :], x[bass.ds(4 * n, 4), :, :].rearrange("b (c p) d -> p (b c) d", p=128)).then_inc(xin_in.sem, 16)

                def store(n):
                    VE.wait(e, n, "row")
                    e.dma_start(rows(H0, n), hrow[:, :, :].rearrange("p (b a) d -> p b (a d)", a=2)).then_inc(out.sem, 16)
                    VE.wait(e, n, "xn")
                    e.dma_start(rows(X0, n), xn[:, :, :].rearrange("p (b a) d -> p b (a d)", a=2)).then_inc(out.sem, 16)

                load(0)
                with e.Fori(1, G) as n:
                    load(n)
                    store(n - 1)
                store(G - 1)
                out.count(e, G)

            @block.tensor
            def _(e):
                e.wait_ge(s_id, 2)
                e.wait_ge(s_wf, 2)
                e.nop().then_inc(T.sem, T.P)
                e.nop().then_inc(TE.sem, TE.P)

                def end(n):
                    A.wait(e, n, "relu")
                    VE.wait(e, n, "row", 1)
                    for q in range(4):
                        mm = e.transpose(bank[3][0:TL, 128 * q:128 * q + 128], ht[:, TL * q:TL * q + TL], ident[:, :])
                    mm.then_inc(TE.sem, 1)

                def group(n, before):
                    xin_in.wait(e, n, "x")
                    V.wait(e, n, "xt", 1)
                    A.wait(e, n, "xt", 1)
                    for k in range(8):
                        mm = e.transpose(bank[k // 4][:, 128 * (k % 4):128 * (k % 4) + 128], xin[:, k, :], ident[:, :])
                    mm.then_inc(T.sem, 1)
                    if before:
                        end(n - 1)
                    V.wait(e, n, "xt")
                    A.wait(e, n, "xt")
                    for f in range(FS):
                        for g in range(2):
                            mm = e.matmul(bank[2][D * g:D * g + D, 0:2 * L], wf[:, f, :], xt[:, 2 * g:2 * g + 2, f:f + L],
                                          start=(f == 0), stop=(f == FS - 1))
                    mm.then_inc(T.sem, 1)

                group(0, False)
                with e.Fori(1, G) as n:
                    group(n, True)
                end(G - 1)

            @block.scalar
            def _(e):
                e.nop().then_inc(A.sem, A.P)
                e.nop().then_inc(AE.sem, AE.P)
                e.preload_act_table(ACT.Sqrt)

                def group(n, before):
                    T.wait(e, n, "xt")
                    T.wait(e, n, "conv", 1)
                    e.activation(xt[:, 2:4, :], bank[1].rearrange("p (a l) -> p a l", a=2), ACT.Copy).then_inc(A.sem, 1)
                    if before:
                        norm_scalar(e, VE, AE, n - 1, s2, eps)
                    T.wait(e, n, "conv")
                    TE.wait(e, n, "turn", 1)
                    e.activation(ht[:, :], bank[2][:, 0:2 * L], ACT.Relu, bias=bk[:, 0:1]).then_inc(A.sem, 1)

                group(0, False)
                with e.Fori(1, G) as n:
                    group(n, True)
                norm_scalar(e, VE, AE, G - 1, s2, eps)

            @block.vector
            def _(e):
                e.memset(eps[:, :], EPS).then_inc(s_wf, 1)
                e.wait_ge(s_w, 64)
                e.tensor_tensor(wf[:, :, :], wk[:, :, :], ft[:, :].unsqueeze(2).to_broadcast([DIN, FS, D]), ALU.mult).then_inc(s_wf, 1)
                e.nop().then_inc(V.sem, V.P)
                e.nop().then_inc(VE.sem, VE.P)

                def end(n):
                    TE.wait(e, n, "turn")
                    out.count(e, n)
                    e.tensor_copy(hrow[:, :, :].rearrange("p (g q) d -> p g q d", g=2),
                                  bank[3][0:TL, :].rearrange("p (q g d) -> p g q d", q=4, g=2)).then_inc(VE.sem, 1)
                    VE.wait(e, n, "row")
                    norm_vector(e, VE, AE, n, hrow[:, :, :], 8, (s1, s2, sq), xn[:, :, :])

                def group(n, before):
                    T.wait(e, n, "xt")
                    T.wait(e, n, "conv", 1)
                    e.tensor_copy(xt[:, 0:2, :], bank[0].rearrange("p (a l) -> p a l", a=2)).then_inc(V.sem, 1)
                    if before:
                        end(n - 1)

                group(0, False)
                with e.Fori(1, G) as n:
                    group(n, True)
                end(G - 1)


def attention_layer(nc, Wqk, Wv, Wpos, bpos, Wproj, bproj, gating, H0, X0, H1):
    with ExitStack() as ctx:
        S = Space(nc, ctx, "att")
        ident = S.sb("ident", [128, 128])
        w_raw = S.sb("w_raw", [128, 3, D])
        wT = S.sb("wT", [D + 1, 4, D])
        prm = S.sb("prm", [TL, 40])
        hm = S.sb("hm", [D, NH])
        dist, dist2, cst = S.sb("dist", [TL, 2, L]), S.sb("dist2", [TL, 2, L]), S.sb("cst", [TL, NH])
        pe, pst = S.sb("pe", [TL, L]), S.sb("pst", [TL, 4])
        rt = S.sb("rt", [TL, NH, 2, L])
        omg, sgg = S.sb("omg", [TL, 2, 2, 4]), S.sb("sgg", [TL, 2, 2, 4])
        ht, xn = S.sb("ht", [TL, 2, D]), S.sb("xn", [TL, 2, D])
        xT = S.sb("xT", [D, L])
        qn, qa, ka = S.sb("qn", [128, L]), S.sb("qa", [128, L]), S.sb("ka", [128, NH, L])
        va = S.sb("va", [TL, 2, NH, 32])
        mx = S.sb("mx", [TL, 2, NH])
        ex = S.sb("ex", [TL, NH, 2, L])
        evs, rvs = S.sb("evs", [128, 2 * L]), S.sb("rvs", [128, 2 * L])
        rz, num, rv = S.sb("rz", [TL, 16]), S.sb("num", [TL, 16, 9]), S.sb("rv", [TL, 16, 9])
        at, aT, h1 = S.sb("at", [TL, 2, D]), S.sb("aT", [D + 1, L]), S.sb("h1", [TL, 2, D])
        bank = S.banks()
        s_id, s_w, s_v, s_t, s_a, s_own = S.sem("ident"), S.sem("weights"), S.sem("set_v"), S.sem("set_t"), S.sem("set_a"), S.sem("settled")
        s_own_sp = S.sem("settled_sp")
        V = Loop(S.sem("vector"), [f"mx{i}" for i in range(8)] + ["nm", "xT", "q", "k", "evs", "v"])
        VE = Loop(S.sem("vector_end"), ["rz", "rzg", "num", "rv", "sum", "rd", "at0", "at1", "aT", "h1"])
        A = Loop(S.sem("scalar"), ["rvs"] + [f"e{h}" for h in range(NH)] + ["qc"])
        T = Loop(S.sem("tensor"), [f"s{i}" for i in range(8)] + ["rv", "nm"] + [f"st{h}" for h in range(NH)] +
                 ["xT", "qk", "ev", "v"])
        TE = Loop(S.sem("tensor_end"), ["te", "tr", "aT", "pr"])
        xin = Loop(S.sem("x_in"), ["x"], 16, 0)
        s_x0, s_t0, s_v0, s_a0 = S.sem("first_x_in"), S.sem("first_tensor"), S.sem("first_vector"), S.sem("first_scalar")
        hin = Loop(S.sem("h_in"), ["h"], 16, 0)
        out = Loop(S.sem("out"), ["h"], 16, 0)
        with nc.Block() as block:
            @block.gpsimd
            def _(e):
                make_identity(e, ident, s_id)
                e.wait_ge(s_id, 2)
                e.memset(hm[:, :], 1.0).then_inc(s_id, 1)
                e.wait_ge(s_id, 3)
                e.memset(ka[D:, :, :], 1.0).then_inc(s_id, 1)
                e.wait_ge(s_id, 4)
                e.memset(va[:, :, :, :], 0.0).then_inc(s_id, 1)
                e.wait_ge(s_id, 5)
                e.affine_select(out=hm[:, :], in_=hm[:, :], compare_op=ALU.is_ge, fill=0.0, base=0,
                                pattern=[[-8, NH]], channel_multiplier=1).then_inc(s_id, 1)
                e.wait_ge(s_id, 6)
                e.affine_select(out=hm[:, :], in_=hm[:, :], compare_op=ALU.is_ge, fill=0.0, base=7,
                                pattern=[[8, NH]], channel_multiplier=-1).then_inc(s_id, 1)
                e.wait_ge(s_id, 7)
                e.affine_select(out=ka[D:, :, :], in_=ka[D:, :, :], compare_op=ALU.is_equal, fill=0.0, base=0,
                                pattern=[[-1, NH], [0, L]], channel_multiplier=1).then_inc(s_id, 1)
                e.wait_ge(s_id, 8)
                e.iota(dist[:, :, :], pattern=[[-TL, 2], [1, L]], base=0, channel_multiplier=-1,
                       allow_small_or_imprecise_dtypes=True).then_inc(s_id, 1)
                e.wait_ge(s_id, 9)
                e.memset(va[:, :, :, 8:9], 1.0).then_inc(s_id, 1)
                e.wait_ge(s_id, 10)
                e.memset(aT[D:D + 1, :], 1.0).then_inc(s_id, 1)

            @block.sync
            def _(e):
                e.dma_start(w_raw[:, 0, :], Wqk).then_inc(s_w, 16)
                e.dma_start(w_raw[0:D, 1, :], Wv).then_inc(s_w, 16)
                e.dma_start(w_raw[0:D, 2, :], Wproj).then_inc(s_w, 16)
                e.dma_start(wT[D:D + 1, 3, :], bproj.rearrange("(a n) -> a n", a=1)).then_inc(s_w, 16)
                e.dma_start(prm[:, 0:24], Wpos.rearrange("h c -> (h c)").partition_broadcast(TL)).then_inc(s_w, 16)
                e.dma_start(prm[:, 24:32], bpos.partition_broadcast(TL)).then_inc(s_w, 16)
                e.dma_start(prm[:, 32:40], gating.partition_broadcast(TL)).then_inc(s_w, 16)
                row = lambda t, n: t[bass.ds(n, 1), :, :, :].rearrange("b p a d -> p (b a) d")
                e.dma_start(xn[:, :, :], X0[0]).then_inc(s_x0, 16)
                e.wait_ge(s_t0, 1)

                def store(n):
                    VE.wait(e, n, "h1")
                    settled(e, s_own_sp)
                    e.dma_start(row(H1, n), h1[:, :, :]).then_inc(out.sem, 16)

                def batch(n, ahead, before):
                    if ahead:
                        T.wait(e, n, "xT", 1)
                        settled(e, s_own_sp)
                        e.dma_start(xn[:, :, :], row(X0, n + 1)).then_inc(xin.sem, 16)
                    if before:
                        store(n - 1)
                    e.dma_start(ht[:, :, :], row(H0, n)).then_inc(hin.sem, 16)

                batch(0, True, False)
                with e.Fori(1, B - 1) as n:
                    batch(n, True, True)
                batch(B - 1, False, True)
                store(B - 1)
                out.count(e, B)

            @block.tensor
            def _(e):
                e.wait_ge(s_w, 16 * 7)
                e.wait_ge(s_id, 2)
                e.transpose(bank[0][0:D, 0:128], w_raw[:, 0, :], ident[:, :]).then_inc(s_t, 1)
                for i in (1, 2):
                    e.transpose(bank[0][0:D, 64 + 64 * i:128 + 64 * i], w_raw[0:D, i, :], ident[0:D, 0:D]).then_inc(s_t, 1)
                for k in range(16):
                    e.wait_ge(s_v, 9 + 6 * k)
                    for mh in range(2):
                        e.transpose(bank[1][0:TL, 128 * mh:128 * mh + TL], pe[:, TL * mh:TL * mh + TL], ident[0:TL, 0:TL]).then_inc(s_t, 1)
                e.wait_ge(s_v, 101)
                e.nop().then_inc(T.sem, T.P)
                e.nop().then_inc(TE.sem, TE.P)

                def turn_x():
                    for a in range(2):
                        mm = e.transpose(bank[5][0:D, TL * a:TL * a + TL], xn[:, a, :], ident[0:TL, 0:TL])
                    return mm

                def queries_keys():
                    for w in range(2):
                        mm = e.matmul(bank[3][0:D, L * w:L * w + L], wT[0:D, w, :], xT[:, :], start=True, stop=True)
                    return mm

                def values():
                    for a in range(2):
                        mm = e.matmul(bank[4][0:TL, D * a:D * a + D], xT[:, TL * a:TL * a + TL], wT[0:D, 2, :], start=True, stop=True)
                    return mm

                def weighted(wts, bk, exps):
                    for g in range(2):
                        for mh in range(2):
                            for j in range(4):
                                if exps is not None and mh == 0:
                                    A.wait(e, exps, f"e{4 * g + j}")
                                mm = e.matmul(bk[32 * j:32 * j + 32, L * g:L * g + L], va[:, mh, 4 * g + j, :], wts[:, 4 * g + j, mh, :],
                                              start=(mh == 0), stop=(mh == 1))
                    return mm

                e.wait_ge(s_x0, 16)
                turn_x().then_inc(s_t0, 1)
                e.wait_ge(s_v0, 1)
                queries_keys().then_inc(s_t0, 1)
                values().then_inc(s_t0, 1)
                e.wait_ge(s_v0, 5)
                e.wait_ge(s_a0, 1)

                def end_turned(n):
                    for src, bk in ((evs, bank[0]), (rvs, bank[1])):
                        if src is rvs:
                            A.wait(e, n, "rvs")
                        else:
                            V.wait(e, n, "evs")
                        for g in range(2):
                            for a in range(2):
                                mm = e.transpose(bk[0:TL, 128 * (2 * g + a):128 * (2 * g + a) + 128], src[:, L * g + TL * a:L * g + TL * a + TL], ident[:, :])
                        mm.then_inc(TE.sem, 1)

                def end_attended(n):
                    VE.wait(e, n, "at1")
                    settled(e, s_own)
                    for a in range(2):
                        mm = e.transpose(bank[2][0:D, 128 + TL * a:128 + TL * a + TL], at[:, a, :], ident[0:TL, 0:TL])
                    mm.then_inc(TE.sem, 1)

                def end_projected(n):
                    VE.wait(e, n, "aT")
                    for a in range(2):
                        mm = e.matmul(bank[2][0:TL, D * a:D * a + D], aT[:, TL * a:TL * a + TL], wT[:, 3, :], start=True, stop=True)
                    mm.then_inc(TE.sem, 1)

                def batch(n, ahead, before):
                    V.wait(e, n, "v", 1)
                    for i in range(8):
                        a, hp = i // 4, i % 4
                        if i >= 2:
                            V.wait(e, n, f"mx{i - 2}")
                        e.matmul(bank[3 + i % 2][0:TL, 0:2 * L], qn[:, TL * a:TL * a + TL], ka[:, 2 * hp:2 * hp + 2, :],
                                 start=True, stop=True).then_inc(T.sem, 1)
                        if before and i == 1:
                            end_turned(n - 1)
                        if before and i == 4:
                            end_attended(n - 1)
                        if before and i == 6:
                            end_projected(n - 1)
                    weighted(rt, bank[7], None).then_inc(T.sem, 1)
                    V.wait(e, n, "mx7")
                    for a in range(2):
                        mm = e.matmul(bank[5][D:D + NH, TL * a:TL * a + TL], mx[:, a, :], ident[0:TL, 0:TL], start=True, stop=True)
                    mm.then_inc(T.sem, 1)
                    A.wait(e, n, "qc", 1)
                    V.wait(e, n, "nm")
                    for h in range(NH):
                        if h >= 2:
                            A.wait(e, n, f"e{h - 2}")
                        for mh in range(2):
                            mm = e.matmul(bank[3 + h % 2][0:TL, L * mh:L * mh + L], ka[:, h, TL * mh:TL * mh + TL], qa[:, :],
                                          start=True, stop=True)
                        mm.then_inc(T.sem, 1)
                    if ahead:
                        xin.wait(e, n, "x")
                        settled(e, s_own)
                        turn_x().then_inc(T.sem, 1)
                        A.wait(e, n, "e6")
                        V.wait(e, n, "xT")
                        settled(e, s_own)
                        queries_keys().then_inc(T.sem, 1)
                    else:
                        T.wait(e, n, "st7")
                        e.nop().then_inc(T.sem, 2)
                    weighted(ex, bank[6], n).then_inc(T.sem, 1)
                    if ahead:
                        values().then_inc(T.sem, 1)
                    else:
                        T.wait(e, n, "ev")
                        e.nop().then_inc(T.sem, 1)

                batch(0, True, False)
                with e.Fori(1, B - 1) as n:
                    batch(n, True, True)
                batch(B - 1, False, True)
                end_turned(B - 1)
                end_attended(B - 1)
                end_projected(B - 1)

            @block.scalar
            def _(e):
                e.nop().then_inc(A.sem, A.P)
                e.wait_ge(s_w, 16 * 7)
                e.activation(prm[:, 32:40], prm[:, 32:40], ACT.Sigmoid).then_inc(s_a, 1)
                for k in range(16):
                    e.wait_ge(s_v, 7 + 6 * k)
                    e.activation(pe[:, :], pe[:, :], ACT.Exp, bias=pst[:, 1:2], accum_out=pst[:, 2:3]).then_inc(s_a, 1)
                e.wait_ge(s_v0, 2)
                e.activation(qa[0:D, :], qn[0:D, :], ACT.Copy).then_inc(s_a0, 1)

                def batch(n, ahead, before):
                    TE.wait(e, n, "tr", 1)
                    T.wait(e, n, "rv")
                    e.activation(rvs[:, :], bank[7][:, 0:2 * L], ACT.Copy).then_inc(A.sem, 1)
                    for h in range(NH):
                        T.wait(e, n, f"st{h}")
                        e.activation(ex[:, h, :, :], bank[3 + h % 2][0:TL, 0:2 * L].rearrange("p (m n) -> p m n", m=2), ACT.Exp).then_inc(A.sem, 1)
                    if ahead:
                        V.wait(e, n, "q")
                        e.activation(qa[0:D, :], qn[0:D, :], ACT.Copy).then_inc(A.sem, 1)

                batch(0, True, False)
                with e.Fori(1, B - 1) as n:
                    batch(n, True, True)
                batch(B - 1, False, True)

            @block.vector
            def _(e):
                e.nop().then_inc(V.sem, V.P)
                e.nop().then_inc(VE.sem, VE.P)
                for t in (qn, qa):
                    ins = e.memset(t[D:, :], 0.0)
                ins.then_inc(s_v, 1)
                e.wait_ge(s_t, 3)
                e.wait_ge(s_w, 16 * 7)
                e.tensor_copy(wT[0:D, :, :].rearrange("p a b -> p (a b)"), bank[0][0:D, 0:256]).then_inc(s_v, 1)
                e.scalar_tensor_tensor(out=cst[:, :], in0=prm[:, 1:24:3], scalar=0.0, in1=prm[:, 24:32],
                                       op0=ALU.mult, op1=ALU.add).then_inc(s_v, 1)
                e.wait_ge(s_id, 11)
                e.tensor_tensor(dist2[:, :, :], dist[:, :, :], dist[:, :, :], ALU.mult).then_inc(s_v, 1)
                e.wait_ge(s_v, 4)
                for k in range(16):
                    h, nh = k // 2, k % 2
                    v0 = 4 + 6 * k
                    if k:
                        e.wait_ge(s_v, v0)
                    e.tensor_scalar(pe[:, :], dist2[:, nh, :], prm[:, 3 * h + 2:3 * h + 3], cst[:, h:h + 1], ALU.mult, ALU.add).then_inc(s_v, 1)
                    e.wait_ge(s_v, v0 + 1)
                    e.scalar_tensor_tensor(out=pe[:, :], in0=dist[:, nh, :], scalar=prm[:, 3 * h:3 * h + 1], in1=pe[:, :],
                                           op0=ALU.mult, op1=ALU.add).then_inc(s_v, 1)
                    e.wait_ge(s_v, v0 + 2)
                    e.tensor_reduce(pst[:, 1:2], pe[:, :], AX, ALU.max, negate=True).then_inc(s_v, 1)
                    e.wait_ge(s_a, 2 + k)
                    e.reciprocal(pst[:, 3:4], pst[:, 2:3]).then_inc(s_v, 1)
                    e.wait_ge(s_v, v0 + 4)
                    e.tensor_scalar(pe[:, :], pe[:, :], pst[:, 3:4], None, ALU.mult).then_inc(s_v, 1)
                    e.wait_ge(s_t, 3 + 2 * k + 2)
                    e.tensor_copy(rt[:, h, :, TL * nh:TL * nh + TL], bank[1][0:TL, 0:256].rearrange("p (m n) -> p m n", m=2)[:, :, 0:TL]).then_inc(s_v, 1)
                for g in range(2):
                    sg = prm[:, 32 + 4 * g:36 + 4 * g].unsqueeze(1).to_broadcast([TL, 2, 4])
                    e.tensor_copy(sgg[:, g, :, :], sg)
                    ins = e.tensor_scalar(omg[:, g, :, :], sg, -1.0, 1.0, ALU.mult, ALU.add)
                ins.then_inc(s_v, 1)
                e.wait_ge(s_v, 101)

                def turned_x():
                    return e.tensor_copy(xT[:, :], bank[5][0:D, 0:L])

                def queries():
                    return e.tensor_scalar(qn[0:D, :], bank[3][0:D, 0:L], float(NH) ** -0.5, None, ALU.mult)

                def keys():
                    return e.tensor_tensor(ka[0:D, :, :], bank[3][0:D, L:2 * L].unsqueeze(1).to_broadcast([D, NH, L]),
                                           hm[:, :].unsqueeze(2).to_broadcast([D, NH, L]), ALU.mult)

                def values():
                    return e.tensor_copy(va[:, :, :, 0:8], bank[4][0:TL, 0:128].rearrange("p (a h d) -> p a h d", a=2, h=NH))

                e.wait_ge(s_t0, 1)
                turned_x().then_inc(s_v0, 1)
                e.wait_ge(s_t0, 2)
                queries().then_inc(s_v0, 1)
                keys().then_inc(s_v0, 1)
                e.wait_ge(s_t0, 3)
                values().then_inc(s_v0, 2)

                def end_weighted(n):
                    TE.wait(e, n, "tr")
                    ev = bank[0][0:TL, :].rearrange("p (q c) -> p q c", c=32)
                    rvt = bank[1][0:TL, :].rearrange("p (q c) -> p q c", c=32)
                    flat = lambda t: t[:, :, :, :].rearrange("p g a j -> p (g a j)")
                    e.reciprocal(rz[:, :].unsqueeze(2), ev[:, :, 8:9]).then_inc(VE.sem, 1)
                    VE.wait(e, n, "rz")
                    e.tensor_tensor(rz[:, :], rz[:, :], flat(omg), ALU.mult).then_inc(VE.sem, 1)
                    VE.wait(e, n, "rzg")
                    e.tensor_tensor(num[:, :, :], ev[:, :, 0:9], rz[:, :].unsqueeze(2).to_broadcast([TL, 16, 9]), ALU.mult).then_inc(VE.sem, 1)
                    e.tensor_tensor(rv[:, :, :], rvt[:, :, 0:9], flat(sgg).unsqueeze(2).to_broadcast([TL, 16, 9]), ALU.mult).then_inc(VE.sem, 1)
                    VE.wait(e, n, "rv")
                    e.tensor_tensor(num[:, :, :], num[:, :, :], rv[:, :, :], ALU.add).then_inc(VE.sem, 1)
                    VE.wait(e, n, "sum")
                    e.reciprocal(rz[:, :].unsqueeze(2), num[:, :, 8:9]).then_inc(VE.sem, 1)
                    VE.wait(e, n, "rd")
                    for a in range(2):
                        v = lambda t: t.rearrange("p (g a j) c -> p a g j c", g=2, a=2)[:, a]
                        e.tensor_tensor(at[:, a, :].rearrange("p (g j c) -> p g j c", g=2, j=4), v(num[:, :, 0:8]),
                                        v(rz[:, :].unsqueeze(2).to_broadcast([TL, 16, 8])), ALU.mult).then_inc(VE.sem, 1)

                def end_attended(n):
                    TE.wait(e, n, "aT")
                    e.tensor_copy(aT[0:D, :], bank[2][0:D, 128:128 + L]).then_inc(VE.sem, 1)

                def end_projected(n):
                    TE.wait(e, n, "pr")
                    hin.wait(e, n, "h")
                    out.count(e, n)
                    e.tensor_tensor(h1[:, :, :], bank[2][0:TL, 0:128].rearrange("p (a d) -> p a d", a=2), ht[:, :, :], ALU.add).then_inc(VE.sem, 1)

                def batch(n, ahead, before):
                    for i in range(8):
                        T.wait(e, n, f"s{i}")
                        e.tensor_reduce(mx[:, i // 4, 2 * (i % 4):2 * (i % 4) + 2],
                                        bank[3 + i % 2][0:TL, 0:2 * L].rearrange("p (h m) -> p h m", h=2), AX, ALU.max).then_inc(V.sem, 1)
                        if before and i == 1:
                            end_weighted(n - 1)
                        if before and i == 4:
                            end_attended(n - 1)
                        if before and i == 6:
                            end_projected(n - 1)
                    T.wait(e, n, "nm")
                    e.tensor_scalar(qa[D:D + NH, :], bank[5][D:D + NH, 0:L], -1.0, None, ALU.mult).then_inc(V.sem, 1)
                    if ahead:
                        T.wait(e, n, "xT")
                        turned_x().then_inc(V.sem, 1)
                        T.wait(e, n, "qk")
                        queries().then_inc(V.sem, 1)
                        keys().then_inc(V.sem, 1)
                    else:
                        e.engine_nop().then_inc(V.sem, 3)
                    T.wait(e, n, "ev")
                    e.tensor_copy(evs[:, :], bank[6][:, 0:2 * L]).then_inc(V.sem, 1)
                    if ahead:
                        T.wait(e, n, "v")
                        values().then_inc(V.sem, 1)
                    else:
                        e.engine_nop().then_inc(V.sem, 1)

                batch(0, True, False)
                with e.Fori(1, B - 1) as n:
                    batch(n, True, True)
                batch(B - 1, False, True)
                end_weighted(B - 1)
                end_attended(B - 1)
                end_projected(B - 1)


def ffn_layer(nc, wr, br, w1, b1, w2, b2, H1, H2, XN, WD, SW):
    G = B // 4
    with ExitStack() as ctx:
        S = Space(nc, ctx, "ffn")
        ident = S.sb("ident", [128, 128])
        eps = S.sb("eps", [128, 1])
        wrb, brb = S.sb("wrb", [TL, D]), S.sb("brb", [TL, 1])
        w1s, w2s, b1s, b2s = S.sb("w1s", [D, HID]), S.sb("w2s", [128, 2, D]), S.sb("b1s", [128, 2]), S.sb("b2s", [128, 1])
        ht, xn, sq = S.sb("ht", [TL, 8, D]), S.sb("xn", [TL, 8, D]), S.sb("sq", [TL, 8, D])
        s1, s2 = S.sb("s1", [TL, 8]), S.sb("s2", [TL, 8])
        wt = S.sb("wt", [TL, 128])
        wtt = S.sb("wtt", [128, TL])
        wv, wk, m8, ge, eq, pre = S.sb("wv", [B, L]), S.sb("wk", [B, L]), S.sb("m8", [B, 8]), S.sb("ge", [B, L]), S.sb("eq", [B, L]), S.sb("pre", [B, L])
        cnt = S.sb("cnt", [B, 2])
        swp, sw = S.sb("swp", [128, TL]), S.sb("sw", [TL, 128])
        xT = S.sb("xT", [D, 4 * L])
        u, t2, gg = S.sb("u", [128, 4, 2 * L]), S.sb("t2", [128, 4, 2 * L]), S.sb("gg", [128, 4, 2 * L])
        yT, h2, hx = S.sb("yT", [128, 2 * L]), S.sb("h2", [TL, 8, D]), S.sb("hx", [TL, 2, 8, D])
        bank = S.banks()
        s_id, s_w, s_own, s_own_sp = S.sem("ident"), S.sem("weights"), S.sem("settled"), S.sem("settled_sp")
        bc = lambda a, k: a.unsqueeze(2).to_broadcast([TL, k, D])

        with nc.Block() as block:
            V = Loop(S.sem("vector"), NORM_V + ["xr", "w"])
            A = Loop(S.sem("scalar"), ["std"])
            hin, out = Loop(S.sem("h_in"), ["h"], 16, 0), Loop(S.sem("out"), ["x"], 16, 0)
            s_v = S.sem("set")

            @block.gpsimd
            def _(e):
                make_identity(e, ident, s_id)

            @block.sync
            def _(e):
                e.dma_start(wrb[:, :], wr.rearrange("d a -> (d a)").partition_broadcast(TL)).then_inc(s_w, 16)
                e.dma_start(brb[:, :], br.partition_broadcast(TL)).then_inc(s_w, 16)
                e.dma_start(w1s[:, :], w1).then_inc(s_w, 16)
                e.dma_start(w2s[:, :, :], w2.rearrange("(a p) d -> p a d", a=2)).then_inc(s_w, 16)
                with nc.allow_non_contiguous_dma("biases, one an element"):
                    e.dma_start(b1s[:, :], b1.rearrange("(a p) -> p a", a=2)).then_inc(s_w, 16)
                for g in range(2):
                    e.dma_start(b2s[D * g:D * g + D, :], b2.rearrange("(d a) -> d a", a=1)).then_inc(s_w, 16)
                with e.Fori(0, G) as n:
                    V.wait(e, n, "cen", 1)
                    e.dma_start(ht[:, :, :].rearrange("p (b a) d -> p b (a d)", a=2), H1[bass.ds(4 * n, 4), :, :, :].rearrange("b p a d -> p b (a d)")).then_inc(hin.sem, 16)
                    V.wait(e, n, "xn")
                    e.dma_start(XN[bass.ds(4 * n, 4), :, :, :].rearrange("b p a d -> p b (a d)"), xn[:, :, :].rearrange("p (b a) d -> p b (a d)", a=2)).then_inc(out.sem, 16)
                out.count(e, G)

            @block.scalar
            def _(e):
                e.nop().then_inc(A.sem, A.P)
                e.preload_act_table(ACT.Sqrt)
                with e.Fori(0, G) as n:
                    norm_scalar(e, V, A, n, s2, eps)

            @block.vector
            def _(e):
                e.memset(eps[:, :], EPS).then_inc(s_v, 1)
                e.wait_ge(s_v, 1)
                e.nop().then_inc(V.sem, V.P)
                e.wait_ge(s_w, 16 * 7)
                with e.Fori(0, G) as n:
                    hin.wait(e, n, "h")
                    out.count(e, n)
                    V.wait(e, n, "w", 1)
                    norm_vector(e, V, A, n, ht[:, :, :], 8, (s1, s2, sq), xn[:, :, :])
                    V.wait(e, n, "xn")
                    e.tensor_tensor(sq[:, :, :], xn[:, :, :], wrb[:, :].unsqueeze(1).to_broadcast([TL, 8, D]), ALU.mult).then_inc(V.sem, 1)
                    V.wait(e, n, "xr")
                    e.tensor_reduce(wt[:, bass.ds(8 * n, 8)], sq[:, :, :], AX, ALU.add).then_inc(V.sem, 1)

        with nc.Block() as block:
            s_c, s_d, s_t = S.sem("choice"), S.sem("choice_dma"), S.sem("choice_turned")

            @block.tensor
            def _(e):
                e.wait_ge(s_c, 1)
                e.transpose(bank[0][:, 0:TL], wt[:, :], ident[0:TL, 0:TL]).then_inc(s_t, 1)
                e.wait_ge(s_d, 64)
                e.transpose(bank[1][0:TL, 0:128], swp[:, :], ident[:, :]).then_inc(s_t, 1)

            @block.sync
            def _(e):
                e.wait_ge(s_c, 2)
                e.dma_start(WD.rearrange("b (a t) -> (b a) t", a=2), wtt[:, :]).then_inc(s_d, 16)
                e.wait_ge(s_d, 16)
                e.dma_start(wv[:, :], WD).then_inc(s_d, 16)
                e.wait_ge(s_c, 3 + 2 * 15 + 9)
                e.dma_start(SW, pre[:, :]).then_inc(s_d, 16)
                e.wait_ge(s_d, 48)
                e.dma_start(swp[:, :], SW.rearrange("b (a t) -> (b a) t", a=2)).then_inc(s_d, 16)

            @block.vector
            def _(e):
                at = [0]

                def done(ins):
                    ins.then_inc(s_c, 1)
                    at[0] += 1
                    e.wait_ge(s_c, at[0])

                done(e.tensor_scalar(wt[:, :], wt[:, :], brb[:, 0:1], None, ALU.add))
                e.wait_ge(s_t, 1)
                done(e.tensor_copy(wtt[:, :], bank[0][:, 0:TL]))
                e.wait_ge(s_d, 32)
                done(e.tensor_copy(wk[:, :], wv[:, :]))
                rounds, last = divmod(TOPK - 1, 8)
                assert rounds == 15
                for _ in range(rounds):
                    done(e.max(m8[:, :], wk[:, :]))
                    done(e.match_replace(wk[:, :], m8[:, :], wk[:, :], -3.0e38))
                done(e.max(m8[:, :], wk[:, :]))
                thr = m8[:, last:last + 1]
                done(e.tensor_scalar(ge[:, :], wv[:, :], thr, None, ALU.is_gt))
                done(e.tensor_reduce(cnt[:, 0:1], ge[:, :], AX, ALU.add))
                done(e.tensor_scalar(cnt[:, 1:2], cnt[:, 0:1], -1.0, float(TOPK), ALU.mult, ALU.add))
                done(e.tensor_scalar(eq[:, :], wv[:, :], thr, None, ALU.is_equal))
                done(e.tensor_tensor_scan(pre[:, :], eq[:, :], eq[:, :], 0.0, ALU.add, ALU.bypass))
                done(e.scalar_tensor_tensor(out=eq[:, :], in0=pre[:, :], scalar=cnt[:, 1:2], in1=eq[:, :], op0=ALU.is_le, op1=ALU.mult))
                done(e.tensor_tensor(ge[:, :], ge[:, :], eq[:, :], ALU.add))
                done(e.tensor_tensor(pre[:, :], ge[:, :], wv[:, :], ALU.mult))
                e.wait_ge(s_t, 2)
                done(e.tensor_copy(sw[:, :], bank[1][0:TL, 0:128]))

        with nc.Block() as block:
            VS, AS, TS = Loop(S.sem("vector2_start"), ["xT0"]), Loop(S.sem("scalar2_start"), ["xT1"]), Loop(S.sem("tensor2_start"), ["xT"] + [f"h{i}" for i in range(4)])
            V = Loop(S.sem("vector2"), ["hx", "uu0", "uv0", "uw0", "uu1", "uv1", "uw1", "gg0", "uu2", "uv2", "uw2", "gg1", "uu3", "uv3", "uw3", "gg2", "gg3"])
            A = Loop(S.sem("scalar2"), ["u0", "u1", "th0", "u2", "th1", "u3", "th2", "th3"])
            VE, AE, TE = Loop(S.sem("vector2_end"), ["yw", "h2"]), Loop(S.sem("scalar2_end"), ["yT"]), Loop(S.sem("tensor2_end"), ["y", "turn"])
            hin, xin = Loop(S.sem("h_in2"), ["h"], 16, 0), Loop(S.sem("x_in2"), ["x"], 16, 0)
            out = Loop(S.sem("out2"), ["h"], 16, 0)
            s_v = S.sem("set2")
            grp = lambda t: t.rearrange("p (b a) d -> p b (a d)", a=2)
            dr = lambda t, n: t[bass.ds(4 * n, 4), :, :, :].rearrange("b p a d -> p b (a d)")

            @block.sync
            def _(e):
                def load(n):
                    V.wait(e, n, "hx", 1)
                    settled(e, s_own_sp)
                    TS.wait(e, n, "xT", 1)
                    settled(e, s_own_sp)
                    e.dma_start(grp(xn[:, :, :]), dr(XN, n)).then_inc(xin.sem, 16)
                    e.dma_start(grp(ht[:, :, :]), dr(H1, n)).then_inc(hin.sem, 16)

                def store(n):
                    VE.wait(e, n, "h2")
                    settled(e, s_own_sp)
                    e.dma_start(dr(H2, n), grp(h2[:, :, :])).then_inc(out.sem, 16)

                load(0)
                load(1)
                with e.Fori(2, G) as n:
                    load(n)
                    store(n - 2)
                store(G - 2)
                store(G - 1)
                out.count(e, G)

            @block.tensor
            def _(e):
                e.nop().then_inc(TS.sem, TS.P)
                e.wait_ge(s_v, 1)

                def start(n):
                    xin.wait(e, n, "x")
                    settled(e, s_own)
                    for k in range(8):
                        mm = e.transpose(bank[k // 4][0:D, TL * (k % 4):TL * (k % 4) + TL], xn[:, k, :], ident[0:TL, 0:TL])
                    mm.then_inc(TS.sem, 1)
                    VS.wait(e, n, "xT0")
                    AS.wait(e, n, "xT1")

                def hidden(n, half):
                    for i in (2 * half, 2 * half + 1):
                        q, a = i // 2, i % 2
                        A.wait(e, n, f"u{i}", 1)
                        e.matmul(bank[2 + i][:, 0:2 * L], w1s[:, 128 * a:128 * a + 128], xT[:, 2 * L * q:2 * L * q + 2 * L],
                                 start=True, stop=True).then_inc(TS.sem, 1)

                def output(n):
                    V.wait(e, n, "gg3")
                    for a in range(2):
                        for q in range(2):
                            mm = e.matmul(bank[6][D * q:D * q + D, 0:2 * L], w2s[:, a, :], gg[:, 2 * q + a, :], start=(a == 0), stop=(a == 1))
                    mm.then_inc(TE.sem, 1)

                def turn(n):
                    AE.wait(e, n, "yT")
                    VE.wait(e, n, "yw", 1)
                    for k in range(4):
                        mm = e.transpose(bank[7][0:TL, 128 * k:128 * k + 128], yT[:, TL * k:TL * k + TL], ident[:, :])
                    mm.then_inc(TE.sem, 1)

                e.nop().then_inc(TE.sem, TE.P)
                start(0)
                hidden(0, 0)
                hidden(0, 1)
                with e.Fori(1, G) as n:
                    start(n)
                    hidden(n, 0)
                    output(n - 1)
                    hidden(n, 1)
                    turn(n - 1)
                output(G - 1)
                turn(G - 1)

            @block.scalar
            def _(e):
                e.nop().then_inc(A.sem, A.P)
                e.nop().then_inc(AS.sem, AS.P)
                e.nop().then_inc(AE.sem, AE.P)
                e.preload_act_table(ACT.Tanh)

                def start(n):
                    TS.wait(e, n, "xT")
                    e.activation(xT[:, 2 * L:], bank[1][0:D, 0:2 * L], ACT.Copy).then_inc(AS.sem, 1)

                def end(n):
                    TE.wait(e, n, "y")
                    e.activation(yT[:, :], bank[6][:, 0:2 * L], ACT.Identity, bias=b2s[:, 0:1]).then_inc(AE.sem, 1)

                def hidden(n, i):
                    TS.wait(e, n, f"h{i}")
                    V.wait(e, n, f"gg{i}", 1)
                    e.activation(u[:, i, :], bank[2 + i][:, 0:2 * L], ACT.Identity, bias=b1s[:, i % 2:i % 2 + 1]).then_inc(A.sem, 1)

                def tanh(n, i):
                    V.wait(e, n, f"uw{i}")
                    e.activation(t2[:, i, :], t2[:, i, :], ACT.Tanh, scale=0.7978845608028654).then_inc(A.sem, 1)

                def group(n, before, ahead):
                    hidden(n, 0)
                    hidden(n, 1)
                    tanh(n, 0)
                    hidden(n, 2)
                    if before is not None:
                        end(before)
                    tanh(n, 1)
                    hidden(n, 3)
                    tanh(n, 2)
                    if ahead is not None:
                        start(ahead)
                    tanh(n, 3)

                start(0)
                group(0, None, 1)
                with e.Fori(1, G - 1) as n:
                    group(n, n - 1, n + 1)
                group(G - 1, G - 2, None)
                end(G - 1)

            @block.vector
            def _(e):
                e.nop().then_inc(V.sem, V.P)
                e.nop().then_inc(VS.sem, VS.P)
                e.nop().then_inc(VE.sem, VE.P)
                e.tensor_scalar(w2s[:, :, :], w2s[:, :, :], 0.5, None, ALU.mult).then_inc(s_v, 1)

                def start(n):
                    TS.wait(e, n, "xT")
                    e.tensor_copy(xT[:, 0:2 * L], bank[0][0:D, 0:2 * L]).then_inc(VS.sem, 1)

                def end(n, par):
                    TE.wait(e, n, "turn")
                    out.count(e, n)
                    e.tensor_tensor(h2[:, :, :].rearrange("p (q k) d -> p q k d", q=2),
                                    bank[7][0:TL, :].rearrange("p (k q d) -> p q k d", k=4, q=2),
                                    sw[:, bass.ds(8 * n, 8)].rearrange("p (q k) -> p q k", q=2).unsqueeze(3).to_broadcast([TL, 2, 4, D]), ALU.mult).then_inc(VE.sem, 1)
                    VE.wait(e, n, "yw")
                    V.wait(e, n, "hx")
                    e.tensor_tensor(h2[:, :, :], h2[:, :, :], hx[:, par, :, :], ALU.add).then_inc(VE.sem, 1)

                def inner(n, i):
                    A.wait(e, n, f"u{i}")
                    e.tensor_tensor(t2[:, i, :], u[:, i, :], u[:, i, :], ALU.mult).then_inc(V.sem, 1)
                    V.wait(e, n, f"uu{i}")
                    e.tensor_scalar(t2[:, i, :], t2[:, i, :], 0.044715, 1.0, ALU.mult, ALU.add).then_inc(V.sem, 1)
                    V.wait(e, n, f"uv{i}")
                    e.tensor_tensor(t2[:, i, :], t2[:, i, :], u[:, i, :], ALU.mult).then_inc(V.sem, 1)

                def outer(n, i):
                    A.wait(e, n, f"th{i}")
                    e.scalar_tensor_tensor(out=gg[:, i, :], in0=t2[:, i, :], scalar=1.0, in1=u[:, i, :], op0=ALU.add, op1=ALU.mult).then_inc(V.sem, 1)

                def group(n, par, before, ahead):
                    V.wait(e, n, "gg3", 1)
                    hin.wait(e, n, "h")
                    xin.wait(e, n, "x")
                    e.tensor_tensor(hx[:, par, :, :], xn[:, :, :], ht[:, :, :], ALU.add).then_inc(V.sem, 1)
                    inner(n, 0)
                    inner(n, 1)
                    TE.wait(e, n, "y", 1)
                    outer(n, 0)
                    inner(n, 2)
                    outer(n, 1)
                    if before is not None:
                        end(before, 1 - par)
                    inner(n, 3)
                    outer(n, 2)
                    if ahead is not None:
                        start(ahead)
                    outer(n, 3)

                start(0)
                group(0, 0, None, 1)
                with e.Fori(0, G // 2 - 1) as m:
                    group(2 * m + 1, 1, 2 * m, 2 * m + 2)
                    group(2 * m + 2, 0, 2 * m + 1, 2 * m + 3)
                group(G - 1, 1, G - 2, None)
                end(G - 1, 1)


def key_layer(nc, W_fused, H2, ZR, VR, GR):
    NF = 3 * D + 3
    with ExitStack() as ctx:
        S = Space(nc, ctx, "key")
        ident, eps = S.sb("ident", [128, 128]), S.sb("eps", [128, 1])
        wr, wT = S.sb("wr", [128, 2, D]), S.sb("wT", [D, NF])
        zero = S.sb("zero", [128, 64 * D])
        ht, xn, sq = S.sb("ht", [TL, 8, D]), S.sb("xn", [TL, 8, D]), S.sb("sq", [TL, 8, D])
        s1, s2 = S.sb("s1", [TL, 8]), S.sb("s2", [TL, 8])
        xT = S.sb("xT", [D, 4 * L])
        sg, silu, kqv = S.sb("sg", [TL, 8, NF]), S.sb("silu", [TL, 3, 8, D]), S.sb("kqv", [TL, 3, 8, D])
        k2, ss, gt = S.sb("k2", [TL, 16, D]), S.sb("ss", [TL, 16]), S.sb("gt", [TL, 8, 4])
        bank = S.banks()
        s_own, s_own_sp, s_own_pe = S.sem("settled"), S.sem("settled_sp"), S.sem("settled_pe")
        s_id, s_w, s_z, s_v, s_t = S.sem("ident"), S.sem("weights"), S.sem("zeros"), S.sem("set_v"), S.sem("set_t")
        G = B // 4
        V, A = Loop(S.sem("vector"), NORM_V), Loop(S.sem("scalar"), ["std"])
        T = Loop(S.sem("tensor"), ["xT"] + [f"f{i}" for i in range(4)])
        VE = Loop(S.sem("vector_end"), ["xT0"] + [f"si{i}" for i in range(4)] + ["k2", "ss", "g0", "g1", "g2", "g3", "mx", "rn", "kn"])
        AE = Loop(S.sem("scalar_end"), ["xT1"] + [f"sg{i}" for i in range(4)] + ["nrm", "v"])
        hin = Loop(S.sem("h_in"), ["h"], 16, 0)
        out = Loop(S.sem("out"), ["z"], 16 * 8, 0)
        with nc.Block() as block:
            @block.gpsimd
            def _(e):
                make_identity(e, ident, s_id)
                with e.Fori(0, G) as n:
                    V.wait(e, n, "cen", 1)
                    settled(e, s_own)
                    e.dma_start(ht[:, :, :].rearrange("p (b a) d -> p b (a d)", a=2),
                                H2[bass.ds(4 * n, 4), :, :, :].rearrange("b p a d -> p b (a d)")).then_inc(hin.sem, 16)

            @block.sync
            def _(e):
                e.dma_start(wr[:, 0, :], W_fused[0:128, :]).then_inc(s_w, 16)
                e.dma_start(wr[0:NF - 128, 1, :], W_fused[128:NF, :]).then_inc(s_w, 16)
                e.wait_ge(s_v, 1)
                z3 = lambda k: zero[:, 0:k * D].rearrange("p (t d) -> p t d", d=D)
                nz = 0
                for t0 in range(0, VR.shape[0], 64):
                    k = min(64, VR.shape[0] - t0)
                    e.dma_start(VR[t0:t0 + k, :, :].rearrange("t p d -> p t d"), z3(k)).then_inc(s_z, 16)
                    nz += 1
                e.dma_start(ZR[0:CH + 1, :, :].rearrange("t p d -> p t d"), z3(CH + 1)).then_inc(s_z, 16)
                k = ZR.shape[0] - CH - L
                e.dma_start(ZR[CH + L:, :, :].rearrange("t p d -> p t d"), z3(k)).then_inc(s_z, 16)
                e.dma_start(GR[:, L:, :], zero[0:B, 0:4 * (CH * NCH - L)].rearrange("p (t g) -> p t g", g=4)).then_inc(s_z, 16)
                e.wait_ge(s_z, 16 * (nz + 3))
                with e.Fori(0, 4) as j:
                    with e.Fori(0, 4) as q:
                        n = 4 * j + q
                        VE.wait(e, n, "kn")
                        settled(e, s_own_sp)
                        AE.wait(e, n, "v")
                        settled(e, s_own_sp)
                        for a in range(2):
                            t0 = TL * a
                            for w, (dst, row) in enumerate(((ZR[CH + 1 + t0:CH + 1 + t0 + TL], 16), (ZR[CH + t0:CH + t0 + TL], 0), (VR[t0:t0 + TL], 0))):
                                e.dma_start(dst[:, bass.ds(32 * j + 4 * q + row, 4), :], kqv[:, w, a:8:2, :]).then_inc(out.sem, 16)
                            e.dma_start(GR[bass.ds(4 * n, 4), t0:t0 + TL, :].rearrange("b t g -> t b g"), gt[:, a:8:2, :]).then_inc(out.sem, 16)
                out.count(e, B // 4)

            @block.tensor
            def _(e):
                e.wait_ge(s_w, 32)
                e.wait_ge(s_id, 2)
                e.transpose(bank[0][0:D, 0:128], wr[:, 0, :], ident[:, :]).then_inc(s_t, 1)
                e.transpose(bank[0][0:D, 128:NF], wr[0:NF - 128, 1, :], ident[0:NF - 128, 0:NF - 128]).then_inc(s_t, 1)
                e.nop().then_inc(T.sem, T.P)
                e.wait_ge(s_v, 3)
                with e.Fori(0, B // 4) as n:
                    V.wait(e, n, "xn")
                    settled(e, s_own_pe)
                    for k in range(8):
                        mm = e.transpose(bank[k // 4][0:D, TL * (k % 4):TL * (k % 4) + TL], xn[:, k, :], ident[0:TL, 0:TL])
                    mm.then_inc(T.sem, 1)
                    VE.wait(e, n, "xT0")
                    AE.wait(e, n, "xT1")
                    for i in range(4):
                        for a in range(2):
                            k = 2 * i + a
                            mm = e.matmul(bank[2 + i][0:TL, NF * a:NF * a + NF], xT[:, TL * k:TL * k + TL], wT[:, :], start=True, stop=True)
                        mm.then_inc(T.sem, 1)

            @block.scalar
            def _(e):
                e.nop().then_inc(AE.sem, AE.P)
                e.nop().then_inc(A.sem, A.P)

                def end(m, ahead):
                    T.wait(e, m, "xT")
                    e.activation(xT[:, 2 * L:], bank[1][0:D, 0:2 * L], ACT.Copy).then_inc(AE.sem, 1)
                    VE.wait(e, m, "g3", 1)
                    for i in range(4):
                        T.wait(e, m, f"f{i}")
                        e.activation(sg[:, 2 * i:2 * i + 2, :], bank[2 + i][0:TL, 0:2 * NF].rearrange("p (a f) -> p a f", a=2), ACT.Sigmoid).then_inc(AE.sem, 1)
                    if ahead is not None:
                        norm_scalar(e, V, A, ahead, s2, eps)
                    VE.wait(e, m, "ss")
                    e.activation(ss[:, :], ss[:, :], ACT.Sqrt).then_inc(AE.sem, 1)
                    out.count(e, m)
                    e.activation(kqv[:, 2, :, :], silu[:, 2, :, :], ACT.Copy).then_inc(AE.sem, 1)

                norm_scalar(e, V, A, 0, s2, eps)
                with e.Fori(1, G) as n:
                    end(n - 1, n)
                end(G - 1, None)

            @block.vector
            def _(e):
                e.memset(zero[:, :], 0.0).then_inc(s_v, 1)
                e.memset(eps[:, :], EPS).then_inc(s_v, 1)
                e.wait_ge(s_t, 2)
                e.tensor_copy(wT[:, :], bank[0][0:D, 0:NF]).then_inc(s_v, 1)
                e.wait_ge(s_v, 3)
                e.nop().then_inc(V.sem, V.P)
                e.nop().then_inc(VE.sem, VE.P)
                t = (s1, s2, sq)

                def start(n):
                    hin.wait(e, n, "h")
                    V.wait(e, n, "xn", 1)
                    norm_center(e, V, n, ht[:, :, :], 8, t, xn[:, :, :])
                    norm_square(e, V, n, 8, t, xn[:, :, :])

                def end(m, ahead):
                    T.wait(e, m, "xT")
                    e.tensor_copy(xT[:, 0:2 * L], bank[0][0:D, 0:2 * L]).then_inc(VE.sem, 1)
                    if ahead is not None:
                        start(ahead)
                    AE.wait(e, m, "v", 1)
                    VE.wait(e, m, "kn", 1)
                    for i in range(4):
                        AE.wait(e, m, f"sg{i}")
                        e.tensor_tensor(silu[:, :, 2 * i:2 * i + 2, :].rearrange("p w a d -> p a w d"),
                                        bank[2 + i][0:TL, 0:2 * NF].rearrange("p (a f) -> p a f", a=2)[:, :, 0:3 * D].rearrange("p a (w d) -> p a w d", w=3),
                                        sg[:, 2 * i:2 * i + 2, 0:3 * D].rearrange("p a (w d) -> p a w d", w=3), ALU.mult).then_inc(VE.sem, 1)
                    VE.wait(e, m, "si3")
                    qk = lambda buf: buf[:, 0:2, :, :].rearrange("p w k d -> p (w k) d")
                    e.tensor_tensor(k2[:, :, :], qk(silu), qk(silu), ALU.mult).then_inc(VE.sem, 1)
                    VE.wait(e, m, "k2")
                    e.tensor_reduce(ss[:, :], k2[:, :, :], AX, ALU.add).then_inc(VE.sem, 1)
                    out.count(e, m)
                    e.tensor_copy(gt[:, :, 0:1], sg[:, :, NF - 1:NF]).then_inc(VE.sem, 1)
                    e.tensor_scalar(gt[:, :, 1:2], sg[:, :, NF - 3:NF - 2], -1.0, 1.0, ALU.mult, ALU.add).then_inc(VE.sem, 1)
                    e.tensor_scalar(gt[:, :, 2:3], sg[:, :, NF - 2:NF - 1], -0.1 * 4.0 / D, None, ALU.mult).then_inc(VE.sem, 1)
                    e.tensor_copy(gt[:, :, 3:4], sg[:, :, NF - 1:NF]).then_inc(VE.sem, 1)
                    if ahead is not None:
                        norm_scale(e, V, A, ahead, 8, t, xn[:, :, :])
                    AE.wait(e, m, "nrm")
                    e.tensor_scalar(ss[:, :], ss[:, :], 1e-12, None, ALU.max).then_inc(VE.sem, 1)
                    VE.wait(e, m, "mx")
                    e.reciprocal(ss[:, :], ss[:, :]).then_inc(VE.sem, 1)
                    VE.wait(e, m, "rn")
                    e.tensor_tensor(qk(kqv), qk(silu), ss[:, :].unsqueeze(2).to_broadcast([TL, 16, D]), ALU.mult).then_inc(VE.sem, 1)

                start(0)
                norm_scale(e, V, A, 0, 8, t, xn[:, :, :])
                with e.Fori(1, G) as n:
                    end(n - 1, n)
                end(G - 1, None)


def expert_layer(nc, Wg, bg, W1, b1, W2, b2, H2, YR, out_dram):
    G = B // 4
    E = NH
    with ExitStack() as ctx:
        S = Space(nc, ctx, "moe")
        ident, eps = S.sb("ident", [128, 128]), S.sb("eps", [128, 1])
        wraw = S.sb("wraw", [128, 2, HID])
        W_PARTS = [S.sb(f"w_{q}", [128, E, HID], BF16) for q in ("11", "22", "31")]
        wrest = S.sb("wrest", [D, HID])
        w2T = S.sb("w2T", [128, E, 2, D])
        x21s, x13s, xrest = S.sb("x21", [128, 2, 4 * L], BF16), S.sb("x13", [128, 2, 4 * L], BF16), S.sb("xrest", [D, 4 * L])
        c123s, cpart, crest = S.sb("c123", [72, 2, 4 * L], BF16), S.sb("cpart", [E, 4 * L], BF16), S.sb("crest", [E, 4 * L])
        wgr, wgT, bgb = S.sb("wgr", [E, D]), S.sb("wgT", [D, E]), S.sb("bgb", [TL, E])
        b1s, b2s = S.sb("b1s", [128, E, 2]), S.sb("b2s", [E, D])
        sel = S.sb("sel", [72, E, 128], BF16)
        tri = S.sb("tri", [128, E, E])
        hts, yt, xn, sq = S.sb("ht", [TL, 2, 8, D]), S.sb("yt", [TL, 8, D]), S.sb("xn", [TL, 8, D]), S.sb("sq", [TL, 8, D])
        s1, s2 = S.sb("s1", [TL, 8]), S.sb("s2", [TL, 8])
        xT = S.sb("xT", [D, 4 * L])
        gs, rk, ex, mz = S.sb("gs", [TL, 8, E]), S.sb("rk", [TL, 8, E]), S.sb("ex", [TL, 8, E]), S.sb("mz", [TL, 2, 8])
        c1, c2 = S.sb("c1", [TL, 8, E, E]), S.sb("c2", [TL, 8, E, E])
        cTs = S.sb("cT", [E, 2, 4 * L])
        hb, hw = S.sb("hb", [128, 2, 2, 2 * L]), S.sb("hw", [128, 2, 2, 2 * L])
        yT, o = S.sb("yT", [128, 2 * L]), S.sb("o", [TL, 8, D])
        bank = S.banks()
        s_own, s_own_sp, s_own_pe = S.sem("settled"), S.sem("settled_sp"), S.sem("settled_pe")
        s_id, s_w, s_v, s_t = S.sem("ident"), S.sem("weights"), S.sem("set_v"), S.sem("set_t")
        NW = 8
        EH = [(x_, a) for x_ in range(E) for a in range(2)]
        names = [f"w{x_}{a}{q}" for x_, a in EH for q in range(2)] + ["o"]
        V = Loop(S.sem("vector"), names, before=2 * len(names))
        A = Loop(S.sem("scalar"), [f"h{x_}{a}{q}" for x_, a in EH for q in range(2)] + ["yT"])
        order = []
        for i, (x_, a) in enumerate(EH):
            order += ([f"b{x_}0", f"b{x_}1"] if a == 0 else []) + [f"h{x_}{a}0", f"h{x_}{a}1"] + ([f"y{i - 1}"] if i else [])
        T = Loop(S.sem("tensor"), order + ["y15", "yb", "turn"])
        VP = Loop(S.sem("vector_prep"), ["h3"] + NORM_V + ["xT0", "xT1", "x1", "xr", "x3", "gs", "gt", "eq", "eqt", "cmp", "rk", "m1", "gm",
                                                         "sel", "z", "rz", "cmb", "cT0", "cT1", "cr", "cp", "c3"])
        AP = Loop(S.sem("scalar_prep"), ["std", "x1", "x2", "exp", "c1", "c2"])
        TP = Loop(S.sem("tensor_prep"), ["xT0", "xT1", "g", "cT0", "cT1"])
        hin = Loop(S.sem("h_in"), ["h"], 48, 0)
        out = Loop(S.sem("out"), ["h"], 32, 0)
        with nc.Block() as block:
            @block.gpsimd
            def _(e):
                make_identity(e, ident, s_id)
                e.wait_ge(s_id, 2)
                e.memset(tri[:, :, :], 1.0).then_inc(s_id, 1)
                e.wait_ge(s_id, 3)
                e.affine_select(out=tri[:, :, :], in_=tri[:, :, :], compare_op=ALU.is_gt, fill=0.0, base=0,
                                pattern=[[1, E], [-1, E]], channel_multiplier=0).then_inc(s_id, 1)
                with e.Fori(0, 4) as j:
                    with e.Fori(0, 2) as q2:
                        for par in range(2):
                            q = 2 * q2 + par
                            n = 4 * j + q
                            V.wait(e, n, "o", 2)
                            settled(e, s_own)
                            VP.wait(e, n, "h3", 1)
                            settled(e, s_own)
                            e.dma_start(hts[:, par, :, :].rearrange("p (b a) d -> p b (a d)", a=2),
                                        H2[bass.ds(4 * n, 4), :, :, :].rearrange("b p a d -> p b (a d)")).then_inc(hin.sem, 16)
                            for a in range(2):
                                e.dma_start(yt[:, a:8:2, :], YR[1 + TL * a:1 + TL * a + TL, bass.ds(32 * j + 4 * q + 16, 4), :]).then_inc(hin.sem, 16)

            @block.sync
            def _(e):
                e.dma_start(wgr[:, :], Wg).then_inc(s_w, 16)
                e.dma_start(bgb[:, :], bg.partition_broadcast(TL)).then_inc(s_w, 16)
                with nc.allow_non_contiguous_dma("biases, one an element"):
                    for a in range(2):
                        e.dma_start(b1s[:, :, a], b1[:, 128 * a:128 * a + 128].rearrange("e p -> p e")).then_inc(s_w, 16)
                e.dma_start(b2s[:, :], b2).then_inc(s_w, 16)
                for x_ in range(E):
                    if x_:
                        e.wait_ge(s_t, 1 + 4 * x_)
                    e.dma_start(wraw[:, 0, 0:2 * D].rearrange("p (a d) -> p a d", a=2), W1[x_].rearrange("(a p) d -> p a d", a=2)).then_inc(s_w, 16)
                    e.dma_start(wraw[0:D, 1, :], W2[x_]).then_inc(s_w, 16)
                with e.Fori(0, 4) as j:
                    with e.Fori(0, 2) as q2:
                        for par in range(2):
                            q = 2 * q2 + par
                            n = 4 * j + q
                            V.wait(e, n, "o")
                            settled(e, s_own_sp)
                            for a in range(2):
                                e.dma_start(out_dram[bass.ds(4 * n, 4), TL * a:TL * a + TL, :].rearrange("b t d -> t b d"), o[:, a:8:2, :]).then_inc(out.sem, 16)
                out.count(e, G)

            @block.tensor
            def _(e):
                e.wait_ge(s_id, 2)
                e.wait_ge(s_w, 16 * 7)
                e.transpose(bank[0][0:D, 0:E], wgr[:, :], ident[0:E, 0:E]).then_inc(s_t, 1)
                for x_ in range(E):
                    e.wait_ge(s_w, 16 * (7 + 2 * x_))
                    if x_:
                        e.wait_ge(s_v, 2 + NW * x_)
                    for a in range(2):
                        e.transpose(bank[1][0:D, 128 * a:128 * a + 128], wraw[:, 0, D * a:D * a + D], ident[:, :]).then_inc(s_t, 1)
                    for a in range(2):
                        e.transpose(bank[2][:, D * a:D * a + D], wraw[0:D, 1, 128 * a:128 * a + 128], ident[0:D, 0:D]).then_inc(s_t, 1)
                e.wait_ge(s_v, 2 + NW * E + 5)
                e.wait_ge(s_id, 4)
                e.nop().then_inc(T.sem, T.P)
                e.nop().then_inc(TP.sem, TP.P)

                def prep_x(n, q):
                    if q == 0:
                        V.wait(e, n, "o", 2)
                        settled(e, s_own_pe)
                        VP.wait(e, n, "xn")
                    else:
                        VP.wait(e, n, "xT0")
                    settled(e, s_own_pe)
                    for k in range(4):
                        mm = e.transpose(bank[7][0:D, TL * k:TL * k + TL], xn[:, 4 * q + k, :], ident[0:TL, 0:TL])
                    mm.then_inc(TP.sem, 1)

                def prep_scores(n):
                    VP.wait(e, n, "xT1")
                    for k in range(8):
                        mm = e.matmul(bank[7][0:TL, E * k:E * k + E], xT[:, TL * k:TL * k + TL], wgT[:, :], start=True, stop=True)
                    mm.then_inc(TP.sem, 1)

                def prep_weights(n, q):
                    VP.wait(e, n, "cT0" if q else "cmb")
                    settled(e, s_own_pe)
                    for k in range(4):
                        mm = e.transpose(bank[7][0:E, TL * k:TL * k + TL], ex[:, 4 * q + k, :], ident[0:TL, 0:TL])
                    mm.then_inc(TP.sem, 1)

                def group(n, par, ahead):
                    x21, x13, c123, cT = x21s[:, par, :], x13s[:, par, :], c123s[:, par, :], cTs[:, par, :]
                    VP.wait(e, n, "c3")
                    AP.wait(e, n, "c2")

                    def first(i):
                        x_, a = EH[i]
                        if a == 0:
                            if x_:
                                V.wait(e, n, f"w{x_ - 1}11")
                            for q in range(2):
                                e.matmul(bank[q][:, 0:2 * L], sel[:, x_, :], c123[:, 2 * L * q:2 * L * q + 2 * L], start=True, stop=True).then_inc(T.sem, 1)
                        if i >= 2:
                            A.wait(e, n, "h%d%d1" % EH[i - 2])
                        for q in range(2):
                            for k, (w, xp) in enumerate(zip(W_PARTS, (x21, x21, x13))):
                                mm = e.matmul(bank[2 + 2 * a + q][:, 0:2 * L], w[:, x_, 128 * a:128 * a + 128], xp[:, 2 * L * q:2 * L * q + 2 * L],
                                              start=(k == 0), stop=(k == 2))
                            mm.then_inc(T.sem, 1)

                    def second(i):
                        x_, a = EH[i]
                        V.wait(e, n, f"w{x_}{a}1")
                        for q in range(2):
                            mm = e.matmul(bank[6][D * q:D * q + D, 0:2 * L], w2T[:, x_, a, :], hw[:, a, q, :], start=(i == 0), stop=False)
                        return mm

                    for i in range(2 * E):
                        first(i)
                        if i:
                            second(i - 1).then_inc(T.sem, 1)
                        if ahead and i == 3:
                            prep_x(n + 1, 0)
                        if ahead and i == 5:
                            prep_x(n + 1, 1)
                        if ahead and i == 7:
                            prep_scores(n + 1)
                        if ahead and i == 11:
                            prep_weights(n + 1, 0)
                        if ahead and i == 12:
                            prep_weights(n + 1, 1)
                    second(2 * E - 1).then_inc(T.sem, 1)
                    for q in range(2):
                        mm = e.matmul(bank[6][D * q:D * q + D, 0:2 * L], b2s[:, :], cT[:, 2 * L * q:2 * L * q + 2 * L], start=False, stop=True)
                    mm.then_inc(T.sem, 1)
                    if ahead:
                        VP.wait(e, n + 1, "cT1")
                    A.wait(e, n, "yT")
                    for k in range(4):
                        mm = e.transpose(bank[7][0:TL, 128 * k:128 * k + 128], yT[:, TL * k:TL * k + TL], ident[:, :])
                    mm.then_inc(T.sem, 1)

                prep_x(0, 0)
                prep_x(0, 1)
                prep_scores(0)
                prep_weights(0, 0)
                prep_weights(0, 1)
                with e.Fori(0, G // 2 - 1) as m:
                    group(2 * m, 0, True)
                    group(2 * m + 1, 1, True)
                group(G - 2, 0, True)
                group(G - 1, 1, False)

            @block.scalar
            def _(e):
                e.nop().then_inc(A.sem, A.P)
                e.nop().then_inc(AP.sem, AP.P)

                def prep_first(n, par):
                    VP.wait(e, n, "xT1")
                    e.activation(x21s[D:, par, :], xT[:, :], ACT.Copy).then_inc(AP.sem, 1)

                def prep_second(n, par):
                    VP.wait(e, n, "xr")
                    e.activation(x21s[0:D, par, :], xrest[:, :], ACT.Copy).then_inc(AP.sem, 1)

                def prep_exp(n):
                    VP.wait(e, n, "gm")
                    e.activation(ex[:, :, :], gs[:, :, :], ACT.Exp).then_inc(AP.sem, 1)

                def prep_weight_first(n, par):
                    VP.wait(e, n, "cT1")
                    e.activation(c123s[0:E, par, :], cTs[:, par, :], ACT.Copy).then_inc(AP.sem, 1)

                def prep_weight_second(n, par):
                    VP.wait(e, n, "cr")
                    e.activation(c123s[32:32 + E, par, :], crest[:, :], ACT.Copy).then_inc(AP.sem, 1)

                def group(n, par, ahead):
                    for i, (x_, a) in enumerate(EH):
                        for q in range(2):
                            T.wait(e, n, f"h{x_}{a}{q}")
                            if i >= 2:
                                V.wait(e, n, f"w{x_ - 1}{a}{q}")
                            e.activation(hb[:, a, q, :], bank[2 + 2 * a + q][:, 0:2 * L], ACT.Relu, bias=b1s[:, x_, a:a + 1]).then_inc(A.sem, 1)
                        if ahead and i == 1:
                            norm_scalar(e, VP, AP, n + 1, s2, eps)
                        if ahead and i == 6:
                            prep_first(n + 1, 1 - par)
                        if ahead and i == 7:
                            prep_second(n + 1, 1 - par)
                        if ahead and i == 9:
                            prep_exp(n + 1)
                        if ahead and i == 12:
                            prep_weight_first(n + 1, 1 - par)
                        if ahead and i == 13:
                            prep_weight_second(n + 1, 1 - par)
                    T.wait(e, n, "yb")
                    e.activation(yT[:, :], bank[6][:, 0:2 * L], ACT.Copy).then_inc(A.sem, 1)

                norm_scalar(e, VP, AP, 0, s2, eps)
                prep_first(0, 0)
                prep_second(0, 0)
                prep_exp(0)
                prep_weight_first(0, 0)
                prep_weight_second(0, 0)
                with e.Fori(0, G // 2 - 1) as m:
                    group(2 * m, 0, True)
                    group(2 * m + 1, 1, True)
                group(G - 2, 0, True)
                group(G - 1, 1, False)

            @block.vector
            def _(e):
                e.memset(eps[:, :], EPS).then_inc(s_v, 1)
                e.wait_ge(s_t, 1)
                e.tensor_copy(wgT[:, :], bank[0][0:D, 0:E]).then_inc(s_v, 1)
                for x_ in range(E):
                    e.wait_ge(s_t, 1 + 4 * x_ + 4)
                    w11, w22, w31 = (w[:, x_, :] for w in W_PARTS)
                    ps = bank[1][0:D, 0:HID]
                    for dst in (w11[0:D], w11[D:], w31[D:]):
                        e.tensor_copy(dst, ps).then_inc(s_v, 1)
                    e.wait_ge(s_v, 2 + NW * x_ + 3)
                    e.tensor_tensor(wrest[:, :], ps, w11[0:D], ALU.subtract).then_inc(s_v, 1)
                    e.wait_ge(s_v, 2 + NW * x_ + 4)
                    for dst in (w22[0:D], w22[D:]):
                        e.tensor_copy(dst, wrest[:, :]).then_inc(s_v, 1)
                    e.wait_ge(s_v, 2 + NW * x_ + 6)
                    e.tensor_tensor(w31[0:D], wrest[:, :], w22[0:D], ALU.subtract).then_inc(s_v, 1)
                    e.tensor_copy(w2T[:, x_, :, :].rearrange("p a d -> p (a d)"), bank[2][:, 0:2 * D]).then_inc(s_v, 1)
                e.wait_ge(s_id, 4)
                e.memset(sel[:, :, :], 0.0).then_inc(s_v, 1)
                e.memset(c123s[:, :, :], 0.0).then_inc(s_v, 1)
                e.wait_ge(s_v, 2 + NW * E + 2)
                for g in range(3):
                    e.tensor_copy(sel[32 * g:32 * g + E, :, :], ident[32 * g:32 * g + E, 32 * g:32 * g + E].unsqueeze(2).to_broadcast([E, E, 128])).then_inc(s_v, 1)
                e.wait_ge(s_v, 2 + NW * E + 5)
                e.nop().then_inc(V.sem, V.before)
                e.nop().then_inc(VP.sem, VP.P)
                tok = lambda t: t.unsqueeze(2).to_broadcast([TL, 8, E])

                t_norm = (s1, s2, sq)

                def prep_center(n, par):
                    ht = hts[:, par, :, :]
                    hin.wait(e, n, "h")
                    e.tensor_tensor(ht, ht, yt[:, :, :], ALU.add).then_inc(VP.sem, 1)
                    VP.wait(e, n, "h3")
                    norm_center(e, VP, n, ht, 8, t_norm, xn[:, :, :])

                def prep_x(n, q):
                    TP.wait(e, n, f"xT{q}")
                    e.tensor_copy(xT[:, 2 * L * q:2 * L * q + 2 * L], bank[7][0:D, 0:2 * L]).then_inc(VP.sem, 1)

                def prep_rest(n, par):
                    x13 = x13s[:, par, :]
                    VP.wait(e, n, "xT1")
                    e.tensor_copy(x13[0:D, :], xT[:, :]).then_inc(VP.sem, 1)
                    VP.wait(e, n, "x1")
                    e.tensor_tensor(xrest[:, :], xT[:, :], x13[0:D, :], ALU.subtract).then_inc(VP.sem, 1)

                def prep_scores(n, par):
                    AP.wait(e, n, "x2")
                    e.tensor_tensor(x13s[D:, par, :], xrest[:, :], x21s[0:D, par, :], ALU.subtract).then_inc(VP.sem, 1)
                    TP.wait(e, n, "g")
                    e.tensor_tensor(gs[:, :, :], bank[7][0:TL, 0:8 * E].rearrange("p (k x) -> p k x", x=E),
                                    bgb[:, :].unsqueeze(1).to_broadcast([TL, 8, E]), ALU.add).then_inc(VP.sem, 1)
                    VP.wait(e, n, "gs")
                    mine = gs[:, :, :].unsqueeze(3).to_broadcast([TL, 8, E, E])
                    other = gs[:, :, :].unsqueeze(2).to_broadcast([TL, 8, E, E])
                    e.tensor_tensor(c1[:, :, :, :], other, mine, ALU.is_gt).then_inc(VP.sem, 1)
                    e.tensor_tensor(c2[:, :, :, :], other, mine, ALU.is_equal).then_inc(VP.sem, 1)
                    VP.wait(e, n, "eq")
                    trif = tri[0:TL, :, :].rearrange("p x y -> p (x y)").unsqueeze(1).to_broadcast([TL, 8, E * E])
                    pairs = lambda t: t[:, :, :, :].rearrange("p k x y -> p k (x y)")
                    e.tensor_tensor(pairs(c2), pairs(c2), trif, ALU.mult).then_inc(VP.sem, 1)

                def prep_rank(n):
                    VP.wait(e, n, "eqt")
                    e.tensor_tensor(c1[:, :, :, :], c1[:, :, :, :], c2[:, :, :, :], ALU.add).then_inc(VP.sem, 1)
                    VP.wait(e, n, "cmp")
                    e.tensor_reduce(rk[:, :, :], c1[:, :, :, :], AX, ALU.add).then_inc(VP.sem, 1)
                    e.tensor_reduce(mz[:, 0, :], gs[:, :, :], AX, ALU.max).then_inc(VP.sem, 1)
                    VP.wait(e, n, "m1")
                    e.tensor_tensor(gs[:, :, :], gs[:, :, :], tok(mz[:, 0, :]), ALU.subtract).then_inc(VP.sem, 1)

                def prep_softmax(n):
                    AP.wait(e, n, "exp")
                    VP.wait(e, n, "rk")
                    e.scalar_tensor_tensor(out=ex[:, :, :], in0=rk[:, :, :], scalar=1.5, in1=ex[:, :, :], op0=ALU.is_lt, op1=ALU.mult).then_inc(VP.sem, 1)
                    VP.wait(e, n, "sel")
                    e.tensor_reduce(mz[:, 1, :], ex[:, :, :], AX, ALU.add).then_inc(VP.sem, 1)
                    VP.wait(e, n, "z")
                    e.reciprocal(mz[:, 1, :], mz[:, 1, :]).then_inc(VP.sem, 1)
                    VP.wait(e, n, "rz")
                    e.tensor_tensor(ex[:, :, :], ex[:, :, :], tok(mz[:, 1, :]), ALU.mult).then_inc(VP.sem, 1)

                def prep_weights(n, par, q):
                    TP.wait(e, n, f"cT{q}")
                    e.tensor_copy(cTs[:, par, 2 * L * q:2 * L * q + 2 * L], bank[7][0:E, 0:2 * L]).then_inc(VP.sem, 1)

                def prep_weight_rest(n, par):
                    c123, cT = c123s[:, par, :], cTs[:, par, :]
                    AP.wait(e, n, "c1")
                    e.tensor_tensor(crest[:, :], cT, c123[0:E, :], ALU.subtract).then_inc(VP.sem, 1)
                    VP.wait(e, n, "cr")
                    e.tensor_copy(cpart[:, :], crest[:, :]).then_inc(VP.sem, 1)

                def prep_weight_third(n, par):
                    c123 = c123s[:, par, :]
                    VP.wait(e, n, "cp")
                    e.tensor_tensor(c123[64:64 + E, :], crest[:, :], cpart[:, :], ALU.subtract).then_inc(VP.sem, 1)

                def group(n, par, ahead):
                    for i, (x_, a) in enumerate(EH):
                        for q in range(2):
                            A.wait(e, n, f"h{x_}{a}{q}")
                            T.wait(e, n, f"b{x_}{q}" if a == 0 or i < 2 else f"y{i - 2}")
                            e.tensor_tensor(hw[:, a, q, :], hb[:, a, q, :], bank[q][:, 0:2 * L], ALU.mult).then_inc(V.sem, 1)
                        if ahead and i == 0:
                            prep_center(n + 1, 1 - par)
                        if ahead and i == 1:
                            norm_square(e, VP, n + 1, 8, t_norm, xn[:, :, :])
                        if ahead and i == 2:
                            norm_scale(e, VP, AP, n + 1, 8, t_norm, xn[:, :, :])
                        if ahead and i == 4:
                            prep_x(n + 1, 0)
                        if ahead and i == 6:
                            prep_x(n + 1, 1)
                        if ahead and i == 7:
                            prep_rest(n + 1, 1 - par)
                        if ahead and i == 8:
                            prep_scores(n + 1, 1 - par)
                        if ahead and i == 9:
                            prep_rank(n + 1)
                        if ahead and i == 10:
                            prep_softmax(n + 1)
                        if ahead and i == 11:
                            prep_weights(n + 1, 1 - par, 0)
                        if ahead and i == 12:
                            prep_weights(n + 1, 1 - par, 1)
                        if ahead and i == 13:
                            prep_weight_rest(n + 1, 1 - par)
                        if ahead and i == 14:
                            prep_weight_third(n + 1, 1 - par)
                    T.wait(e, n, "turn")
                    out.count(e, n)
                    e.tensor_tensor(o[:, :, :].rearrange("p (q k) d -> p q k d", q=2),
                                    bank[7][0:TL, :].rearrange("p (k q d) -> p q k d", k=4, q=2),
                                    hts[:, par, :, :].rearrange("p (q k) d -> p q k d", q=2), ALU.add).then_inc(V.sem, 1)

                prep_center(0, 0)
                norm_square(e, VP, 0, 8, t_norm, xn[:, :, :])
                norm_scale(e, VP, AP, 0, 8, t_norm, xn[:, :, :])
                prep_x(0, 0)
                prep_x(0, 1)
                prep_rest(0, 0)
                prep_scores(0, 0)
                prep_rank(0)
                prep_softmax(0)
                prep_weights(0, 0, 0)
                prep_weights(0, 0, 1)
                prep_weight_rest(0, 0)
                prep_weight_third(0, 0)
                with e.Fori(0, G // 2 - 1) as m:
                    group(2 * m, 0, True)
                    group(2 * m + 1, 1, True)
                group(G - 2, 0, True)
                group(G - 1, 1, False)


class Stages:

    def __init__(self, sem, update, step, unit=1):
        self.sem, self.unit = sem, unit
        self.update, self.steps = update, step
        self.U, self.P = len(update), len(step)
        self.base = self.P
        assert len(set(step)) == self.P and len(set(update)) == self.U
        self.su = {n: i + 1 for i, n in enumerate(step)}
        self.uu = {n: i + 1 for i, n in enumerate(update)}
        self.chunk = self.U + CH * self.P

    def begun(self, c):
        return c * (self.chunk * self.unit) + self.base * self.unit

    def upd(self, c, name):
        return c * (self.chunk * self.unit) + (self.base + self.uu[name]) * self.unit

    def step(self, c, s, name, back=0):
        k = self.base + self.U + self.su[name] - back * self.P
        return c * (self.chunk * self.unit) + s * (self.P * self.unit) + k * self.unit


def recurrent_layer(nc, ZR, VR, GR, YR, S0D, BASED, W0, P0, W1, P1):
    with ExitStack() as ctx:
        def sb(name, shape):
            return ctx.enter_context(nc.sbuf_tensor(name, shape, F32))

        def sem(name):
            return ctx.enter_context(nc.semaphore(name))

        HD, D = 256, 64
        LAST = L + 1 - CH * (NCH - 1)
        MW = CH + 2 * D
        mv1 = sb("mv1", [128, 2, 16, 4, MW])
        mvt = sb("mvt", [128, 32, 2 * HD])
        hist = sb("hist", [128, 8, 2 * HD + D])
        yth = sb("yth", [128, 32, CH])
        hdiag = sb("hdiag", [128, 2, 16, 4, 32])
        ydiag = sb("ydiag", [128, 8, 4, 32])
        gdiag = sb("gdiag", [128, 2, 4, 32])
        ddiag = sb("ddiag", [128, 2, 4, 32])
        adiag = sb("adiag", [128, 2, 4, 32])
        ident = sb("r_ident", [128, 128])
        ones = sb("r_ones", [128, 128])
        repl = sb("repl", [128, 128])
        mi = sb("mi", [128, 8])
        mu = sb("mu", [128, 2])
        xb = sb("xb", [128, HD])
        BW = 2 * HD + CH
        work = sb("work", [128, 2 * BW])
        x, sg, om, sp = (work[:, HD * q:HD * q + HD] for q in range(4))
        h = sb("h", [128, HD])
        dh = sb("dh", [128, HD])
        dl = sb("dl", [128, HD])
        rep = sb("rep", [128, 3, 8, CH])
        y1 = sb("y1", [128, D])
        y = sb("y", [128, 2, D])
        al = sb("al", [128, 1])
        U = sb("U", [128, CH + 2])
        W = sb("W", [128, CH + 2])
        FAC = sb("FAC", [128, CH + 2])
        Wp = sb("Wp", [128, CH + 2])
        Wn = sb("Wn", [128, CH + 2])
        gates = sb("gates", [128, CH, 4])
        baset = sb("baset", [128, BW])
        dott = baset[:, 2 * HD:]
        vt = sb("vt", [128, D])
        cm = sb("cm", [128, 2, 128])
        cu = sb("cu", [128, 3, 8, 4])
        wy, wk = (h[:, :], dh[:, :]), (dl[:, :], xb[:, :])
        SB = 4
        s0s = sb("s0s", [128, SB, 2 * HD])
        zr = sb("zr", [CH * 2, 2, 128])
        ztm = sb("ztm", [128, 2, 2, 32])
        kt = sb("kt", [128, 2, CH])
        krow = sb("krow", [128, 8, D])
        bs = work[:, :].rearrange("p (a f) -> p a f", a=2)
        d3 = work[:, 0:384].rearrange("p (w q) -> p w q", w=3)
        bank = [ctx.enter_context(nc.psum_tensor(f"bank{i}", [128, 512], F32)) for i in range(8)]
        b = [t[:, :] for t in bank]
        psT = (b[0][:, 0:128], b[1][:, 0:128])
        psDT = b[0][:, 128:256]
        psP, psD = b[2], b[2][:, 256:256 + CH]
        psAT, psYT = b[3][:, 0:128], b[3][:, 128:256]
        psGT, psY = b[4][:, 0:128], b[4][:, 128:128 + D]
        psH = b[5]
        psR, psA = b[7][:, HD:], b[6][:, HD:2 * HD]
        psE = b[7]
        psZ, psDots, psC, psBase = b[0][:, 0:32], b[0][:, 32:64], b[6], (b[3], b[4])
        psNew = ((b[5], b[7]), (b[1], b[2]))

        SLABS = [(n, j) for n in range(8) for j in range(4)]
        vec_u = ["nfac", "srep", "cm0", "cm1", "d3a", "d3b", "d3c", "cu0", "cu1", "wy0", "wk0"]
        for k in range(32):
            vec_u += [f"wy{k + 1}", f"wk{k + 1}"] if k < 31 else []
            vec_u += [f"{a}{k}" for a in ("sa", "oa", "sb", "ob", "sn", "on")]
        vec_u += ["rw", "rw1", "ru", "ru1", "rf", "rf1", "rp", "ral", "x0"]
        vec_s = ["xa", "xz", "ha", "h", "hd0", "om", "sp", "tabu", "tabw", "tabp", "arep", "alast", "xb1", "xb2",
                 "setu", "setw", "setf", "setn", "grep", "adiag", "y1", "gdiag", "y2", "y", "ydiag", "xpre", "drep",
                 "ddiag", "dh1", "dh2", "newp", "dh3a", "dh3", "da", "d"]
        act_u = []
        for k in range(32):
            act_u += [f"kt{k}", f"zm0{k}", f"zm1{k}", f"c0{k}", f"c1{k}"] + ([f"ds{k}", f"bs0{k}", f"bs1{k}"] if k % 4 == 3 else [])
        act_s = ["siga", "sig", "hd1", "ht", "yt0", "yt1"]
        pe_u = ["ct0", "ct1", "cb", "st0", "so0"]
        for k in range(32):
            pe_u += [f"st{k + 1}", f"so{k + 1}"] if k < 31 else []
            pe_u += [f"zt{k}", f"tr{k}", f"ba{k}"]
        pe_s = ["tra", "tr", "pred", "at", "gt", "yp", "a", "yt", "sprep", "dd", "dt", "dhp", "e"]
        V = Stages(sem("vector_landed"), vec_u, vec_s)
        A = Stages(sem("scalar_landed"), act_u, act_s)
        T = Stages(sem("tensor_landed"), pe_u, pe_s)
        slab_in = [Stages(sem(f"slab_in{q}"), [f"s{k}" for k in range(q, 32, SB)], [], 16) for q in range(SB)]
        slab_out = [Stages(sem(f"slab_out{q}"), [f"s{k}" for k in range(q, 32, SB)], [], 16) for q in range(SB)]
        zr_in = [Stages(sem(f"zr_in{q}"), [f"z{k}" for k in range(q, 32, 2)], [], 16) for q in range(2)]
        base_out = Stages(sem("base_out"), [f"b{n}" for n in range(8)], [], 8 * 16)
        gates_in = Stages(sem("gates_in"), ["in"], [], 8 * 16)
        keys_in = Stages(sem("keys_in"), ["in"], [], 16 * 16)
        base_in = Stages(sem("base_in"), ["first"], ["next"], 16)
        value_in = Stages(sem("value_in"), ["first"], ["next"], 16)
        hist_h = Stages(sem("hist_h"), [], ["h"], 16 * NH)
        hist_y = Stages(sem("hist_y"), [], ["y"], 16 * (NH + 1))
        hist_d = Stages(sem("hist_d"), [], ["d"], 16 * NH)
        for q in (*slab_in, *zr_in, *slab_out, base_out, gates_in, keys_in, base_in, value_in, hist_h, hist_y, hist_d):
            q.base = 0
        s_set, s_own = sem("set_dma"), sem("settled")
        s_pool = sem("pool_set")
        s_v = sem("vec_set")
        s_p = sem("pe_set")
        s_init = sem("init_out")

        def ap(t, off, *dims):
            row = 1
            for q in t.shape[1:]:
                row *= q
            return bass.AP(t, off, [[row, t.shape[0]]] + [list(q) for q in dims])

        def p_dims(src, off=0):
            return src

        w1s, p1s = x[:, 0:128], x[:, 128:256]
        with nc.Block() as block:
            @block.gpsimd
            def _(e):
                e.memset(ident[:, :], 0.0).then_inc(s_pool, 1)
                e.memset(mi[:, :], 1.0).then_inc(s_pool, 1)
                e.memset(mu[:, :], 1.0).then_inc(s_pool, 1)
                e.wait_ge(s_pool, 3)
                e.affine_select(out=ident[:, :], in_=ident[:, :], compare_op=ALU.not_equal, fill=1.0, base=0,
                                pattern=[[-1, 128]], channel_multiplier=1).then_inc(s_pool, 1)
                for k, (t, w, c) in enumerate(((mi, 8, 16), (mu, 2, 64))):
                    e.affine_select(out=t[:, :], in_=t[:, :], compare_op=ALU.is_ge, fill=0.0, base=0,
                                    pattern=[[-c, w]], channel_multiplier=1).then_inc(s_pool, 1)
                    e.wait_ge(s_pool, 5 + 2 * k)
                    e.affine_select(out=t[:, :], in_=t[:, :], compare_op=ALU.is_ge, fill=0.0, base=c - 1,
                                    pattern=[[c, w]], channel_multiplier=-1).then_inc(s_pool, 1)
                    e.wait_ge(s_pool, 6 + 2 * k)
                e.memset(mv1[:, :, :, :, :], 0.0).then_inc(s_pool, 1)
                e.memset(hdiag[:, :, :, :, :], 0.0).then_inc(s_pool, 1)
                e.memset(hist[:, :, :], 0.0).then_inc(s_pool, 1)

            @block.sync
            def _(e):
                e.dma_start(w1s.rearrange("p (a d) -> p a d", a=2), W1.rearrange("(a p) d -> p a d", p=128)).then_inc(s_set, 16)
                e.dma_start(p1s.rearrange("p (a d) -> p a d", a=2), P1.rearrange("(a p) d -> p a d", p=128)).then_inc(s_set, 16)
                for u in range(2):
                    e.dma_start(sg[64 * u:64 * u + 64, :], W0).then_inc(s_set, 16)
                    e.dma_start(h[64 * u:64 * u + 64, :], P0).then_inc(s_set, 16)
                e.wait_ge(s_v, 7)
                for k in range(32):
                    e.dma_start(S0D[k, :, :], s0s[:, 0, :]).then_inc(s_init, 16)
                e.dma_start(BASED[CH, :, 0:2 * HD], s0s[:, 0, :]).then_inc(s_init, 16)
                e.dma_start(BASED[CH, :, 2 * HD:], yth[:, 0, :]).then_inc(s_init, 16)
                e.wait_ge(s_init, 34 * 16)

            @block.vector
            def _(e):
                e.wait_ge(s_set, 96)
                e.memset(mvt[:, :, :], 0.0).then_inc(s_v, 1)
                e.memset(s0s[:, 0, HD:], 0.0).then_inc(s_v, 1)
                e.memset(ydiag[:, :, :, :], 0.0).then_inc(s_v, 1)
                e.tensor_tensor(s0s[:, 0, 0:HD], sg, h[:, :], ALU.add).then_inc(s_v, 1)
                for u in range(2):
                    e.tensor_tensor(om.rearrange("p (a u d) -> p a u d", a=2, u=2)[:, :, u, :],
                                    w1s.rearrange("p (a d) -> p a d", a=2),
                                    p1s.rearrange("p (a d) -> p a d", a=2), ALU.add).then_inc(s_v, 1)
                e.memset(yth[:, :, :], 0.0).then_inc(s_v, 1)
                for t in (gdiag, ddiag, adiag):
                    e.memset(t[:, :, :, :], 0.0).then_inc(s_v, 1)
                e.memset(ones[:, :], 1.0).then_inc(s_v, 1)
                e.memset(U[:, :], 0.0).then_inc(s_v, 1)
                e.memset(Wp[:, :], 0.0).then_inc(s_v, 1)
                e.memset(FAC[:, :], 1.0).then_inc(s_v, 1)
                e.memset(y[:, :, :], 0.0).then_inc(s_v, 1)
                e.memset(dl[:, :], 0.0).then_inc(s_v, 1)
                e.wait_ge(s_v, 16)
                e.memset(U[:, CH + 1:CH + 2], 1.0).then_inc(s_v, 1)
                e.memset(Wp[:, CH:CH + 1], 1.0).then_inc(s_v, 1)
                e.wait_ge(s_pool, 4)
                for st in range(2):
                    e.tensor_copy(ap(repl, 16 * st, [32, 4], [1, 16]), ap(ident, 0, [32, 4], [1, 16])).then_inc(s_v, 1)
                e.wait_ge(s_p, 2)
                for a in range(2):
                    e.tensor_copy(mvt[:, :, 128 * a:128 * a + 128], psT[a].unsqueeze(1).to_broadcast([128, 32, 128])).then_inc(s_v, 1)
                e.wait_ge(s_v, 22)
                e.engine_nop().then_inc(V.sem, V.base)

            @block.tensor
            def _(e):
                e.wait_ge(s_v, 6)
                e.wait_ge(s_pool, 4)
                for a in range(2):
                    e.transpose(psT[a], om[:, 128 * a:128 * a + 128], ident[:, :]).then_inc(s_p, 1)
                e.wait_ge(s_p, 2)
                e.nop().then_inc(T.sem, T.base)

            @block.scalar
            def _(e):
                e.nop().then_inc(A.sem, A.base)

        def load_base(e, s):
            e.dma_start(baset[:, :].unsqueeze(1), BASED[s:s + 1, :, :].rearrange("a p f -> p a f")).then_inc(base_in.sem, 16)

        def load_value(e, c, s):
            e.dma_start(vt[:, :].unsqueeze(1), VR[bass.ds(c * CH + s, 1), :, :].rearrange("a p f -> p a f")).then_inc(value_in.sem, 16)

        def to_hist(e, s, src, lo, hi, sm):
            for m in range(2):
                for j in range(4):
                    row = 8 * (2 * HD + D)
                    dst = bass.AP(hist, s * row + (m * 4 + j) * (2 * HD + D) + lo, [[CH * row, 8], [1, hi - lo]])
                    p = 32 * j + 8 * m
                    e.dma_start(dst, src[p:p + 8, :]).then_inc(sm, 16)

        def slab_done(e, c, k):
            e.wait_ge(T.sem, T.upd(c, f"ba{k}"))
            settled(e, s_own)
            e.wait_ge(V.sem, V.upd(c, f"on{k}"))
            e.dma_start(S0D[k, :, :], s0s[:, k % SB, :]).then_inc(slab_out[k % SB].sem, 16)

        def products_done(e, c, n, half):
            e.wait_ge(A.sem, A.upd(c, f"bs1{4 * n + 3}"))
            settled(e, s_own)
            for j in (2 * half, 2 * half + 1):
                for u in range(2):
                    dst = BASED[0:CH, :, :].rearrange("t (q r) f -> r q t f", r=16)[2 * n + u, 2 * j:2 * j + 2]
                    row = 64 * (j % 2) + 32 * u
                    e.dma_start(dst, bs[row:row + 32, half, :]).then_inc(base_out.sem, 16)

        def load_slab(e, k):
            e.dma_start(s0s[:, k % SB, :], S0D[k, :, :]).then_inc(slab_in[k % SB].sem, 16)

        def load_new_keys(e, c, k):
            n, j = SLABS[k]
            src = ZR[bass.ds(c * CH + CH, CH), :, :].rearrange("t (q n u) d -> t q n (u d)", q=8, n=8)
            e.dma_start(zr[:, k % 2, :], src[:, 2 * j:2 * j + 2, n, :].rearrange("t st f -> st t f")).then_inc(zr_in[k % 2].sem, 16)

        def load_ahead(e, c):
            for i in range(8):
                for m in range(2):
                    src = ZR[bass.ds(c * CH, CH), :, :].rearrange("t (j st m i) d -> i st m t j d", j=4, st=2, m=2)[i, 0, m]
                    e.dma_start(krow[16 * i:16 * i + 16, 4 * m:4 * m + 4, :], src).then_inc(keys_in.sem, 16)
            for k in range(SB):
                load_slab(e, k)
            for k in range(2):
                load_new_keys(e, c, k)

        def diag_h(hf):
            return ap(hdiag, hf * 2048, [16, 8], [129, 16])

        def turned_h(hf):
            return psT[hf].rearrange("p (q r) -> p q r", r=16)

        def spread(dst, src):
            return (ap(dst, 0, [16, 8], [136, 2], [1, 8]), src.rearrange("p (q m i) -> p q m i", q=8, m=2),
                    ap(mi, 0, [0, 8], [0, 2], [1, 8]), ALU.mult)

        with nc.Block() as block:
            @block.sync
            def _(e):
                load_ahead(e, 0)

                def chunk(c, steps):
                    e.wait_ge(V.sem, V.begun(c))
                    e.wait_ge(T.sem, T.begun(c))
                    e.wait_ge(A.sem, A.begun(c))
                    for q in range(8):
                        e.dma_start(gates[16 * q:16 * q + 16, :, :],
                                    GR[16 * (q // 2):16 * (q // 2) + 16, bass.ds(c * CH, CH), :]).then_inc(gates_in.sem, 16)
                    for k in range(2, 32 + 2):
                        if k < 32:
                            if k >= SB:
                                e.wait_ge(slab_out[k % SB].sem, slab_out[k % SB].upd(c, f"s{k - SB}"))
                                settled(e, s_own)
                                load_slab(e, k)
                            e.wait_ge(T.sem, T.upd(c, f"zt{k - 2}"))
                            settled(e, s_own)
                            load_new_keys(e, c, k)
                        slab_done(e, c, k - 2)
                        if k >= 6 and k % 4 in (2, 3):
                            products_done(e, c, k // 4 - 1, k % 4 - 2)
                    for half in range(2):
                        products_done(e, c, 7, half)
                    for k in range(32 - SB, 32):
                        e.wait_ge(slab_out[k % SB].sem, slab_out[k % SB].upd(c, f"s{k}"))
                        settled(e, s_own)
                    e.wait_ge(base_out.sem, base_out.upd(c, "b7"))
                    load_base(e, 0)
                    load_value(e, c, 0)
                    for s in range(steps):
                        e.wait_ge(V.sem, V.step(c, s - 1, "xb2") if s else V.upd(c, "x0"))
                        load_base(e, s + 1)
                        e.wait_ge(V.sem, V.step(c, s, "h"))
                        to_hist(e, s, h[:, :], 0, HD, hist_h.sem)
                        if s == 0 and steps == CH:
                            load_ahead(e, c + 1)
                        e.wait_ge(V.sem, V.step(c, s, "y1"))
                        settled(e, s_own)
                        load_value(e, c, s + 1)
                        e.wait_ge(V.sem, V.step(c, s, "y"))
                        to_hist(e, s, y[:, 0, :], HD, HD + D, hist_y.sem)
                        e.dma_start(YR[bass.ds(c * CH + s, 1), :, :].rearrange("a p d -> p a d"), y[:, 0:1, :]).then_inc(hist_y.sem, 16)
                        e.wait_ge(V.sem, V.step(c, s, "d"))
                        to_hist(e, s, dl[:, :], HD + D, 2 * HD + D, hist_d.sem)

                with e.Fori(0, NCH - 1) as c:
                    chunk(c, CH)
                chunk(NCH - 1, LAST)
                e.wait_ge(hist_h.sem, hist_h.unit * (L + 1))
                e.wait_ge(hist_y.sem, hist_y.unit * (L + 1))
                e.wait_ge(hist_d.sem, hist_d.unit * (L + 1))

            @block.scalar
            def _(e):
                e.preload_act_table(ACT.Sigmoid)

                def chunk(c, steps):
                    for k, (n, j) in enumerate(SLABS):
                        e.wait_ge(T.sem, T.upd(c, f"zt{k}"))
                        e.activation(kt[:, k % 2, :], psZ[:, 0:CH], ACT.Copy).then_inc(A.sem, 1)
                        for u in range(2):
                            e.activation(ztm[:, k % 2, u, :], psZ, ACT.Copy, scale=mu[:, u:u + 1]).then_inc(A.sem, 1)
                        e.wait_ge(T.sem, T.upd(c, f"tr{k}"))
                        for hf in range(2):
                            src = psC[:, 256 * hf:256 * hf + 256].rearrange("p (w u d) -> p u w d", w=2, u=2)
                            dst = mv1[:, hf, 2 * n:2 * n + 2, j, CH:].rearrange("p u (w d) -> p u w d", w=2)
                            e.activation(dst, src, ACT.Copy).then_inc(A.sem, 1)
                        if k % 4 == 3:
                            e.wait_ge(T.sem, T.upd(c, f"ba{k}"))
                            if k > 3:
                                e.wait_ge(base_out.sem, base_out.upd(c, f"b{n - 1}"))
                            e.wait_ge(T.sem, T.upd(c, "cb"))
                            e.activation(bs[:, :, 2 * HD:], psDots.rearrange("p (a s) -> p a s", a=2), ACT.Copy).then_inc(A.sem, 1)
                            for a in range(2):
                                e.activation(bs[:, a, 0:2 * HD], psBase[a], ACT.Copy).then_inc(A.sem, 1)
                    with e.Fori(0, steps) as s:
                        for hf, name in enumerate(("xa", "xz")):
                            e.wait_ge(V.sem, V.step(c, s, name))
                            half = slice(128 * hf, 128 * hf + 128)
                            e.activation(sg[:, half], x[:, half], ACT.Sigmoid).then_inc(A.sem, 1)
                        e.wait_ge(T.sem, T.step(c, s, "tr"))
                        e.activation(diag_h(1), turned_h(1), ACT.Copy).then_inc(A.sem, 1)
                        e.wait_ge(T.sem, T.step(c, s, "pred"))
                        src = ap(hdiag, 0, [2048, 2], [129, 16], [32, 4])
                        dst = mv1[:, :, :, :, bass.ds(s, 1)].rearrange("p a r j o -> p a r (j o)")
                        e.activation(dst, src, ACT.Copy).then_inc(A.sem, 1)
                        e.wait_ge(T.sem, T.step(c, s, "dd"))
                        for u in range(2):
                            src = bass.AP(ydiag, 64 * u * 1024 + u, [[1024, 64], [130, 8], [32, 4]])
                            dst = yth[64 * u:64 * u + 64, :, bass.ds(s, 1)].rearrange("p (n j) o -> p n (j o)", n=8)
                            e.activation(dst, src, ACT.Copy).then_inc(A.sem, 1)

                with e.Fori(0, NCH - 1) as c:
                    chunk(c, CH)
                chunk(NCH - 1, LAST)

            @block.tensor
            def _(e):
                def chunk(c, steps):
                    for w in range(2):
                        e.wait_ge(V.sem, V.upd(c, "srep"))
                        e.matmul(psP[:, 128 * w:128 * w + 128], rep[:, w, :, :].rearrange("p i s -> p (i s)"), ident[:, :],
                                 start=True, stop=True).then_inc(T.sem, 1)
                    e.wait_ge(V.sem, V.upd(c, "d3c"))
                    e.matmul(psH[:, 0:384], ones[:, :], d3.rearrange("p w q -> p (w q)"), start=True, stop=True).then_inc(T.sem, 1)

                    def new_terms(k):
                        n, j = SLABS[k]
                        slot = (n // 4) * 4 + j
                        e.wait_ge(V.sem, V.upd(c, f"wk{k}"))
                        if k == 0:
                            e.wait_ge(V.sem, V.upd(c, "cu1"))
                            e.wait_ge(hist_h.sem, c * (hist_h.unit * CH))
                            e.wait_ge(hist_d.sem, c * (hist_d.unit * CH))
                        if k >= 2:
                            e.wait_ge(V.sem, V.upd(c, f"on{k - 2}"))
                        for lay, wt, lo in ((0, wy[k % 2], 0), (1, wk[k % 2], HD + D)):
                            for w in range(2):
                                mm = e.matmul(psNew[k % 2][lay][:, HD * w:HD * w + HD], wt[:, 128 * w:128 * w + 128],
                                              hist[:, slot, lo:lo + HD], start=True, stop=True)
                            mm.then_inc(T.sem, 1)

                    new_terms(0)
                    for k, (n, j) in enumerate(SLABS):
                        if k < 31:
                            new_terms(k + 1)
                        e.wait_ge(zr_in[k % 2].sem, zr_in[k % 2].upd(c, f"z{k}"))
                        if k:
                            e.wait_ge(A.sem, A.upd(c, f"ds{k - 1}" if k % 4 == 0 else f"zm1{k - 1}"))
                        e.matmul(psZ, zr[:, k % 2, :], ident[0:32, 0:32], start=True, stop=True).then_inc(T.sem, 1)
                        e.wait_ge(V.sem, V.upd(c, f"sn{k}"))
                        if k:
                            e.wait_ge(A.sem, A.upd(c, f"c1{k - 1}"))
                        for hf in range(2):
                            for w in range(2):
                                o = 256 * hf + 128 * w
                                mm = e.transpose(psC[:, o:o + 128], mvt[:, k, HD * w + 128 * hf:HD * w + 128 * hf + 128], ident[:, :])
                        mm.then_inc(T.sem, 1)
                        e.wait_ge(V.sem, V.upd(c, f"on{k}"))
                        e.wait_ge(A.sem, A.upd(c, f"zm1{k}"))
                        rows, zk = slice(64 * (j % 2), 64 * (j % 2) + 64), ztm[:, k % 2, :, :].rearrange("p u z -> p (u z)")
                        e.matmul(psBase[j // 2][rows, :], zk, s0s[:, k % SB, :], start=True, stop=True)
                        e.matmul(psDots[rows, CH * (j // 2):CH * (j // 2) + CH], zk, kt[:, k % 2, :], start=True, stop=True).then_inc(T.sem, 1)
                    with e.Fori(0, steps) as s:
                        e.wait_ge(A.sem, A.step(c, s, "yt1", 1))
                        for hf, name in enumerate(("ha", "h")):
                            e.wait_ge(V.sem, V.step(c, s, name))
                            e.transpose(psT[hf], h[:, 128 * hf:128 * hf + 128], ident[:, :]).then_inc(T.sem, 1)
                        for hf in range(2):
                            if hf == 0:
                                e.wait_ge(V.sem, V.step(c, s, "hd0"))
                            else:
                                e.wait_ge(A.sem, A.step(c, s, "hd1"))
                            for r in range(16):
                                for j in range(4):
                                    mm = e.matmul(psP[32 * j:32 * j + 32, 0:MW], hdiag[:, hf, r, j, :], mv1[:, hf, r, j, :],
                                                  start=(hf == 0 and r == 0), stop=(hf == 1 and r == 15))
                        mm.then_inc(T.sem, 1)
                        e.wait_ge(V.sem, V.step(c, s, "arep"))
                        e.matmul(psAT, rep[:, 0, :, :].rearrange("p i s -> p (i s)"), ident[:, :], start=True, stop=True).then_inc(T.sem, 1)
                        e.wait_ge(V.sem, V.step(c, s, "grep"))
                        e.matmul(psGT, rep[:, 1, :, :].rearrange("p i s -> p (i s)"), ident[:, :], start=True, stop=True).then_inc(T.sem, 1)
                        e.wait_ge(V.sem, V.step(c, s, "adiag"))
                        e.wait_ge(hist_d.sem, c * (hist_d.unit * CH) + s * hist_d.unit)
                        def ahead(m):
                            for j in range(4):
                                mm = e.matmul(psA[32 * j:32 * j + 32, :], adiag[:, m, j, :], hist[:, m * 4 + j, HD + D:],
                                              start=(m == 0), stop=(m == 1))
                            return mm

                        ahead(0)
                        e.wait_ge(V.sem, V.step(c, s, "gdiag"))
                        e.wait_ge(hist_y.sem, c * (hist_y.unit * CH) + s * hist_y.unit)
                        for m in range(2):
                            for j in range(4):
                                mm = e.matmul(psY[32 * j:32 * j + 32, :], gdiag[:, m, j, :], hist[:, m * 4 + j, HD:HD + D],
                                              start=(m == 0), stop=(m == 1))
                        mm.then_inc(T.sem, 1)
                        ahead(1).then_inc(T.sem, 1)
                        e.wait_ge(V.sem, V.step(c, s, "y"))
                        e.matmul(psYT, y[:, :, :].rearrange("p u d -> p (u d)"), repl[:, :], start=True, stop=True).then_inc(T.sem, 1)
                        e.wait_ge(V.sem, V.step(c, s, "sp"))
                        e.matmul(psR, repl[:, :], sp, start=True, stop=True).then_inc(T.sem, 1)
                        e.wait_ge(V.sem, V.step(c, s, "ydiag"))
                        for n in range(8):
                            for j in range(4):
                                mm = e.matmul(psD[32 * j:32 * j + 32, :], ydiag[:, n, j, :], yth[:, 4 * n + j, :],
                                              start=(n == 0), stop=(n == 7))
                        mm.then_inc(T.sem, 1)
                        for n in range(8):
                            if n == 4:
                                e.wait_ge(V.sem, V.step(c, s, "drep"))
                                e.matmul(psDT, rep[:, 2, :, :].rearrange("p i s -> p (i s)"), ident[:, :], start=True, stop=True).then_inc(T.sem, 1)
                            for j in range(4):
                                mm = e.matmul(psH[32 * j:32 * j + 32, :], ydiag[:, n, j, :], mvt[:, 4 * n + j, :],
                                              start=(n == 0), stop=(n == 7))
                        mm.then_inc(T.sem, 1)
                        e.wait_ge(V.sem, V.step(c, s, "ddiag"))
                        e.wait_ge(hist_h.sem, hist_h.step(c, s, "h"))
                        for m in range(2):
                            for j in range(4):
                                mm = e.matmul(psE[32 * j:32 * j + 32, 0:HD], ddiag[:, m, j, :], hist[:, m * 4 + j, 0:HD],
                                              start=(m == 0), stop=(m == 1))
                        mm.then_inc(T.sem, 1)
                        for k in range(WARM):
                            e.matmul(b[1][:, HD:], ident[:, :], mvt[:, k, 0:HD], start=True, stop=True)

                with e.Fori(0, NCH - 1) as c:
                    chunk(c, CH)
                chunk(NCH - 1, LAST)

            @block.vector
            def _(e):
                def own(val):
                    e.wait_ge(V.sem, val)

                def chunk(c, steps):
                    def go(ins, name):
                        ins.then_inc(V.sem, 1)

                    own(V.begun(c))
                    N16, N17 = slice(CH, CH + 1), slice(CH + 1, CH + 2)
                    go(e.tensor_tensor(Wn[:, :], U[:, :], FAC[:, :], ALU.mult), "nfac")
                    own(V.upd(c, "nfac"))
                    e.wait_ge(T.sem, T.begun(c))
                    for w, t in enumerate((Wp, Wn)):
                        ins = e.tensor_copy(rep[:, w, :, :], t[:, 0:CH].unsqueeze(1).to_broadcast([128, 8, CH]))
                    go(ins, "srep")
                    for w in range(2):
                        e.wait_ge(T.sem, T.upd(c, "ct1"))
                        go(e.tensor_tensor(cm[:, w, :].rearrange("p (q i) -> p q i", i=8),
                                           psP[:, 128 * w:128 * w + 128].rearrange("p (q i) -> p q i", i=8),
                                           ap(mi, 0, [0, 16], [1, 8]), ALU.mult), "cm")
                    e.wait_ge(A.sem, A.begun(c))
                    e.wait_ge(base_out.sem, c * (base_out.unit * 8))
                    for w, col in enumerate((Wp[:, N16], Wp[:, N17], Wn[:, N17])):
                        go(e.tensor_scalar(d3[:, w, :], ident[:, :], col, None, ALU.mult), "d3")
                    e.wait_ge(T.sem, T.upd(c, "cb"))
                    for u in range(2):
                        src = psH[64 * u:64 * u + 64, 0:384].rearrange("p (w j st n u) -> p w st u n j", w=3, j=4, st=2, u=2)[:, :, 0, u]
                        go(e.tensor_copy(cu[64 * u:64 * u + 64, :, :, :], src), "cu")
                    own(V.upd(c, "cu1"))
                    e.wait_ge(keys_in.sem, keys_in.upd(c, "in"))
                    e.wait_ge(hist_y.sem, c * (hist_y.unit * CH))

                    def weigh(k):
                        n, j = SLABS[k]
                        slot = (n // 4) * 4 + j
                        if k >= 2:
                            e.wait_ge(T.sem, T.upd(c, f"so{k - 2}"))
                        wt = cm[:, :, 32 * j + 2 * n:32 * j + 2 * n + 2].unsqueeze(3).to_broadcast([128, 2, 2, D])
                        for t, row, name in ((wy, hist[:, slot, HD:HD + D], "wy"), (wk, krow[:, slot, :], "wk")):
                            src = row.unsqueeze(1).unsqueeze(1).to_broadcast([128, 2, 2, D])
                            go(e.tensor_tensor(t[k % 2].rearrange("p (w u d) -> p w u d", w=2, u=2), src, wt, ALU.mult), name)

                    e.wait_ge(hist_h.sem, c * (hist_h.unit * CH))
                    e.wait_ge(hist_d.sem, c * (hist_d.unit * CH))
                    weigh(0)
                    for k, (n, j) in enumerate(SLABS):
                        if k < 31:
                            weigh(k + 1)
                        ca, cb, ce = (cu[:, w, n, j:j + 1] for w in range(3))
                        e.wait_ge(slab_in[k % SB].sem, slab_in[k % SB].upd(c, f"s{k}"))
                        both = ((mvt[:, k, :], psNew[k % 2][0], "s"), (s0s[:, k % SB, :], psNew[k % 2][1], "o"))
                        for t, ps, lay in both:
                            e.wait_ge(T.sem, T.upd(c, f"st{k}" if lay == "s" else f"so{k}"))
                            go(e.scalar_tensor_tensor(out=t[:, 0:HD], in0=t[:, 0:HD], scalar=ca, in1=ps[:, 0:HD],
                                                      op0=ALU.mult, op1=ALU.add), lay + "a")
                        for t, ps, lay in both:
                            own(V.upd(c, f"{lay}a{k}"))
                            go(e.scalar_tensor_tensor(out=t[:, 0:HD], in0=t[:, HD:], scalar=cb, in1=t[:, 0:HD],
                                                      op0=ALU.mult, op1=ALU.add), lay + "b")
                        for t, ps, lay in both:
                            own(V.upd(c, f"{lay}b{k}"))
                            go(e.scalar_tensor_tensor(out=t[:, HD:], in0=t[:, HD:], scalar=ce, in1=ps[:, HD:2 * HD],
                                                      op0=ALU.mult, op1=ALU.add), lay + "n")
                    own(V.upd(c, "on31"))
                    go(e.memset(W[:, :], 0.0), "rw")
                    own(V.upd(c, "rw"))
                    go(e.memset(W[:, N16], 1.0), "rw1")
                    go(e.memset(U[:, :], 0.0), "ru")
                    own(V.upd(c, "ru"))
                    go(e.memset(U[:, N17], 1.0), "ru1")
                    go(e.memset(FAC[:, 0:CH], 0.0), "rf")
                    go(e.memset(FAC[:, CH:], 1.0), "rf1")
                    own(V.upd(c, "rf1"))
                    go(e.tensor_copy(Wp[:, :], W[:, :]), "rp")
                    go(e.memset(al[:, :], 0.0), "ral")
                    e.wait_ge(gates_in.sem, gates_in.upd(c, "in"))
                    e.wait_ge(base_in.sem, base_in.upd(c, "first"))
                    e.wait_ge(T.sem, T.upd(c, "ba31"))
                    go(e.tensor_copy(xb[:, :], baset[:, 0:HD]), "x0")
                    with e.Fori(0, steps) as s:
                        def st(name, back=0):
                            return V.step(c, s, name, back)

                        nm = lambda ins: ins.then_inc(V.sem, 1)
                        if True:
                            own(V.upd(c, "x0") + s * V.P)
                            for hf in range(2):
                                half = slice(128 * hf, 128 * hf + 128)
                                nm(e.scalar_tensor_tensor(out=x[:, half], in0=dl[:, half], scalar=al[:, 0:1], in1=xb[:, half],
                                                          op0=ALU.mult, op1=ALU.add))
                            e.wait_ge(hist_h.sem, c * (hist_h.unit * CH) + s * hist_h.unit)
                            for hf, name in enumerate(("siga", "sig")):
                                half = slice(128 * hf, 128 * hf + 128)
                                e.wait_ge(A.sem, A.step(c, s, name))
                                nm(e.tensor_tensor(h[:, half], x[:, half], sg[:, half], ALU.mult))
                            e.wait_ge(T.sem, T.step(c, s, "tra"))
                            e.wait_ge(A.sem, A.step(c, s, "yt1", 1))
                            nm(e.tensor_copy(diag_h(0), turned_h(0)))
                            own(st("h"))
                            nm(e.scalar_tensor_tensor(out=om, in0=sg, scalar=1.0, in1=h[:, :],
                                                      op0=ALU.subtract, op1=ALU.mult))
                            own(st("om"))
                            nm(e.tensor_tensor(sp, sg, om, ALU.subtract))
                            g = lambda q: gates[:, bass.ds(s, 1), q:q + 1].rearrange("p a b -> p (a b)")
                            nm(e.tensor_scalar(U[:, :], U[:, :], g(0), None, ALU.mult))
                            own(st("tabu"))
                            nm(e.scalar_tensor_tensor(out=W[:, :], in0=W[:, :], scalar=g(1), in1=U[:, :],
                                                      op0=ALU.mult, op1=ALU.add))
                            own(st("tabw"))
                            nm(e.tensor_tensor(Wn[:, :], W[:, :], FAC[:, :], ALU.mult))
                            e.wait_ge(base_in.sem, base_in.step(c, s, "next"))
                            own(st("tabp"))
                            nm(e.tensor_tensor(rep[:, 0, :, :], dott.unsqueeze(1).to_broadcast([128, 8, CH]),
                                               Wn[:, 0:CH].unsqueeze(1).to_broadcast([128, 8, CH]), ALU.mult))
                            nm(e.tensor_scalar(al[:, :], dott[:, bass.ds(s, 1)], g(2), None, ALU.mult))
                            nm(e.tensor_scalar(xb[:, :], baset[:, 0:HD], Wn[:, N16], None, ALU.mult))
                            own(st("xb1"))
                            nm(e.scalar_tensor_tensor(out=xb[:, :], in0=baset[:, HD:2 * HD], scalar=Wn[:, N17], in1=xb[:, :],
                                                      op0=ALU.mult, op1=ALU.add))
                            own(st("xb2"))
                            nm(e.tensor_copy(U[:, bass.ds(s, 1)], ones[:, 0:1]))
                            nm(e.tensor_copy(W[:, bass.ds(s, 1)], ones[:, 0:1]))
                            nm(e.tensor_copy(FAC[:, bass.ds(s, 1)], g(2)))
                            nm(e.tensor_copy(Wn[:, bass.ds(s, 1)], g(2)))
                            e.wait_ge(T.sem, T.step(c, s, "pred"))
                            nm(e.tensor_tensor(rep[:, 1, :, :], psP[:, 0:CH].unsqueeze(1).to_broadcast([128, 8, CH]),
                                               Wp[:, 0:CH].unsqueeze(1).to_broadcast([128, 8, CH]), ALU.mult))
                            e.wait_ge(T.sem, T.step(c, s, "at"))
                            nm(e.tensor_tensor(*spread(adiag, psAT)))
                            e.wait_ge(value_in.sem, value_in.upd(c, "first") + s * 16)
                            nm(e.scalar_tensor_tensor(out=y1[:, :], in0=psP[:, CH:CH + D], scalar=Wp[:, N16], in1=vt[:, :],
                                                      op0=ALU.mult, op1=ALU.subtract))
                            e.wait_ge(T.sem, T.step(c, s, "gt"))
                            nm(e.tensor_tensor(*spread(gdiag, psGT)))
                            own(st("y1"))
                            nm(e.scalar_tensor_tensor(out=y1[:, :], in0=psP[:, CH + D:MW], scalar=Wp[:, N17], in1=y1[:, :],
                                                      op0=ALU.mult, op1=ALU.add))
                            e.wait_ge(T.sem, T.step(c, s, "yp"))
                            own(st("y2"))
                            e.wait_ge(hist_y.sem, c * (hist_y.unit * CH) + s * hist_y.unit)
                            nm(e.tensor_tensor(y[:, :, :], psY.unsqueeze(1).to_broadcast([128, 2, D]),
                                               y1[:, :].unsqueeze(1).to_broadcast([128, 2, D]), ALU.add))
                            e.wait_ge(T.sem, T.step(c, s, "yt"))
                            nm(e.tensor_tensor(ap(ydiag, 0, [16, 8], [130, 8], [1, 2]),
                                               psYT.rearrange("p (q n u) -> p q n u", q=8, n=8),
                                               ap(mu, 0, [0, 8], [0, 8], [1, 2]), ALU.mult))
                            e.wait_ge(T.sem, T.step(c, s, "a"))
                            nm(e.tensor_tensor(xb[:, :], xb[:, :], psA, ALU.add))
                            e.wait_ge(T.sem, T.step(c, s, "dd"))
                            nm(e.tensor_tensor(rep[:, 2, :, :], psD.unsqueeze(1).to_broadcast([128, 8, CH]),
                                               Wp[:, 0:CH].unsqueeze(1).to_broadcast([128, 8, CH]), ALU.mult))
                            e.wait_ge(T.sem, T.step(c, s, "dt"))
                            nm(e.tensor_tensor(*spread(ddiag, psDT)))
                            e.wait_ge(T.sem, T.step(c, s, "dhp"))
                            nm(e.tensor_scalar(dh[:, :], psH[:, 0:HD], Wp[:, N16], None, ALU.mult))
                            own(st("dh1"))
                            nm(e.scalar_tensor_tensor(out=dh[:, :], in0=psH[:, HD:], scalar=Wp[:, N17], in1=dh[:, :],
                                                      op0=ALU.mult, op1=ALU.add))
                            own(st("dh2"))
                            nm(e.tensor_copy(Wp[:, :], Wn[:, :]))
                            e.wait_ge(T.sem, T.step(c, s, "e"))
                            halves = (slice(0, 128), slice(128, 256))
                            for half in halves:
                                nm(e.tensor_tensor(dh[:, half], dh[:, half], psE[:, half], ALU.add))
                            e.wait_ge(hist_d.sem, c * (hist_d.unit * CH) + s * hist_d.unit)
                            for half, name in zip(halves, ("dh3a", "dh3")):
                                own(st(name))
                                nm(e.tensor_tensor(dl[:, half], dh[:, half], psR[:, half], ALU.mult))

                with e.Fori(0, NCH - 1) as c:
                    chunk(c, CH)
                chunk(NCH - 1, LAST)


def audio_tower(nc, x, filt, W_k, b_k, Wqk, Wv, Wpos, bpos, Wproj, bproj, gating, wr, br, w1, b1, w2, b2,
                W_fused, W0, W1, P0, P1, Wg, bg, E1, be1, E2, be2, out):
    def scratch(name, *shape):
        return nc.dram_tensor(f"between_{name}", shape, F32, kind="Internal").ap()

    H0, X0, H1, H2, XN = (scratch(n, B, TL, 2, D) for n in ("h_tok", "x_att", "h_att", "h_ffn", "x_ffn"))
    T_ = CH * NCH
    ZR, VR, YR = scratch("keys", T_ + CH + 1, 128, D), scratch("values", T_ + 1, 128, D), scratch("recurrent", T_, 128, D)
    GR = scratch("gates", B, T_, 4)
    token_layer(nc, x, filt, W_k, b_k, H0, X0)
    attention_layer(nc, Wqk, Wv, Wpos, bpos, Wproj, bproj, gating, H0, X0, H1)
    ffn_layer(nc, wr, br, w1, b1, w2, b2, H1, H2, XN, scratch("w_by_tile", B, L), scratch("w_by_batch", B, L))
    key_layer(nc, W_fused, H2, ZR, VR, GR)
    recurrent_layer(nc, ZR, VR, GR, YR, scratch("state0", 32, 128, 512), scratch("base", CH + 1, 128, 512 + CH),
                    W0, P0, W1, P1)
    expert_layer(nc, Wg, bg, E1, be1, E2, be2, H2, YR, out)


_INS = ['x', 'L0_tok_filt', 'L0_tok_W_k', 'L0_tok_b_k', 'L0_attn_Wqk', 'L0_attn_Wv', 'L0_attn_Wpos', 'L0_attn_bpos',
        'L0_attn_Wproj', 'L0_attn_bproj', 'L0_attn_gating', 'L0_ffn_wr', 'L0_ffn_br', 'L0_ffn_w1', 'L0_ffn_b1',
        'L0_ffn_w2', 'L0_ffn_b2', 'L1_attn_W_fused', 'L1_attn_W0', 'L1_attn_W1', 'L1_attn_P0', 'L1_attn_P1',
        'L1_ffn_Wg', 'L1_ffn_bg', 'L1_ffn_W1', 'L1_ffn_b1', 'L1_ffn_W2', 'L1_ffn_b2']
_OUTS = [((64, 248, 64), 'float32')]


def kernel(**inputs):
    import numpy as _np
    import concourse.bacc as _bacc
    from concourse import mybir as _mybir
    from concourse.bass_utils import run_bass_kernel_spmd as _run

    nc = _bacc.Bacc("TRN2", target_bir_lowering=False, num_devices=1)
    arrays, args = {}, []
    for name in _INS:
        a = _np.ascontiguousarray(inputs[name])
        arrays[f"in_{name}_dram"] = a
        args.append(nc.dram_tensor(f"in_{name}_dram", a.shape, _mybir.dt.from_np(a.dtype), kind="ExternalInput").ap())
    for i, (shape, dtype) in enumerate(_OUTS):
        dt = _mybir.dt.from_np(_np.dtype(dtype))
        args.append(nc.dram_tensor(f"out_{i}_dram", shape, dt, kind="ExternalOutput").ap())
    audio_tower(nc, *args)
    r = _run(nc, [arrays], core_ids=[0])
    got = tuple(r.results[0][f"out_{i}_dram"] for i in range(len(_OUTS)))
    return got[0]
```
